# Optimizing a Trainium2 kernel written in Bass

```python
import numpy as np
import jax
import jax.numpy as jnp

def _softmax(x, axis=-1):
    return jax.nn.softmax(x, axis=axis)

def _gelu(x):
    return jax.nn.gelu(x, approximate=True)

def _silu(x):
    return jax.nn.silu(x)

def _sigmoid(x):
    return jax.nn.sigmoid(x)

def _layernorm(x, axis=-1, eps=1e-05):
    m = jnp.mean(x, axis=axis, keepdims=True)
    v = jnp.var(x, axis=axis, keepdims=True)
    return (x - m) / jnp.sqrt(v + eps)

def _scatter_add(tgt, idx, src, axis=0):
    return tgt.at[idx].add(src)

def _segment_sum(src, seg, n):
    return jax.ops.segment_sum(src, seg, n)
kernel_name = 'mk_gnn_resnorm_d4_gnn_r64_0ad9c0'

def setup_inputs(seed: int=0):
    np.random.seed(seed)
    _w = jnp.asarray

    def _rec_inputs():
        import jax
        import jax.numpy as jnp
        _gk = jax.random.key(seed)
        x = -0.0001006 + 1 * jax.random.normal(jax.random.fold_in(_gk, 1), (50000, 96), jnp.float32)
        src = jax.random.randint(jax.random.fold_in(_gk, 2), (25000,), 0, 50000, jnp.int32)
        dst = jax.random.randint(jax.random.fold_in(_gk, 3), (25000,), 0, 50000, jnp.int32)
        _o = jnp.argsort(dst, stable=True)
        src = src[_o]
        dst = dst[_o]
        edge_attr_17 = jax.random.uniform(jax.random.fold_in(_gk, 12), (25000, 17), jnp.float32, 0.0, 1)
        edge_attr_32 = 0.000196303 + 1.00016 * jax.random.normal(jax.random.fold_in(_gk, 13), (25000, 32), jnp.float32)
        return (x, src, dst, edge_attr_17, edge_attr_32)
    x, src, dst, edge_attr_17, edge_attr_32 = _rec_inputs()

    def _L0_gnn_setup():
        import jax, jax.numpy as jnp
        import numpy as np
        N, E = (50000, 12500)
        DIN = DOUT = 96
        DE = 32

        def _egnn_conv(x, src, dst, edge_attr, W_msg, W_edge, W_root, b):
            msg = x[src] @ W_msg + edge_attr @ W_edge
            agg = jax.ops.segment_max(msg, dst, num_segments=x.shape[0])
            agg = jnp.where(jnp.isneginf(agg), 0.0, agg)
            return agg + x @ W_root + b
        key = jax.random.key(seed)
        ks = jax.random.split(key, 10)
        rn = lambda k, sh, sc: jax.random.normal(k, sh, jnp.float32) * sc
        return {'X': rn(ks[0], (N, DIN), 1.0), 'edge_index': jax.random.randint(ks[1], (2, E), 0, N, jnp.int32), 'edge_attr': rn(ks[2], (E, DE), 1.0), 'W1_msg': rn(ks[3], (DIN, DOUT), DIN ** (-0.5)), 'W1_edge': rn(ks[4], (DE, DOUT), DE ** (-0.5)), 'W1_root': rn(ks[5], (DIN, DOUT), DIN ** (-0.5)), 'b1': jnp.zeros((DOUT,), jnp.float32), 'W2_msg': rn(ks[6], (DOUT, DOUT), DOUT ** (-0.5)), 'W2_edge': rn(ks[7], (DE, DOUT), DE ** (-0.5)), 'W2_root': rn(ks[8], (DOUT, DOUT), DOUT ** (-0.5)), 'b2': jnp.zeros((DOUT,), jnp.float32)}
    _L0_gnn_all = _L0_gnn_setup()
    _L0_gnn_in = {k: v for k, v in _L0_gnn_all.items() if k in ('W1_msg', 'W1_edge', 'W1_root', 'b1', 'W2_msg', 'W2_edge', 'W2_root', 'b2')}
    del _L0_gnn_all

    def _L1_gnn_setup():
        import jax, jax.numpy as jnp
        import numpy as np
        K = 10
        ALPHA = 0.1
        BETA = 0.9
        N_NODES = 50000
        N_EDGES = 12500
        D_FEAT = 96
        key = jax.random.key(seed)
        k1, k2, k3 = jax.random.split(key, 3)
        x = jax.random.normal(k1, (N_NODES, D_FEAT), dtype=jnp.float32)
        row = jax.random.randint(k2, (N_EDGES,), 0, N_NODES, dtype=jnp.int64)
        col = jax.random.randint(k3, (N_EDGES,), 0, N_NODES, dtype=jnp.int64)
        edge_index = jnp.stack([row, col], axis=0)
        return {'x': x, 'edge_index': edge_index}
    _L1_gnn_all = _L1_gnn_setup()
    _L1_gnn_in = {k: v for k, v in _L1_gnn_all.items() if k in ()}
    del _L1_gnn_all

    def _L2_gnn_setup():
        import jax, jax.numpy as jnp
        import numpy as np
        N_NODES = 50000
        N_EDGES = 12500
        IN_FEATS = 96
        OUT_FEATS = 96
        key = jax.random.key(seed)
        k1, k2, k3, k4, k5 = jax.random.split(key, 5)
        feat = jax.random.normal(k1, (N_NODES, IN_FEATS), dtype=jnp.float32)
        weight = jax.random.normal(k2, (IN_FEATS, OUT_FEATS), dtype=jnp.float32) * 0.05
        bias = jax.random.normal(k3, (OUT_FEATS,), dtype=jnp.float32) * 0.05
        src = jax.random.randint(k4, (N_EDGES,), 0, N_NODES, dtype=jnp.int64 if jax.config.jax_enable_x64 else jnp.int32)
        dst = jax.random.randint(k5, (N_EDGES,), 0, N_NODES, dtype=jnp.int64 if jax.config.jax_enable_x64 else jnp.int32)
        return {'feat': feat, 'weight': weight, 'bias': bias, 'src': src, 'dst': dst}
    _L2_gnn_all = _L2_gnn_setup()
    _L2_gnn_in = {k: v for k, v in _L2_gnn_all.items() if k in ('weight', 'bias')}
    del _L2_gnn_all

    def _L3_gnn_setup():
        import jax, jax.numpy as jnp
        import numpy as np
        N = 50000
        E = 12500
        D = 96
        ED = 17
        key = jax.random.key(seed)
        ks = jax.random.split(key, 12)
        x = jax.random.normal(ks[0], (N, D), dtype=jnp.float32)
        edge_index = jax.random.randint(ks[1], (2, E), 0, N, dtype=jnp.int64)
        edge_attr = jax.random.uniform(ks[2], (E, ED), dtype=jnp.float32)
        s = 1.0 / np.sqrt(ED)
        W1 = jax.random.uniform(ks[3], (D, ED), jnp.float32, -s, s)
        b1 = jax.random.uniform(ks[4], (D,), jnp.float32, -s, s)
        s = 1.0 / np.sqrt(D)
        W2 = jax.random.uniform(ks[5], (D, D), jnp.float32, -s, s)
        b2 = jax.random.uniform(ks[6], (D,), jnp.float32, -s, s)
        Ws = jax.random.uniform(ks[7], (D, D), jnp.float32, -s, s)
        bs = jax.random.uniform(ks[8], (D,), jnp.float32, -s, s)
        Wn = jax.random.uniform(ks[9], (D, D), jnp.float32, -s, s)
        bn = jax.random.uniform(ks[10], (D,), jnp.float32, -s, s)
        return {'x': x, 'edge_index': edge_index, 'edge_attr': edge_attr, 'W1': W1, 'b1': b1, 'W2': W2, 'b2': b2, 'Ws': Ws, 'bs': bs, 'Wn': Wn, 'bn': bn}
    _L3_gnn_all = _L3_gnn_setup()
    _L3_gnn_in = {k: v for k, v in _L3_gnn_all.items() if k in ('W1', 'b1', 'W2', 'b2', 'Ws', 'bs', 'Wn', 'bn')}
    del _L3_gnn_all
    return {'x': x, 'src': src, 'dst': dst, 'edge_attr_17': edge_attr_17, 'edge_attr_32': edge_attr_32, 'L0_gnn_W1_msg': _L0_gnn_in['W1_msg'], 'L0_gnn_W1_edge': _L0_gnn_in['W1_edge'], 'L0_gnn_W1_root': _L0_gnn_in['W1_root'], 'L0_gnn_b1': _L0_gnn_in['b1'], 'L0_gnn_W2_msg': _L0_gnn_in['W2_msg'], 'L0_gnn_W2_edge': _L0_gnn_in['W2_edge'], 'L0_gnn_W2_root': _L0_gnn_in['W2_root'], 'L0_gnn_b2': _L0_gnn_in['b2'], 'L2_gnn_weight': _L2_gnn_in['weight'], 'L2_gnn_bias': _L2_gnn_in['bias'], 'L3_gnn_W1': _L3_gnn_in['W1'], 'L3_gnn_b1': _L3_gnn_in['b1'], 'L3_gnn_W2': _L3_gnn_in['W2'], 'L3_gnn_b2': _L3_gnn_in['b2'], 'L3_gnn_Ws': _L3_gnn_in['Ws'], 'L3_gnn_bs': _L3_gnn_in['bs'], 'L3_gnn_Wn': _L3_gnn_in['Wn'], 'L3_gnn_bn': _L3_gnn_in['bn']}

def reference(x, src, dst, edge_attr_17, edge_attr_32, L0_gnn_W1_msg, L0_gnn_W1_edge, L0_gnn_W1_root, L0_gnn_b1, L0_gnn_W2_msg, L0_gnn_W2_edge, L0_gnn_W2_root, L0_gnn_b2, L2_gnn_weight, L2_gnn_bias, L3_gnn_W1, L3_gnn_b1, L3_gnn_W2, L3_gnn_b2, L3_gnn_Ws, L3_gnn_bs, L3_gnn_Wn, L3_gnn_bn):
    import jax
    import jax.numpy as jnp

    def _L0_gnn_ref(X, edge_index, edge_attr, W1_msg, W1_edge, W1_root, b1, W2_msg, W2_edge, W2_root, b2):
        import jax, jax.numpy as jnp
        import numpy as np
        N, E = (50000, 12500)
        DIN = DOUT = 96
        DE = 32

        def _egnn_conv(x, src, dst, edge_attr, W_msg, W_edge, W_root, b):
            msg = x[src] @ W_msg + edge_attr @ W_edge
            agg = jax.ops.segment_max(msg, dst, num_segments=x.shape[0])
            agg = jnp.where(jnp.isneginf(agg), 0.0, agg)
            return agg + x @ W_root + b
        src, dst = (edge_index[0], edge_index[1])
        c1 = jax.nn.leaky_relu(_egnn_conv(X, src, dst, edge_attr, W1_msg, W1_edge, W1_root, b1))
        c2 = jax.nn.leaky_relu(_egnn_conv(c1, src, dst, edge_attr, W2_msg, W2_edge, W2_root, b2))
        return c2

    def _L1_gnn_ref(x, edge_index):
        import jax, jax.numpy as jnp
        import numpy as np
        K = 10
        ALPHA = 0.1
        BETA = 0.9
        N_NODES = 50000
        N_EDGES = 12500
        D_FEAT = 96
        n = x.shape[0]
        row, col = (edge_index[0], edge_index[1])
        ones = jnp.ones((edge_index.shape[1],), dtype=x.dtype)
        deg_row = jnp.maximum(jax.ops.segment_sum(ones, row, num_segments=n), 1.0)
        deg_col = jnp.maximum(jax.ops.segment_sum(ones, col, num_segments=n), 1.0)
        w = jax.lax.rsqrt(deg_row[row] * deg_col[col])

        def spmm(feat):
            msg = feat[col] * w[:, None]
            return jax.ops.segment_sum(msg, row, num_segments=n)
        h = x
        out = h
        for _ in range(K):
            out = spmm(out) * BETA + h * ALPHA
        theta = BETA ** K + ALPHA * sum((BETA ** i for i in range(K)))
        return out / jnp.asarray(theta, dtype=x.dtype)

    def _L2_gnn_ref(feat, weight, bias, src, dst):
        import jax, jax.numpy as jnp
        import numpy as np
        N_NODES = 50000
        N_EDGES = 12500
        IN_FEATS = 96
        OUT_FEATS = 96
        N = feat.shape[0]
        ones = jnp.ones(src.shape, dtype=feat.dtype)
        out_deg = jnp.clip(jax.ops.segment_sum(ones, src, num_segments=N), 1.0)
        in_deg = jnp.clip(jax.ops.segment_sum(ones, dst, num_segments=N), 1.0)
        feat_n = feat * (out_deg ** (-0.5))[:, None]
        agg = jax.ops.segment_sum(feat_n[src], dst, num_segments=N)
        rst = agg @ weight
        rst = rst * (in_deg ** (-0.5))[:, None]
        return rst + bias

    def _L3_gnn_ref(x, edge_index, edge_attr, W1, b1, W2, b2, Ws, bs, Wn, bn):
        import jax, jax.numpy as jnp
        import numpy as np
        N = 50000
        E = 12500
        D = 96
        ED = 17
        src, dst = (edge_index[0], edge_index[1])
        h = jax.nn.relu(edge_attr @ W1.T + b1)
        w = h @ W2.T + b2
        msg = w * x[src]
        agg = jax.ops.segment_sum(msg, dst, num_segments=x.shape[0])
        return jax.nn.relu(x @ Ws.T + bs + agg @ Wn.T + bn)
    edge_index = jnp.stack([src, dst])
    x = _layernorm(x + _L0_gnn_ref(x, edge_index, edge_attr_32, L0_gnn_W1_msg, L0_gnn_W1_edge, L0_gnn_W1_root, L0_gnn_b1, L0_gnn_W2_msg, L0_gnn_W2_edge, L0_gnn_W2_root, L0_gnn_b2), axis=-1)
    x = _layernorm(x + _L1_gnn_ref(x, edge_index), axis=-1)
    x = _layernorm(x + _L2_gnn_ref(x, L2_gnn_weight, L2_gnn_bias, src, dst), axis=-1)
    x = _layernorm(x + _L3_gnn_ref(x, edge_index, edge_attr_17, L3_gnn_W1, L3_gnn_b1, L3_gnn_W2, L3_gnn_b2, L3_gnn_Ws, L3_gnn_bs, L3_gnn_Wn, L3_gnn_bn), axis=-1)
    return x

_drawn_inputs = setup_inputs


def setup_inputs(seed=0):
    import zlib

    import numpy as np

    out = dict(_drawn_inputs(seed))
    spreads = {'L0_gnn_b1': (0.0, 0.1), 'L0_gnn_b2': (0.0, 0.1)}
    factors = {'edge_attr_17': 3.755, 'L3_gnn_b1': 4.093, 'L3_gnn_b2': 3.659}
    for name, (base, spread) in spreads.items():
        noise = np.random.default_rng([zlib.crc32(name.encode()), seed]).standard_normal(out[name].shape)
        drawn = base * np.exp(spread * noise) if base else spread * noise
        out[name] = jnp.asarray(drawn.astype(out[name].dtype))
    for name, factor in factors.items():
        out[name] = (out[name] * factor).astype(out[name].dtype)
    return out
```

```python
import numpy as np
import concourse.bass as bass
from concourse import mybir
from concourse.alu_op_type import AluOpType as ALU
from contextlib import ExitStack

F32 = mybir.dt.float32
BF16 = mybir.dt.bfloat16
I32 = mybir.dt.int32
ACT = mybir.ActivationFunctionType
AX_X = mybir.AxisListType.X

N, E, D, DE32, DE17 = 50000, 25000, 96, 32, 17
P = 128
TILES = -(-E // P)
EP = TILES * P
CH = 4
CW = CH * P
CHUNKS = TILES // CH
HALF = TILES // 2
PADKEY = 65535
SKIP = 60000.0
NB = 256
NH = HALF
NT = 2 * NH * NB
J = 10
BN = P * J
BLOCKS = N // BN
REST = N - BLOCKS * BN
NEG = -3.0e38
K_ITERS, ALPHA, BETA = 10, 0.1, 0.9
THETA = BETA ** K_ITERS + ALPHA * sum(BETA ** i for i in range(K_ITERS))
EPS = 1e-5
T1W = 98


def sweep(eng, count, unroll, body, peel=1):
    rounds = (count - 1) // unroll
    for c in range(peel * unroll):
        body(c // unroll, c % unroll)
    with eng.Fori(peel, rounds) as r:
        for u in range(unroll):
            body(r, u)
    for c in range(rounds * unroll, count):
        body(c // unroll, c % unroll)


class Phase:

    def __init__(self, nc, name):
        self.nc, self.name, self.ctx, self.sems = nc, name, ExitStack(), []

    def __enter__(self):
        return self

    def sb(self, name, shape, dt=F32):
        return self.ctx.enter_context(self.nc.sbuf_tensor(f"{self.name}_{name}", shape, dt))

    def ps(self, name, shape, dt=F32):
        return self.ctx.enter_context(self.nc.psum_tensor(f"{self.name}_{name}", shape, dt))

    def sem(self, name):
        s = self.ctx.enter_context(self.nc.semaphore(f"{self.name}_{name}"))
        self.sems.append(s)
        return s

    def __exit__(self, *exc):
        if exc[0] is None:
            self.nc.gpsimd.dma_reset()
            for s in self.sems:
                self.nc.gpsimd.sem_clear(s)
            self.nc.all_engine_barrier()
        self.ctx.close()


def held(eng, tick):
    eng.sem_inc(tick, 1)


def build(nc, a, out):
    dram = {}

    def scratch(name, shape, dt=F32):
        dram[name] = nc.dram_tensor(f"scr_{name}", shape, dt, kind="Internal").ap()
        return dram[name]

    srcp, dstp, dlast = scratch("srcp", (EP,), I32), scratch("dstp", (EP,), I32), scratch("dlast", (EP,), I32)
    slast = scratch("slast", (EP,), I32)
    dflag, sflag = scratch("dflag", (EP,), BF16), scratch("sflag", (EP,), BF16)
    sorted1, sorted2 = scratch("sorted1", (EP, 2), I32), scratch("sorted2", (EP, 2), I32)
    odeg, ideg, olast = scratch("odeg", (NT,)), scratch("ideg", (NT,)), scratch("olast", (NT,))
    aggd, aggs = scratch("aggd", (N, D)), scratch("aggs", (N, D))
    c1, x1, x2, x3, fn = (scratch(k, (N, D)) for k in ("c1", "x1", "x2", "x3", "fn"))
    t1 = scratch("t1", (N, T1W))
    sums = [scratch("sums0", (EP, D)), scratch("sums1", (EP, D))]

    keep = ExitStack()

    def sb(name, shape, dt=F32):
        return keep.enter_context(nc.sbuf_tensor(name, shape, dt))

    with keep:
        ident = sb("ident", [P, P])
        identb = sb("identb", [P, P], BF16)
        ident256 = sb("ident256", [P, P], BF16)
        tri = sb("tri", [P, P])
        trib = sb("trib", [P, P], BF16)
        ones = sb("ones", [P, P])
        onesb = sb("onesb", [P, P], BF16)
        iota = sb("iota", [P, NB], BF16)
        window = sb("window", [P, 2 * HALF - 1], BF16)
        srccol, dstcol = sb("srccol", [P, TILES], I32), sb("dstcol", [P, TILES], I32)
        srcg = sb("srcg", [P, TILES], I32)
        dlcol, slcol = sb("dlcol", [P, TILES], I32), sb("slcol", [P, TILES], I32)
        lastcol = sb("lastcol", [P, TILES], I32)
        flags = sb("flags", [D, EP], BF16)
        w_conv = [sb(f"w_conv{i}", [P, D]) for i in range(2)]
        w_root = [sb(f"w_root{i}", [D + 1, D]) for i in range(2)]
        w_gcn = sb("w_gcn", [D, D])
        w_h = sb("w_h", [P, D])
        w_2 = sb("w_2", [D + 1, D])
        w_s = sb("w_s", [D + 1, D])
        w_n = sb("w_n", [D, D])
        bias_gcn = sb("bias_gcn", [P, D])
        eps = sb("eps", [P, 1])
        rs_id, rs_od, fac, last_n = (sb(k, [P, BLOCKS + 1, J]) for k in ("rs_id", "rs_od", "fac", "last_n"))

        with Phase(nc, "setup") as ph:
            i32a = ph.sb("i32a", [P, NB], I32)
            zero = ph.sb("zero", [P, BN * D // P * 1])
            wt = ph.sb("wt", [D, 5, D])
            brow = ph.sb("brow", [1, 3, D])
            sF, dF, prv, nxt = (ph.sb(k, [P, TILES], I32) for k in ("sF", "dF", "prv", "nxt"))
            fl = ph.sb("fl", [P, TILES])
            lf = ph.sb("lf", [P, TILES])
            flb, li = ph.sb("flb", [P, TILES], BF16), ph.sb("li", [P, TILES], I32)
            pT = ph.ps("pT", [P, 4, P])
            s_c, s_v, s_ld, s_e, s_t, s_cp, s_st, s_z, s_b = (ph.sem(k) for k in (
                "iota", "dve", "weights_in", "edges_in", "turned", "copied", "stored", "zeroed", "bias_sum"))
            full, tail = (P - 1) * TILES, E - (P - 1) * TILES
            with nc.Block() as block:
                @block.gpsimd
                def _(pool):
                    nc.gpsimd.iota(i32a[:, :], pattern=[[1, NB]], base=0, channel_multiplier=0).then_inc(s_c, 1)
                    nc.gpsimd.memset(ones[:, :], 1.0).then_inc(s_c, 1)
                    pool.wait_ge(s_c, 2)
                    nc.gpsimd.affine_select(out=ident[:, :], in_=ones[:, :], compare_op=ALU.is_equal, fill=0.0,
                                            base=0, pattern=[[-1, P]], channel_multiplier=1).then_inc(s_c, 1)
                    nc.gpsimd.affine_select(out=tri[:, :], in_=ones[:, :], compare_op=ALU.is_gt, fill=0.0,
                                            base=0, pattern=[[1, P]], channel_multiplier=-1).then_inc(s_c, 1)

                @block.vector
                def _(dve):
                    nc.vector.memset(zero[:, :], 0.0)
                    nc.vector.memset(eps[:, :], EPS)
                    nc.vector.memset(w_h[:, :], 0.0)
                    nc.vector.memset(window[:, :], 0.0)
                    for x_ in (sF, dF):
                        nc.vector.memset(x_[:, :], PADKEY)
                    nc.vector.memset(nxt[:, :], PADKEY)
                    nc.vector.memset(prv[:, :], -1).then_inc(s_v, 1)
                    dve.wait_ge(s_v, 1)
                    nc.vector.memset(window[:, HALF - 1:HALF], 1.0)
                    dve.wait_ge(s_c, 4)
                    nc.vector.tensor_copy(iota[:, :], i32a[:, :])
                    nc.vector.tensor_copy(identb[:, :], ident[:, :])
                    nc.vector.tensor_copy(trib[:, :], tri[:, :])
                    nc.vector.tensor_copy(onesb[:, :], ones[:, :])
                    nc.vector.tensor_scalar(ident256[:, :], ident[:, :], float(NB), None, ALU.mult)
                    dve.wait_ge(s_e, 16 * 10)
                    nc.vector.tensor_tensor(fl[:, :], dF[:, :], prv[:, :], ALU.not_equal)
                    nc.vector.tensor_tensor(lf[:, :], dF[:, :], nxt[:, :], ALU.is_equal).then_inc(s_v, 1)
                    dve.wait_ge(s_v, 2)
                    nc.vector.tensor_scalar(flb[:, :], fl[:, :], NEG, None, ALU.mult)
                    nc.vector.scalar_tensor_tensor(lf[:, :], lf[:, :], 2.0 * PADKEY, dF[:, :], ALU.mult, ALU.add).then_inc(s_v, 1)
                    dve.wait_ge(s_v, 3)
                    nc.vector.tensor_scalar(li[:, :], lf[:, :], SKIP, None, ALU.min).then_inc(s_v, 1)
                    dve.wait_ge(s_t, 1)
                    nc.vector.tensor_copy(w_2[0:D, :], pT[0:D, 0, 0:D])
                    nc.vector.tensor_copy(w_s[0:D, :], pT[0:D, 1, 0:D])
                    nc.vector.tensor_copy(w_n[:, :], pT[0:D, 2, 0:D])
                    dve.wait_ge(s_ld, 16 * 17)
                    nc.vector.tensor_tensor(brow[:, 2, :], brow[:, 0, :], brow[:, 1, :], ALU.add).then_inc(s_v, 1)

                @block.tensor
                def _(pe):
                    pe.wait_ge(s_ld, 16 * 17)
                    pe.wait_ge(s_c, 4)
                    for n in range(3):
                        last = nc.tensor.transpose(pT[0:D, n, 0:D], wt[:, n, :], ident[0:D, 0:D])
                    last.then_inc(s_t, 1)

                @block.sync
                def _(sp):
                    sp.wait_ge(s_v, 1)
                    for flat, t in ((a["src"], sF), (a["dst"], dF)):
                        sp.dma_start(t[0:P - 1, :], flat[0:full].rearrange("(p j) -> p j", j=TILES)).then_inc(s_e, 16)
                        sp.dma_start(t[P - 1:P, 0:tail], flat[full:E].rearrange("(p j) -> p j", p=1)).then_inc(s_e, 16)
                    d = a["dst"]
                    sp.dma_start(prv[0:1, 1:TILES], d[0:TILES - 1].rearrange("(p j) -> p j", p=1)).then_inc(s_e, 16)
                    sp.dma_start(prv[1:P - 1, :], d[TILES - 1:full - 1].rearrange("(p j) -> p j", j=TILES)).then_inc(s_e, 16)
                    sp.dma_start(prv[P - 1:P, 0:tail + 1], d[full - 1:E].rearrange("(p j) -> p j", p=1)).then_inc(s_e, 16)
                    sp.dma_start(nxt[0:P - 1, :], d[1:full + 1].rearrange("(p j) -> p j", j=TILES)).then_inc(s_e, 16)
                    sp.dma_start(nxt[P - 1:P, 0:tail - 1], d[full + 1:E].rearrange("(p j) -> p j", p=1)).then_inc(s_e, 16)
                    sp.dma_start(bias_gcn[:, :], a["L2_gnn_bias"].rearrange("(p d) -> p d", p=1).broadcast_to([P, D])
                                 ).then_inc(s_e, 16)
                    sp.wait_ge(s_e, 16 * 10)
                    for flat, t in ((srcp, sF), (dstp, dF)):
                        sp.dma_start(flat.rearrange("(p j) -> p j", p=P), t[:, :]).then_inc(s_st, 16)
                    sp.wait_ge(s_v, 4)
                    sp.dma_start(dflag.rearrange("(p j) -> p j", p=P), flb[:, :]).then_inc(s_st, 16)
                    sp.dma_start(dlast.rearrange("(p j) -> p j", p=P), li[:, :]).then_inc(s_st, 16)
                    sp.wait_ge(s_v, 5)
                    sp.dma_start(w_s[D:D + 1, :], brow[:, 2, :]).then_inc(s_st, 16)
                    sp.wait_ge(s_st, 16 * 5)
                    sp.dma_start(flags[:, :], dflag.rearrange("(p e) -> p e", p=1).broadcast_to([D, EP])).then_inc(s_b, 16)
                    sp.wait_ge(s_b, 16)

                @block.scalar
                def _(act):
                    act.wait_ge(s_v, 1)
                    row = lambda v: v.rearrange("(p d) -> p d", p=1)
                    for i in range(2):
                        act.dma_start(w_conv[i][0:D, :], a[f"L0_gnn_W{i + 1}_msg"]).then_inc(s_ld, 16)
                        act.dma_start(w_conv[i][D:P, :], a[f"L0_gnn_W{i + 1}_edge"]).then_inc(s_ld, 16)
                        act.dma_start(w_root[i][0:D, :], a[f"L0_gnn_W{i + 1}_root"]).then_inc(s_ld, 16)
                        act.dma_start(w_root[i][D:D + 1, :], row(a[f"L0_gnn_b{i + 1}"])).then_inc(s_ld, 16)
                    act.dma_start(w_gcn[:, :], a["L2_gnn_weight"]).then_inc(s_ld, 16)
                    act.dma_start(wt[:, 0, :], a["L3_gnn_W2"]).then_inc(s_ld, 16)
                    act.dma_start(wt[:, 1, :], a["L3_gnn_Ws"]).then_inc(s_ld, 16)
                    act.dma_start(wt[:, 2, :], a["L3_gnn_Wn"]).then_inc(s_ld, 16)
                    act.dma_start(w_2[D:D + 1, :], row(a["L3_gnn_b2"])).then_inc(s_ld, 16)
                    act.dma_start(brow[:, 0, :], row(a["L3_gnn_bs"])).then_inc(s_ld, 16)
                    act.dma_start(brow[:, 1, :], row(a["L3_gnn_bn"])).then_inc(s_ld, 16)
                    act.dma_start(w_h[D:D + DE17, :], a["L3_gnn_W1"].rearrange("o k -> k o"), allow_slow_non_contiguous=True).then_inc(s_ld, 16)
                    act.dma_start(w_h[D + DE17:D + DE17 + 1, :], row(a["L3_gnn_b1"])).then_inc(s_ld, 16)
                    act.wait_ge(s_ld, 16 * 17)
                    for t in (aggd, aggs):
                        v = t[0:BLOCKS * BN, :].rearrange("(c p j) d -> c p (j d)", p=P, j=J)
                        for c in range(BLOCKS):
                            act.dma_start(v[c], zero[:, :]).then_inc(s_z, 16)
                        act.dma_start(t[BLOCKS * BN:N, :], zero[0:REST, 0:D]).then_inc(s_z, 16)
                    act.wait_ge(s_z, 16 * 2 * (BLOCKS + 1))

        def columns(name, src, words, outs, convert=None):
            with Phase(nc, name) as ph:
                raw, rawf = ph.sb("raw", [HALF, 2, P * words], I32), ph.sb("rawf", [HALF, 2, P * words])
                pt = ph.ps("pt", [P, 2 * words, P])
                s_in, s_f, s_t, s_o = (ph.sem(k) for k in ("rows_in", "as_float", "turned", "cols"))
                with nc.Block() as block:
                    @block.sync
                    def _(sp):
                        for h in range(2):
                            sp.dma_start(raw[:, h, :], src.rearrange("(h q n) -> h q n", h=2, q=HALF)[h]).then_inc(s_in, 16)

                    @block.vector
                    def _(dve):
                        dve.wait_ge(s_in, 32)
                        nc.vector.tensor_copy(rawf[:, :, :], raw[:, :, :]).then_inc(s_f, 1)
                        dve.wait_ge(s_t, 1)
                        for h in range(2):
                            for w in range(words):
                                nc.vector.tensor_copy(outs[w][:, h * HALF:(h + 1) * HALF], pt[:, h * words + w, 0:HALF])

                    @block.tensor
                    def _(pe):
                        pe.wait_ge(s_f, 1)
                        for h in range(2):
                            v = rawf[:, h, :].rearrange("q (n w) -> q w n", w=words)
                            for w in range(words):
                                last = nc.tensor.transpose(pt[:, h * words + w, 0:HALF], v[:, w, :], ident[0:HALF, 0:HALF])
                        last.then_inc(s_t, 1)

        columns("colsrc", srcp, 1, [srccol])
        columns("coldst", dstp, 1, [dstcol])
        columns("collast", dlast, 1, [dlcol])

        def edge_phase(name, mode, gidx=None, table=None, attr=None, de=0, sidx=None, target=None,
                       weight=None, hh=None, faccol=None, wr=None):
            turn_w = P if mode in ("conv", "edge") else D
            scatter = sidx is not None
            with Phase(nc, name) as ph:
                g = [ph.sb(f"g{u}", [P, CH, P]) for u in range(2)]
                f = [ph.sb(f"f{u}", [P, CH, D]) for u in range(2)] if mode == "prop" else g
                ts = [ph.sb(f"ts{u}", [P, CW]) for u in range(2)]
                sc = [ph.sb(f"sc{u}", [D, CW]) for u in range(2)]
                rows = [ph.sb(f"rows{u}", [P, CH, D]) for u in range(2)]
                gslot = [ph.sb(f"gslot{u}", [P, CH], I32) for u in range(2)]
                sslot = [ph.sb(f"sslot{u}", [P, CH], I32) for u in range(2)]
                pt = [ph.ps(f"pt{u}", [P, CW]) for u in range(2)]
                pr = [ph.ps(f"pr{u}", [P, CW]) for u in range(2)]
                pm = [ph.ps(f"pm{u}", [P, CW]) for u in range(2)]
                if mode == "edge":
                    ph_ = ph.ps("phid", [P, CW])
                    pw_ = ph.ps("pw", [P, CW])
                    hs = ph.sb("hs", [D + 1, CW])
                    msg = ph.sb("msg", [D, CW])
                s_g = [ph.sem(f"gathered{u}") for u in range(2)]
                s_at = [ph.sem(f"attr_in{u}") for u in range(2)]
                s_out = [ph.sem(f"out{u}") for u in range(2)]
                s_ready, s_slot, s_f, s_turn, s_te, s_mm, s_scan, s_back, s_rows, s_tick, s_hid, s_relu, s_w, s_msg, s_one = (
                    ph.sem(k) for k in ("buffers_ready", "slots", "formed", "turned", "turned_copied", "product",
                                        "scanned", "back", "rows", "tick", "hidden", "relu", "edge_weight", "message", "ones_row"))
                gw = T1W if mode == "init" else D

                with nc.Block() as block:
                    @block.gpsimd
                    def _(pool):
                        def put(r, u):
                            c = 2 * r + u
                            pool.wait_ge(s_rows, c + 1)
                            held(pool, s_tick)
                            for j in range(CH):
                                nc.gpsimd.indirect_dma_start(
                                    target[:, :], bass.IndirectOffsetOnAxis(ap=sslot[u][:, j:j + 1], axis=0),
                                    rows[u][:, j, :], None, bounds_check=N - 1, oob_is_err=False).then_inc(s_out[u], 16)

                        def step(r, u):
                            c = 2 * r + u
                            pool.wait_ge(s_slot, c + 1)
                            if not (isinstance(r, int) and r == 0):
                                pool.wait_ge(s_f if mode in ("prop", "init") else s_turn, c - 1)
                                if mode == "init":
                                    pool.wait_ge(s_turn, c - 1)
                            held(pool, s_tick)
                            for j in range(CH):
                                nc.gpsimd.indirect_dma_start(
                                    g[u][:, j, 0:gw], None, table[:, :],
                                    bass.IndirectOffsetOnAxis(ap=gslot[u][:, j:j + 1], axis=0)).then_inc(s_g[u], 16)
                            if scatter and not (isinstance(r, int) and r == 0):
                                put(r - 1, u)

                        if mode in ("conv", "edge"):
                            for u in range(2):
                                nc.gpsimd.memset(g[u][:, :, :], 1.0).then_inc(s_ready, 1)
                            pool.wait_ge(s_ready, 2)
                        sweep(pool, CHUNKS, 2, step)
                        if scatter:
                            put((CHUNKS - 2) // 2, (CHUNKS - 2) % 2)
                            put((CHUNKS - 1) // 2, (CHUNKS - 1) % 2)
                            pool.wait_ge(s_out[0], 64 * ((CHUNKS + 1) // 2))
                            pool.wait_ge(s_out[1], 64 * (CHUNKS // 2))
                        pool.wait_ge(s_g[0], 64 * ((CHUNKS + 1) // 2))
                        pool.wait_ge(s_g[1], 64 * (CHUNKS // 2))

                    @block.sync
                    def _(sp):
                        if attr is not None:
                            def load(r, u):
                                c = 2 * r + u
                                if isinstance(r, int) and r == 0:
                                    sp.wait_ge(s_ready, 2)
                                else:
                                    sp.wait_ge(s_turn, c - 1)
                                if isinstance(c, int) and c == CHUNKS - 1:
                                    left = E - c * CW
                                    nt = left // P
                                    sp.dma_start(g[u][:, 0:nt, D:D + de],
                                                 attr[c * CW:c * CW + nt * P, :].rearrange("(j p) d -> p j d", p=P)
                                                 ).then_inc(s_at[u], 16)
                                    sp.dma_start(g[u][0:left - nt * P, nt, D:D + de], attr[c * CW + nt * P:E, :]
                                                 ).then_inc(s_at[u], 16)
                                else:
                                    sp.dma_start(g[u][:, :, D:D + de],
                                                 attr[bass.ds(c * CW, CW), :].rearrange("(j p) d -> p j d", p=P)
                                                 ).then_inc(s_at[u], 16)
                            sweep(sp, CHUNKS, 2, load)
                        if wr is not None:
                            def store(r, u):
                                c = 2 * r + u
                                sp.wait_ge(s_rows, c + 1)
                                sp.dma_start(wr[bass.ds(c * CW, CW), :].rearrange("(j p) d -> p j d", p=P),
                                             rows[u][:, :, :]).then_inc(s_out[u], 16)
                            sweep(sp, CHUNKS, 2, store)
                            sp.wait_ge(s_out[0], 16 * ((CHUNKS + 1) // 2))
                            sp.wait_ge(s_out[1], 16 * (CHUNKS // 2))

                    @block.scalar
                    def _(act):
                        def slot(r, u):
                            c = 2 * r + u
                            if not (isinstance(r, int) and r == 0):
                                act.wait_ge(s_g[u], 64 * r)
                            nc.scalar.copy(gslot[u][:, :], gidx[:, bass.ds(c * CH, CH)]).then_inc(s_slot, 1)

                        def evict(r, u):
                            c = 2 * r + u
                            if not (isinstance(r, int) and r == 0):
                                act.wait_ge(s_out[u], (64 if scatter else 16) * r)
                            act.wait_ge(s_back, c + 1)
                            if scatter:
                                nc.scalar.copy(sslot[u][:, :], sidx[:, bass.ds(c * CH, CH)])
                            nc.scalar.copy(rows[u][:, :, :], pr[u][:, 0:CH * D].rearrange("p (j d) -> p j d", d=D)
                                           ).then_inc(s_rows, 1)

                        def step(r, u):
                            c = 2 * r + u
                            static = isinstance(c, int)
                            if not (static and c == CHUNKS - 1):
                                slot(r + u, 1 - u)
                            if mode == "init":
                                act.wait_ge(s_g[u], 64 * (r + 1))
                                nc.scalar.copy(hh[:, bass.ds(c * CH, CH), :], g[u][:, :, 0:D])
                                nc.scalar.copy(faccol[:, bass.ds(c * CH, CH)], g[u][:, :, D])
                                nc.scalar.copy(lastcol[:, bass.ds(c * CH, CH)], g[u][:, :, D + 1]).then_inc(s_f, 1)
                            if mode != "prop":
                                act.wait_ge(s_turn, c + 1)
                                if not (isinstance(r, int) and r == 0):
                                    act.wait_ge({"conv": s_mm, "edge": s_msg}.get(mode, s_scan), c - 1)
                                if mode == "init":
                                    nc.scalar.mul(ts[u][0:D, :], pt[u][0:D, :], 1.0 / ALPHA).then_inc(s_te, 1)
                                else:
                                    nc.scalar.copy(ts[u][0:turn_w, :], pt[u][0:turn_w, :]).then_inc(s_te, 1)
                            if mode == "edge":
                                act.wait_ge(s_hid, c + 1)
                                if not (static and c == 0):
                                    act.wait_ge(s_w, c)
                                nc.scalar.activation(hs[0:D, :], ph_[0:D, :], ACT.Relu).then_inc(s_relu, 1)
                            if not (static and c == 0):
                                evict(r + u - 1, 1 - u)

                        slot(0, 0)
                        sweep(act, CHUNKS, 2, step, peel=2)
                        evict((CHUNKS - 1) // 2, (CHUNKS - 1) % 2)

                    @block.tensor
                    def _(pe):
                        def back(r, u):
                            c = 2 * r + u
                            pe.wait_ge(s_scan, c + 1)
                            if not (isinstance(r, int) and r == 0):
                                pe.wait_ge(s_rows, c - 1)
                            for j in range(CH):
                                last = nc.tensor.matmul(pr[u][:, j * D:(j + 1) * D], sc[u][:, j * P:(j + 1) * P],
                                                        weight if weight is not None else ident[0:D, 0:D],
                                                        start=True, stop=True)
                            last.then_inc(s_back, 1)

                        def step(r, u):
                            c = 2 * r + u
                            static = isinstance(c, int)
                            first = isinstance(r, int) and r == 0
                            if mode == "prop":
                                pe.wait_ge(s_f, c + 1)
                                if not first:
                                    pe.wait_ge(s_scan, c - 1)
                            else:
                                pe.wait_ge(s_g[u], 64 * (r + 1))
                                if attr is not None:
                                    n_last = 32 if static and c == CHUNKS - 1 else 16
                                    pe.wait_ge(s_at[u], 16 * r + n_last)
                                if not first:
                                    pe.wait_ge(s_te, c - 1)
                            for j in range(CH):
                                last = nc.tensor.transpose(pt[u][0:turn_w, j * P:(j + 1) * P],
                                                           f[u][:, j, 0:turn_w], ident[:, :])
                            last.then_inc(s_turn, 1)
                            if mode == "conv":
                                pe.wait_ge(s_te, c + 1)
                                if not first:
                                    pe.wait_ge(s_scan, c - 1)
                                nc.tensor.matmul(pm[u][0:D, :], w_conv_used, ts[u][:, :], start=True, stop=True
                                                 ).then_inc(s_mm, 1)
                            if mode == "edge":
                                pe.wait_ge(s_te, c + 1)
                                if not (static and c == 0):
                                    pe.wait_ge(s_relu, c)
                                nc.tensor.matmul(ph_[0:D, :], w_h[:, :], ts[u][:, :], start=True, stop=True
                                                 ).then_inc(s_hid, 1)
                                pe.wait_ge(s_relu, c + 1)
                                if static and c == 0:
                                    pe.wait_ge(s_one, 1)
                                else:
                                    pe.wait_ge(s_msg, c)
                                nc.tensor.matmul(pw_[0:D, :], w_2[:, :], hs[:, :], start=True, stop=True
                                                 ).then_inc(s_w, 1)
                            if not (static and c == 0):
                                back(r + u - 1, 1 - u)

                        sweep(pe, CHUNKS, 2, step, peel=2)
                        back((CHUNKS - 1) // 2, (CHUNKS - 1) % 2)

                    @block.vector
                    def _(dve):
                        if mode == "edge":
                            nc.vector.memset(hs[D:D + 1, :], 1.0).then_inc(s_one, 1)

                        def form(r, u):
                            c = 2 * r + u
                            dve.wait_ge(s_g[u], 64 * (r + 1))
                            if not (isinstance(r, int) and r == 0):
                                dve.wait_ge(s_turn, c - 1)
                            for j in range(CH):
                                last = nc.vector.scalar_tensor_tensor(
                                    f[u][:, j, :], g[u][:, j, 0:D], faccol[:, bass.ds(c * CH + j, 1)],
                                    hh[:, bass.ds(c * CH + j, 1), :].rearrange("p o d -> p (o d)"), ALU.mult, ALU.add)
                            last.then_inc(s_f, 1)

                        def step(r, u):
                            c = 2 * r + u
                            static = isinstance(c, int)
                            first = isinstance(r, int) and r == 0
                            if mode == "edge":
                                dve.wait_ge(s_w, c + 1)
                                if not (static and c == 0):
                                    dve.wait_ge(s_scan, c)
                                nc.vector.tensor_tensor(msg[:, :], pw_[0:D, :], ts[u][0:D, :], ALU.mult
                                                        ).then_inc(s_msg, 1)
                                dve.wait_ge(s_msg, c + 1)
                                data = msg[:, :]
                            elif mode == "conv":
                                dve.wait_ge(s_mm, c + 1)
                                data = pm[u][0:D, :]
                            elif mode == "prop":
                                if static and c == 0:
                                    form(0, 0)
                                if not (static and c == CHUNKS - 1):
                                    form(r + u, 1 - u)
                                dve.wait_ge(s_turn, c + 1)
                                data = pt[u][0:D, :]
                            else:
                                dve.wait_ge(s_te, c + 1)
                                data = ts[u][0:D, :]
                            if not first:
                                dve.wait_ge(s_back, c - 1)
                            if not (static and c == 0):
                                dve.wait_ge(s_scan, c)
                            nc.vector.tensor_tensor_scan(
                                sc[u][:, :], flags[:, bass.ds(c * CW, CW)], data,
                                (0.0 if mode != "conv" else NEG) if static and c == 0 else sc[1 - u][:, CW - 1:CW],
                                ALU.add if mode == "conv" else ALU.mult,
                                ALU.max if mode == "conv" else ALU.add).then_inc(s_scan, 1)

                        sweep(dve, CHUNKS, 2, step)

        with Phase(nc, "clamp") as ph:
            with nc.Block() as block:
                @block.vector
                def _(dve):
                    nc.vector.tensor_scalar(srcg[:, :], srccol[:, :], float(N - 1), None, ALU.min)

        def dense_phase(name, mode):
            U = 3
            with Phase(nc, name) as ph:
                kinds = {"conv1": ["x", "aggd"], "conv2": ["c1", "aggd", "x"], "prop": ["x1", "aggs"],
                         "gcn": ["x2", "aggd"], "edge": ["x3", "aggd"]}[mode]
                product = mode in ("conv1", "conv2", "edge")
                wgt = {"conv1": w_root[0], "conv2": w_root[1], "edge": w_s}.get(mode)
                tabs = dict(dram, x=a["x"])
                bufs = [[ph.sb(f"in_{k}{u}", [P, J, D]) for k in kinds] for u in range(U)]
                xt = ph.sb("xt", [D + 1, J, P]) if product else None
                z = ph.sb("z", [P, J, D])
                z2 = ph.sb("z2", [P, J, D])
                sq = ph.sb("sq", [P, J, D])
                st = ph.sb("st", [P, 4, J])
                res = [ph.sb(f"res{u}", [P, J, D]) for u in range(2)]
                extra_w = {"conv2": T1W, "prop": D}.get(mode)
                ext = [ph.sb(f"ext{u}", [P, J, extra_w]) for u in range(2)] if extra_w else None
                pt = [ph.ps(f"pt{i}", [P, 4, P]) for i in range(3)] if product else None
                py = [ph.ps(f"py{i}", [P, 512]) for i in range(2)] if product else None
                s_in = [ph.sem(f"in{u}") for u in range(U)]
                s_st = [ph.sem(f"stored{u}") for u in range(2)]
                s_turn, s_xt, s_y, s_yd, s_z, s_v, s_sq, s_a, s_res, s_std, s_one = (ph.sem(k) for k in (
                    "turned", "xt", "product", "y_read", "z", "dve", "squares", "act", "result", "std", "ones"))
                n_in, n_out = len(kinds), 1 + (ext is not None)
                out_t = {"conv1": c1, "conv2": x1, "prop": x2, "gcn": x3, "edge": out}[mode]
                ext_t = {"conv2": t1, "prop": fn}.get(mode)

                def shape(c):
                    return (REST, 1) if isinstance(c, int) and c == BLOCKS else (P, J)

                def view(t, c):
                    p, j = shape(c)
                    return t[bass.ds(c * BN, p * j), :].rearrange("(p j) d -> p j d", j=j)

                def steps(eng, body):
                    def six(r, u):
                        body(6 * r + u, 2 * r + u // 3, u % 3, 3 * r + u // 2, u % 2)
                    sweep(eng, BLOCKS + 1, 6, six)

                with nc.Block() as block:
                    @block.sync
                    def _(sp):
                        def load(c, r3, u3, r2, u2):
                            p, j = shape(c)
                            if not (isinstance(c, int) and c < U):
                                sp.wait_ge(s_res, c - U + 1)
                            for k, b in zip(kinds, bufs[u3]):
                                sp.dma_start(b[0:p, 0:j, :], view(tabs[k], c)).then_inc(s_in[u3], 16)
                        steps(sp, load)

                    @block.gpsimd
                    def _(pool):
                        pass

                    @block.tensor
                    def _(pe):
                        if product:
                            def step(c, r3, u3, r2, u2):
                                p, jn = shape(c)
                                c0 = isinstance(c, int) and c == 0
                                pe.wait_ge(s_in[u3], 16 * n_in * (r3 + 1))
                                if not c0:
                                    pe.wait_ge(s_xt, c)
                                for j in range(jn):
                                    last = nc.tensor.transpose(pt[j // 4][0:D, j % 4, 0:p], bufs[u3][0][0:p, j, :],
                                                               ident[0:p, 0:p])
                                last.then_inc(s_turn, 1)
                                pe.wait_ge(s_xt, c + 1)
                                if c0:
                                    pe.wait_ge(s_one, 1)
                                else:
                                    pe.wait_ge(s_yd, c)
                                for j in range(jn):
                                    last = nc.tensor.matmul(py[j // 5][0:p, (j % 5) * D:(j % 5 + 1) * D],
                                                            xt[:, j, 0:p], wgt[:, :], start=True, stop=True)
                                last.then_inc(s_y, 1)
                            steps(pe, step)

                    @block.scalar
                    def _(act):
                        def step(c, r3, u3, r2, u2):
                            p, jn = shape(c)
                            c0 = isinstance(c, int) and c == 0
                            if product:
                                act.wait_ge(s_turn, c + 1)
                                if not c0:
                                    act.wait_ge(s_y, c)
                                for i in range(-(-jn // 4)):
                                    w = min(4, jn - 4 * i)
                                    last = nc.scalar.copy(xt[0:D, 4 * i:4 * i + w, 0:p], pt[i][0:D, 0:w, 0:p])
                                last.then_inc(s_xt, 1)
                            if mode != "conv1":
                                act.wait_ge(s_z, c + 1)
                                nc.scalar.activation(sq[0:p, 0:jn, :], z2[0:p, 0:jn, :], ACT.Square).then_inc(s_sq, 1)
                                act.wait_ge(s_std, c + 1)
                                nc.scalar.activation(st[0:p, 2, 0:jn], st[0:p, 1, 0:jn], ACT.Sqrt, bias=eps[0:p, :],
                                                     scale=1.0 / D).then_inc(s_a, 1)
                            act.wait_ge(s_res, c + 1)
                            act.dma_start(view(out_t, c), res[u2][0:p, 0:jn, :]).then_inc(s_st[u2], 16)
                            if ext is not None:
                                act.dma_start(view(ext_t, c), ext[u2][0:p, 0:jn, :]).then_inc(s_st[u2], 16)
                        steps(act, step)
                        for u in range(2):
                            act.wait_ge(s_st[u], 16 * n_out * ((BLOCKS + 1) // 2))

                    @block.vector
                    def _(dve):
                        if product:
                            nc.vector.memset(xt[D:D + 1, :, :], 1.0).then_inc(s_one, 1)

                        def step(c, r3, u3, r2, u2):
                            p, jn = shape(c)
                            c0 = isinstance(c, int) and c == 0
                            nv = {"conv1": 0, "conv2": 7, "prop": 8, "gcn": 6, "edge": 4}[mode]
                            at = [0]

                            def link(ins):
                                at[0] += 1
                                ins.then_inc(s_v, 1)
                                dve.wait_ge(s_v, c * nv + at[0])

                            B = [b[0:p, 0:jn, :] for b in bufs[u3]]
                            zz, zc, r_ = z[0:p, 0:jn, :], z2[0:p, 0:jn, :], res[u2][0:p, 0:jn, :]
                            s_ = lambda i: st[0:p, i, 0:jn]
                            wide = lambda s: s.rearrange("p (j o) -> p j o", o=1).broadcast_to([p, jn, D])
                            node = lambda t: t[0:p, bass.ds(c, 1), 0:jn].rearrange("p c j -> p (c j)")
                            dve.wait_ge(s_in[u3], 16 * n_in * (r3 + 1))
                            if not (isinstance(c, int) and c < 2):
                                dve.wait_ge(s_st[u2], 16 * n_out * r2)
                            if product:
                                dve.wait_ge(s_y, c + 1)
                                for i in range(-(-jn // 5)):
                                    w = min(5, jn - 5 * i)
                                    last = nc.vector.tensor_tensor(
                                        z[0:p, 5 * i:5 * i + w, :],
                                        py[i][0:p, 0:w * D].rearrange("p (j d) -> p j d", d=D),
                                        bufs[u3][1][0:p, 5 * i:5 * i + w, :], ALU.add)
                                last.then_inc(s_yd, 1)
                                dve.wait_ge(s_yd, c + 1)
                            if mode == "conv1":
                                nc.vector.scalar_tensor_tensor(r_, zz, 0.01, zz, ALU.mult, ALU.max).then_inc(s_res, 1)
                                return
                            if mode == "conv2":
                                link(nc.vector.scalar_tensor_tensor(zz, zz, 0.01, zz, ALU.mult, ALU.max))
                                link(nc.vector.tensor_tensor(zz, zz, B[2], ALU.add))
                            elif mode == "edge":
                                link(nc.vector.scalar_tensor_tensor(zz, zz, 0.0, B[0], ALU.max, ALU.add))
                            elif mode == "prop":
                                link(nc.vector.tensor_tensor(zz, B[1], wide(node(rs_od)), ALU.mult))
                                link(nc.vector.tensor_scalar(zc, B[0], (1.0 + ALPHA / THETA) * THETA / BETA, None, ALU.mult))
                                link(nc.vector.tensor_tensor(zz, zz, zc, ALU.add))
                                link(nc.vector.tensor_scalar(zz, zz, BETA / THETA, None, ALU.mult))
                            else:
                                link(nc.vector.tensor_tensor(zz, B[1], wide(node(rs_id)), ALU.mult))
                                link(nc.vector.tensor_tensor(zz, zz, B[0], ALU.add))
                                link(nc.vector.tensor_tensor(
                                    zz, zz, bias_gcn[0:p, :].rearrange("p (o d) -> p o d", o=1).broadcast_to([p, jn, D]),
                                    ALU.add))
                            link(nc.vector.tensor_reduce(s_(0), zz, AX_X, ALU.add))
                            link(nc.vector.tensor_scalar(s_(0), s_(0), 1.0 / D, None, ALU.mult))
                            if not c0:
                                dve.wait_ge(s_sq, c)
                            nc.vector.tensor_tensor(zc, zz, wide(s_(0)), ALU.subtract).then_inc(s_z, 1)
                            dve.wait_ge(s_sq, c + 1)
                            nc.vector.tensor_reduce(s_(1), sq[0:p, 0:jn, :], AX_X, ALU.add).then_inc(s_std, 1)
                            dve.wait_ge(s_a, c + 1)
                            link(nc.vector.reciprocal(s_(3), s_(2)))
                            if mode in ("gcn", "edge"):
                                nc.vector.tensor_tensor(r_, zc, wide(s_(3)), ALU.mult).then_inc(s_res, 1)
                            elif mode == "conv2":
                                link(nc.vector.tensor_tensor(r_, zc, wide(s_(3)), ALU.mult))
                                e_ = ext[u2]
                                nc.vector.tensor_copy(e_[0:p, 0:jn, D], node(fac))
                                nc.vector.tensor_copy(e_[0:p, 0:jn, D + 1], node(last_n))
                                link(nc.vector.tensor_tensor(e_[0:p, 0:jn, 0:D], r_, wide(node(rs_id)), ALU.mult))
                                nc.vector.tensor_scalar(e_[0:p, 0:jn, 0:D], e_[0:p, 0:jn, 0:D], ALPHA, None,
                                                        ALU.mult).then_inc(s_res, 1)
                            else:
                                link(nc.vector.tensor_tensor(r_, zc, wide(s_(3)), ALU.mult))
                                nc.vector.tensor_tensor(ext[u2][0:p, 0:jn, :], r_, wide(node(rs_od)), ALU.mult
                                                        ).then_inc(s_res, 1)
                            assert at[0] == nv, (mode, at[0], nv)
                        steps(dve, step)

        def histogram(name, cols, table, last_table=None):
            with Phase(nc, name) as ph:
                lo, hi = ph.sb("lo", [P, TILES]), ph.sb("hi", [P, TILES])
                loi, hii = ph.sb("loi", [P, TILES], I32), ph.sb("hii", [P, TILES], I32)
                ohl = [ph.sb(f"ohl{u}", [P, CH, NB], BF16) for u in range(2)]
                ohh = [ph.sb(f"ohh{u}", [P, CH, 2 * NH], BF16) for u in range(2)]
                hist, run = ph.sb("hist", [NH, 2, NB]), ph.sb("run", [NH, 2, NB])
                ones_row = ph.sb("ones_row", [NH, NB])
                off = ph.sb("off", [NH, 2])
                acc = [ph.ps(f"acc{h}", [P, 512]) for h in range(2)]
                po = ph.ps("po", [P, 512])
                po2 = ph.ps("po2", [P, 512])
                s_oh, s_mm, s_h, s_r, s_o, s_st, s_v = (ph.sem(k) for k in (
                    "onehots", "added", "hist", "run", "offsets", "stored", "dve"))
                with nc.Block() as block:
                    @block.vector
                    def _(dve):
                        nc.vector.memset(ones_row[:, :], 1.0)
                        nc.vector.tensor_scalar(hii[:, :], cols[:, :], 8, None, ALU.arith_shift_right)
                        nc.vector.tensor_scalar(loi[:, :], cols[:, :], NB - 1, None, ALU.bitwise_and).then_inc(s_v, 1)
                        dve.wait_ge(s_v, 1)
                        nc.vector.tensor_copy(hi[:, :], hii[:, :])
                        nc.vector.tensor_copy(lo[:, :], loi[:, :]).then_inc(s_v, 1)
                        dve.wait_ge(s_v, 2)

                        def step(r, u):
                            c = 2 * r + u
                            if not (isinstance(r, int) and r == 0):
                                dve.wait_ge(s_mm, c - 1)
                            for j in range(CH):
                                nc.vector.tensor_scalar(ohl[u][:, j, :], iota[:, :], lo[:, bass.ds(c * CH + j, 1)], None, ALU.is_equal)
                                last = nc.vector.tensor_scalar(ohh[u][:, j, :], iota[:, 0:2 * NH], hi[:, bass.ds(c * CH + j, 1)],
                                                               None, ALU.is_equal)
                            last.then_inc(s_oh, 1)
                        sweep(dve, CHUNKS, 2, step)
                        dve.wait_ge(s_mm, CHUNKS)
                        nc.vector.tensor_copy(hist[:, 0, :], acc[0][0:NH, 0:NB])
                        nc.vector.tensor_copy(hist[:, 1, :], acc[1][0:NH, 0:NB]).then_inc(s_h, 1)
                        if last_table is not None:
                            dve.wait_ge(s_h, 1)
                            for h in range(2):
                                last = nc.vector.tensor_tensor_scan(run[:, h, :], ones_row[:, :], hist[:, h, :], 0.0,
                                                                    ALU.mult, ALU.add)
                            last.then_inc(s_r, 1)
                            dve.wait_ge(s_o, 1)
                            nc.vector.tensor_copy(off[:, 0:1], po[0:NH, 0:1])
                            nc.vector.tensor_copy(off[:, 1:2], po2[0:NH, 0:1]).then_inc(s_v, 1)
                            dve.wait_ge(s_v, 3)
                            dve.wait_ge(s_r, 1)
                            for h in range(2):
                                last = nc.vector.tensor_scalar(run[:, h, :], run[:, h, :], off[:, h:h + 1], -1.0, ALU.add, ALU.add)
                            last.then_inc(s_r, 1)
                            dve.wait_ge(s_r, 2)
                            nc.vector.tensor_scalar(run[:, :, :], run[:, :, :], 0.0, None, ALU.max).then_inc(s_r, 1)

                    @block.tensor
                    def _(pe):
                        def step(r, u):
                            c = 2 * r + u
                            static = isinstance(c, int)
                            pe.wait_ge(s_oh, c + 1)
                            for j in range(CH):
                                for h in range(2):
                                    last = nc.tensor.matmul(acc[h][0:NH, 0:NB], ohh[u][:, j, h * NH:(h + 1) * NH], ohl[u][:, j, :],
                                                            start=static and c == 0 and j == 0,
                                                            stop=static and c == CHUNKS - 1 and j == CH - 1)
                            last.then_inc(s_mm, 1)
                        sweep(pe, CHUNKS, 2, step)
                        if last_table is not None:
                            pe.wait_ge(s_r, 1)
                            nc.tensor.matmul(po[0:NH, 0:1], tri[0:NH, 0:NH], run[:, 0, NB - 1:NB], start=True, stop=True)
                            nc.tensor.matmul(po2[0:NH, 0:1], tri[0:NH, 0:NH], run[:, 1, NB - 1:NB], start=True, stop=False)
                            nc.tensor.matmul(po2[0:NH, 0:1], ones[0:NH, 0:NH], run[:, 0, NB - 1:NB], start=False, stop=True
                                             ).then_inc(s_o, 1)

                    @block.sync
                    def _(sp):
                        view = lambda t: t.rearrange("(h q n) -> q h n", h=2, q=NH)
                        sp.wait_ge(s_h, 1)
                        sp.dma_start(view(table), hist[:, :, :]).then_inc(s_st, 16)
                        if last_table is not None:
                            sp.wait_ge(s_r, 3)
                            sp.dma_start(view(last_table), run[:, :, :]).then_inc(s_st, 16)
                        sp.wait_ge(s_st, 32 if last_table is not None else 16)

        def radix_pass(name, keys, vals, shift, target):
            with Phase(nc, name) as ph:
                dig, digi = ph.sb("dig", [P, TILES]), ph.sb("digi", [P, TILES], I32)
                oh = [ph.sb(f"oh{u}", [P, CH, NB], BF16) for u in range(2)]
                junk = ph.sb("junk", [P, NB])
                cnt = [ph.sb(f"cnt{h}", [HALF, NB], BF16) for h in range(2)]
                cntf = ph.sb("cntf", [HALF, NB])
                base = ph.sb("base", [HALF, NB + 1])
                tot = ph.sb("tot", [HALF, NB])
                ones_row = ph.sb("ones_row", [HALF, NB])
                rf = [ph.sb(f"rf{h}", [HALF, NB]) for h in range(2)]
                ri = [ph.sb(f"ri{h}", [HALF, NB], I32) for h in range(2)]
                rhi_i, rlo_i = ([ph.sb(f"{k}{h}", [HALF, NB], I32) for h in range(2)] for k in ("rhi_i", "rlo_i"))
                rhi, rlo = ([ph.sb(f"{k}{h}", [HALF, NB], BF16) for h in range(2)] for k in ("rhi", "rlo"))
                posf = [ph.sb(f"posf{u}", [P, CH]) for u in range(2)]
                pos = [ph.sb(f"pos{u}", [P, CH], I32) for u in range(2)]
                pay = [ph.sb(f"pay{u}", [P, CH, 2], I32) for u in range(2)]
                acc = [ph.ps(f"acc{h}", [P, 512]) for h in range(2)]
                pp = [ph.ps(f"pp{u}", [P, CH, NB]) for u in range(2)]
                s_v, s_oh, s_cnt, s_c, s_pre, s_r, s_oh2, s_pos, s_rank, s_pay, s_tick = (ph.sem(k) for k in (
                    "dve", "onehots", "counted", "counts", "prefixes", "bases", "onehots2", "positions", "ranked", "payload", "tick"))
                s_sc = [ph.sem(f"scattered{u}") for u in range(2)]
                with nc.Block() as block:
                    @block.vector
                    def _(dve):
                        at = [0]

                        def link(ins):
                            at[0] += 1
                            ins.then_inc(s_v, 1)
                            dve.wait_ge(s_v, at[0])

                        nc.vector.memset(ones_row[:, :], 1.0)
                        if shift:
                            link(nc.vector.tensor_scalar(digi[:, :], keys[:, :], shift, None, ALU.arith_shift_right))
                        else:
                            link(nc.vector.tensor_scalar(digi[:, :], keys[:, :], NB - 1, None, ALU.bitwise_and))
                        link(nc.vector.tensor_copy(dig[:, :], digi[:, :]))

                        def onehots(c, u, sem):
                            for j in range(CH):
                                last = nc.vector.tensor_scalar(oh[u][:, j, :], iota[:, :], dig[:, bass.ds(c * CH + j, 1)],
                                                               None, ALU.is_equal)
                            last.then_inc(sem, 1)

                        def count(r, u):
                            if not (isinstance(r, int) and r == 0):
                                dve.wait_ge(s_cnt, 2 * r + u - 1)
                            onehots(2 * r + u, u, s_oh)
                        sweep(dve, CHUNKS, 2, count)
                        dve.wait_ge(s_cnt, CHUNKS)
                        nc.vector.tensor_copy(cntf[:, :], acc[0][0:HALF, 0:NB])
                        nc.vector.tensor_copy(cnt[0][:, :], acc[0][0:HALF, 0:NB])
                        nc.vector.tensor_copy(cnt[1][:, :], acc[1][0:HALF, 0:NB]).then_inc(s_c, 1)
                        dve.wait_ge(s_pre, 1)
                        nc.vector.memset(base[:, 0:1], 0.0)
                        link(nc.vector.tensor_copy(tot[:, :], acc[1][0:HALF, 0:NB]))
                        link(nc.vector.tensor_tensor_scan(base[:, 1:NB + 1], ones_row[:, :], tot[:, :], 0.0, ALU.mult, ALU.add))
                        link(nc.vector.tensor_tensor(rf[0][:, :], acc[0][0:HALF, 0:NB], base[:, 0:NB], ALU.add))
                        link(nc.vector.tensor_tensor(rf[1][:, :], rf[0][:, :], cntf[:, :], ALU.add))
                        for h in range(2):
                            link(nc.vector.tensor_copy(ri[h][:, :], rf[h][:, :]))
                            nc.vector.tensor_scalar(rhi_i[h][:, :], ri[h][:, :], 8, None, ALU.arith_shift_right)
                            link(nc.vector.tensor_scalar(rlo_i[h][:, :], ri[h][:, :], NB - 1, None, ALU.bitwise_and))
                            nc.vector.tensor_copy(rhi[h][:, :], rhi_i[h][:, :])
                            last = nc.vector.tensor_copy(rlo[h][:, :], rlo_i[h][:, :])
                        last.then_inc(s_r, 1)

                        def ready(r, u):
                            if not (isinstance(r, int) and r == 0):
                                dve.wait_ge(s_rank, 2 * r + u - 1)
                            onehots(2 * r + u, u, s_oh2)

                        def rank(r, u):
                            c = 2 * r + u
                            static = isinstance(c, int)
                            if static and c == 0:
                                ready(0, 0)
                            if not (static and c == CHUNKS - 1):
                                ready(r + u, 1 - u)
                            dve.wait_ge(s_pos, c + 1)
                            if not (isinstance(r, int) and r == 0):
                                dve.wait_ge(s_sc[u], 64 * r)
                            for j in range(CH):
                                if not (static and c == 0 and j == 0):
                                    dve.wait_ge(s_v, v0 + CH * c + j)
                                nc.vector.tensor_tensor_reduce(out=junk[:, :], in0=oh[u][:, j, :], in1=pp[u][:, j, :],
                                                               scale=1.0, scalar=0.0, op0=ALU.mult, op1=ALU.add,
                                                               accum_out=posf[u][:, j:j + 1]).then_inc(s_v, 1)
                            dve.wait_ge(s_v, v0 + CH * c + CH)
                            nc.vector.tensor_copy(pos[u][:, :], posf[u][:, :]).then_inc(s_rank, 1)
                        v0 = at[0]
                        dve.wait_ge(s_cnt, CHUNKS)
                        sweep(dve, CHUNKS, 2, rank)

                    @block.tensor
                    def _(pe):
                        def count(r, u):
                            c = 2 * r + u
                            static = isinstance(c, int)
                            pe.wait_ge(s_oh, c + 1)
                            for j in range(CH):
                                last = nc.tensor.matmul(acc[j % 2][0:HALF, 0:NB],
                                                        window[:, bass.ds(HALF - 1 - (2 * c + j // 2), HALF)], oh[u][:, j, :],
                                                        start=static and c == 0 and j < 2,
                                                        stop=static and c == CHUNKS - 1 and j >= 2)
                            last.then_inc(s_cnt, 1)
                        sweep(pe, CHUNKS, 2, count)
                        pe.wait_ge(s_c, 1)
                        nc.tensor.matmul(acc[0][0:HALF, 0:NB], trib[0:HALF, 0:HALF], cnt[0][:, :], start=True, stop=False)
                        nc.tensor.matmul(acc[0][0:HALF, 0:NB], trib[0:HALF, 0:HALF], cnt[1][:, :], start=False, stop=True)
                        nc.tensor.matmul(acc[1][0:HALF, 0:NB], onesb[0:HALF, 0:HALF], cnt[0][:, :], start=True, stop=False)
                        nc.tensor.matmul(acc[1][0:HALF, 0:NB], onesb[0:HALF, 0:HALF], cnt[1][:, :], start=False, stop=True
                                         ).then_inc(s_pre, 1)
                        pe.wait_ge(s_r, 1)

                        def place(r, u):
                            c = 2 * r + u
                            pe.wait_ge(s_oh2, c + 1)
                            if not (isinstance(r, int) and r == 0):
                                pe.wait_ge(s_rank, c - 1)
                            for j in range(CH):
                                nc.tensor.matmul(pp[u][:, j, :], trib[:, :], oh[u][:, j, :], start=True, stop=False)
                                for idn, rr in ((ident256, rhi), (identb, rlo)):
                                    last = nc.tensor.matmul(
                                        pp[u][:, j, :],
                                        idn[0:HALF, bass.ds(2 * c + j // 2, 1)].broadcast_to([HALF, P]),
                                        rr[j % 2][:, :], start=False, stop=rr is rlo)
                            last.then_inc(s_pos, 1)
                        sweep(pe, CHUNKS, 2, place)

                    @block.scalar
                    def _(act):
                        def step(r, u):
                            c = 2 * r + u
                            if not (isinstance(r, int) and r == 0):
                                act.wait_ge(s_sc[u], 64 * r)
                            nc.scalar.copy(pay[u][:, :, 0], keys[:, bass.ds(c * CH, CH)])
                            nc.scalar.copy(pay[u][:, :, 1], vals[:, bass.ds(c * CH, CH)]).then_inc(s_pay, 1)
                        sweep(act, CHUNKS, 2, step)

                    @block.gpsimd
                    def _(pool):
                        def step(r, u):
                            c = 2 * r + u
                            pool.wait_ge(s_pay, c + 1)
                            pool.wait_ge(s_rank, c + 1)
                            held(pool, s_tick)
                            for j in range(CH):
                                nc.gpsimd.indirect_dma_start(
                                    target[:, :], bass.IndirectOffsetOnAxis(ap=pos[u][:, j:j + 1], axis=0),
                                    pay[u][:, j, :], None).then_inc(s_sc[u], 16)
                        sweep(pool, CHUNKS, 2, step)
                        pool.wait_ge(s_sc[0], 64 * ((CHUNKS + 1) // 2))
                        pool.wait_ge(s_sc[1], 64 * (CHUNKS // 2))

        w_conv_used = w_conv[0][:, :]
        edge_phase("conv1", "conv", gidx=srcg, table=a["x"], attr=a["edge_attr_32"], de=DE32, sidx=dlcol, target=aggd)
        dense_phase("node1", "conv1")
        w_conv_used = w_conv[1][:, :]
        edge_phase("conv2", "conv", gidx=srcg, table=c1, attr=a["edge_attr_32"], de=DE32, sidx=dlcol, target=aggd)

        histogram("hout", srccol, odeg, olast)
        histogram("hin", dstcol, ideg)

        with Phase(nc, "factors") as ph:
            od = ph.sb("od", [P, BLOCKS + 1, J])
            has = ph.sb("has", [P, BLOCKS + 1, J])
            s_in, s_m, s_v, s_a = (ph.sem(k) for k in ("tables_in", "cleared", "dve", "act"))
            with nc.Block() as block:
                @block.sync
                def _(sp):
                    sp.wait_ge(s_m, 1)
                    for t, dst in ((odeg, od), (ideg, rs_id), (olast, last_n)):
                        sp.dma_start(dst[:, 0:BLOCKS, :], t[0:BLOCKS * BN].rearrange("(c p j) -> p c j", p=P, j=J)).then_inc(s_in, 16)
                        sp.dma_start(dst[0:REST, BLOCKS, 0:1], t[BLOCKS * BN:N].rearrange("(p j) -> p j", j=1)).then_inc(s_in, 16)

                @block.vector
                def _(dve):
                    for t in (od, rs_id, last_n):
                        last = nc.vector.memset(t[:, :, :], 1.0)
                    last.then_inc(s_m, 1)
                    dve.wait_ge(s_in, 96)
                    nc.vector.tensor_scalar(has[:, :, :], od[:, :, :], 0.0, BETA, ALU.is_gt, ALU.mult)
                    nc.vector.tensor_scalar(rs_od[:, :, :], od[:, :, :], 1.0, None, ALU.max)
                    nc.vector.tensor_scalar(rs_id[:, :, :], rs_id[:, :, :], 1.0, None, ALU.max).then_inc(s_v, 1)
                    dve.wait_ge(s_a, 1)
                    nc.vector.reciprocal(rs_od[:, :, :], rs_od[:, :, :])
                    nc.vector.reciprocal(rs_id[:, :, :], rs_id[:, :, :]).then_inc(s_v, 1)
                    dve.wait_ge(s_v, 2)
                    nc.vector.tensor_tensor(fac[:, :, :], rs_od[:, :, :], rs_id[:, :, :], ALU.mult).then_inc(s_v, 1)
                    dve.wait_ge(s_v, 3)
                    nc.vector.tensor_tensor(fac[:, :, :], fac[:, :, :], has[:, :, :], ALU.mult)

                @block.scalar
                def _(act):
                    act.wait_ge(s_v, 1)
                    nc.scalar.activation(rs_od[:, :, :], rs_od[:, :, :], ACT.Sqrt)
                    nc.scalar.activation(rs_id[:, :, :], rs_id[:, :, :], ACT.Sqrt).then_inc(s_a, 1)

        dense_phase("node2", "conv2")

        radix_pass("radix1", srccol, dstcol, 0, sorted1)
        k1, v1 = sb("k1", [P, TILES], I32), sb("v1", [P, TILES], I32)
        columns("colsort1", sorted1.rearrange("e w -> (e w)"), 2, [k1, v1])
        radix_pass("radix2", k1, v1, 8, sorted2)
        columns("colsort2", sorted2.rearrange("e w -> (e w)"), 2, [k1, v1])

        def order_flags():
            with Phase(nc, "runs") as ph:
                pair = ph.sb("pair", [P, TILES, 2], I32)
                prv, nxt = ph.sb("prv", [P, TILES, 2], I32), ph.sb("nxt", [P, TILES, 2], I32)
                fl, lf = ph.sb("fl", [P, TILES]), ph.sb("lf", [P, TILES])
                flb, li = ph.sb("flb", [P, TILES], BF16), ph.sb("li", [P, TILES], I32)
                s_m, s_in, s_v, s_st, s_b = (ph.sem(k) for k in ("cleared", "in", "dve", "stored", "broadcast"))
                rows2 = sorted2.rearrange("(p j) w -> p j w", p=P)
                flat2 = sorted2
                with nc.Block() as block:
                    @block.vector
                    def _(dve):
                        nc.vector.memset(prv[:, :, :], -1)
                        nc.vector.memset(nxt[:, :, :], -1).then_inc(s_m, 1)
                        nc.vector.tensor_scalar(v1[:, :], v1[:, :], float(N - 1), None, ALU.min)
                        dve.wait_ge(s_in, 16 * 5)
                        nc.vector.tensor_tensor(fl[:, :], pair[:, :, 0], prv[:, :, 0], ALU.is_equal)
                        nc.vector.tensor_tensor(lf[:, :], pair[:, :, 0], nxt[:, :, 0], ALU.is_equal).then_inc(s_v, 1)
                        dve.wait_ge(s_v, 1)
                        nc.vector.tensor_copy(flb[:, :], fl[:, :])
                        nc.vector.scalar_tensor_tensor(lf[:, :], lf[:, :], 2.0 * PADKEY, pair[:, :, 0], ALU.mult, ALU.add).then_inc(s_v, 1)
                        dve.wait_ge(s_v, 2)
                        nc.vector.tensor_scalar(li[:, :], lf[:, :], SKIP, None, ALU.min).then_inc(s_v, 1)

                    @block.sync
                    def _(sp):
                        sp.wait_ge(s_m, 1)
                        sp.dma_start(pair[:, :, :], rows2).then_inc(s_in, 16)
                        sp.dma_start(prv[0:1, 1:TILES, :], flat2[0:TILES - 1, :].rearrange("(p j) w -> p j w", p=1)).then_inc(s_in, 16)
                        sp.dma_start(prv[1:P, :, :], flat2[TILES - 1:EP - 1, :].rearrange("(p j) w -> p j w", j=TILES)).then_inc(s_in, 16)
                        sp.dma_start(nxt[0:P - 1, :, :], flat2[1:EP - TILES + 1, :].rearrange("(p j) w -> p j w", j=TILES)).then_inc(s_in, 16)
                        sp.dma_start(nxt[P - 1:P, 0:TILES - 1, :], flat2[EP - TILES + 1:EP, :].rearrange("(p j) w -> p j w", p=1)).then_inc(s_in, 16)
                        sp.wait_ge(s_v, 3)
                        sp.dma_start(sflag.rearrange("(p j) -> p j", p=P), flb[:, :]).then_inc(s_st, 16)
                        sp.dma_start(slast.rearrange("(p j) -> p j", p=P), li[:, :]).then_inc(s_st, 16)
                        sp.wait_ge(s_st, 32)
                        sp.dma_start(flags[:, :], sflag.rearrange("(p e) -> p e", p=1).broadcast_to([D, EP])).then_inc(s_b, 16)
                        sp.wait_ge(s_b, 16)

        order_flags()
        columns("colslast", slast, 1, [slcol])

        prop = ExitStack()
        with prop:
            hh = prop.enter_context(nc.sbuf_tensor("hh", [P, TILES, D], F32))
            faccol = prop.enter_context(nc.sbuf_tensor("faccol", [P, TILES], F32))
            edge_phase("prop0", "init", gidx=v1, table=t1, hh=hh, faccol=faccol, wr=sums[0])
            with nc.Fori(0, (K_ITERS - 2) // 2):
                for n in range(2):
                    edge_phase(f"prop{1 + n}", "prop", gidx=lastcol, table=sums[n], hh=hh, faccol=faccol, wr=sums[1 - n])
            edge_phase("prop9", "prop", gidx=lastcol, table=sums[0], hh=hh, faccol=faccol, sidx=slcol, target=aggs)
        dense_phase("node3", "prop")

        with Phase(nc, "dflags") as ph:
            s_in = ph.sem("in")
            s_v = ph.sem("dve")
            with nc.Block() as block:
                @block.sync
                def _(sp):
                    sp.dma_start(flags[:, :], dflag.rearrange("(p e) -> p e", p=1).broadcast_to([D, EP])).then_inc(s_in, 16)

                @block.vector
                def _(dve):
                    dve.wait_ge(s_in, 16)
                    nc.vector.tensor_scalar(flags[:, :], flags[:, :], -1.0, None, ALU.is_ge)

        edge_phase("gcn", "gcn", gidx=srcg, table=fn, sidx=dlcol, target=aggd, weight=w_gcn[:, :])
        dense_phase("node4", "gcn")
        edge_phase("edge", "edge", gidx=srcg, table=x3, attr=a["edge_attr_17"], de=DE17, sidx=dlcol, target=aggd,
                   weight=w_n[:, :])
        dense_phase("node5", "edge")


_INS = ["x", "src", "dst", "edge_attr_17", "edge_attr_32", "L0_gnn_W1_msg", "L0_gnn_W1_edge", "L0_gnn_W1_root",
        "L0_gnn_b1", "L0_gnn_W2_msg", "L0_gnn_W2_edge", "L0_gnn_W2_root", "L0_gnn_b2", "L2_gnn_weight", "L2_gnn_bias",
        "L3_gnn_W1", "L3_gnn_b1", "L3_gnn_W2", "L3_gnn_b2", "L3_gnn_Ws", "L3_gnn_bs", "L3_gnn_Wn", "L3_gnn_bn"]


def kernel(**inputs):
    import concourse.bacc as _bacc
    from concourse.bass_utils import run_bass_kernel_spmd as _run
    nc = _bacc.Bacc("TRN2", target_bir_lowering=False, num_devices=1)
    arrays, args = {}, {}
    for name in _INS:
        v = np.ascontiguousarray(inputs[name])
        arrays[f"in_{name}"] = v
        args[name] = nc.dram_tensor(f"in_{name}", v.shape, mybir.dt.from_np(v.dtype), kind="ExternalInput").ap()
    out = nc.dram_tensor("out_0", (N, D), F32, kind="ExternalOutput").ap()
    build(nc, args, out)
    r = _run(nc, [arrays], core_ids=[0])
    return r.results[0]["out_0"]
```

```python
import numpy as np
import concourse.bass as bass
from concourse import mybir
from concourse.alu_op_type import AluOpType as ALU
from contextlib import ExitStack

F32 = mybir.dt.float32
BF16 = mybir.dt.bfloat16
I32 = mybir.dt.int32
ACT = mybir.ActivationFunctionType
AX_X = mybir.AxisListType.X

N, E, D, DE32, DE17 = 50000, 25000, 96, 32, 17
P = 128
TILES = -(-E // P)
EP = TILES * P
CH = 4
CW = CH * P
CHUNKS = TILES // CH
GR = 4
HALF = TILES // 2
PADKEY = 65535
SKIP = 60000.0
NB = 256
NH = HALF
NT = 2 * NH * NB
J = 10
BN = P * J
BLOCKS = N // BN
REST = N - BLOCKS * BN
NEG = -3.0e38
K_ITERS, ALPHA, BETA = 10, 0.1, 0.9
THETA = BETA ** K_ITERS + ALPHA * sum(BETA ** i for i in range(K_ITERS))
EPS = 1e-5
T1W = 98


def sweep(eng, count, unroll, body, peel=1, tail=1):
    rounds = (count - tail) // unroll
    for c in range(peel * unroll):
        body(c // unroll, c % unroll)
    with eng.Fori(peel, rounds) as r:
        for u in range(unroll):
            body(r, u)
    for c in range(rounds * unroll, count):
        body(c // unroll, c % unroll)


class Phase:

    def __init__(self, nc, name):
        self.nc, self.name, self.ctx, self.sems = nc, name, ExitStack(), []

    def __enter__(self):
        return self

    def sb(self, name, shape, dt=F32):
        return self.ctx.enter_context(self.nc.sbuf_tensor(f"{self.name}_{name}", shape, dt))

    def ps(self, name, shape, dt=F32):
        return self.ctx.enter_context(self.nc.psum_tensor(f"{self.name}_{name}", shape, dt))

    def sem(self, name):
        s = self.ctx.enter_context(self.nc.semaphore(f"{self.name}_{name}"))
        self.sems.append(s)
        return s

    def __exit__(self, *exc):
        if exc[0] is None:
            self.nc.gpsimd.dma_reset()
            for s in self.sems:
                self.nc.gpsimd.sem_clear(s)
            self.nc.all_engine_barrier()
        self.ctx.close()


def held(eng, tick):
    eng.sem_inc(tick, 1)


def build(nc, a, out):
    dram = {}

    def scratch(name, shape, dt=F32):
        dram[name] = nc.dram_tensor(f"scr_{name}", shape, dt, kind="Internal").ap()
        return dram[name]

    srcp, dstp, dlast = scratch("srcp", (EP,), I32), scratch("dstp", (EP,), I32), scratch("dlast", (EP,), I32)
    slast = scratch("slast", (EP,), I32)
    dflag, sflag = scratch("dflag", (EP,), BF16), scratch("sflag", (EP,), BF16)
    sorted1, sorted2 = scratch("sorted1", (EP, 2), I32), scratch("sorted2", (EP, 2), I32)
    odeg, ideg, olast = scratch("odeg", (NT,)), scratch("ideg", (NT,)), scratch("olast", (NT,))
    aggd, aggs = scratch("aggd", (N, D)), scratch("aggs", (N, D))
    c1, x1, x2, x3, fn = (scratch(k, (N, D)) for k in ("c1", "x1", "x2", "x3", "fn"))
    t1 = scratch("t1", (N, T1W))
    sums = [scratch("sums0", (EP, D)), scratch("sums1", (EP, D))]

    keep = ExitStack()

    def sb(name, shape, dt=F32):
        return keep.enter_context(nc.sbuf_tensor(name, shape, dt))

    with keep:
        ident = sb("ident", [P, P])
        identb = sb("identb", [P, P], BF16)
        ident256 = sb("ident256", [P, P], BF16)
        tri = sb("tri", [P, P])
        trib = sb("trib", [P, P], BF16)
        ones = sb("ones", [P, P])
        onesb = sb("onesb", [P, P], BF16)
        iota = sb("iota", [P, NB], BF16)
        window = sb("window", [P, 2 * HALF - 1], BF16)
        srccol, dstcol = sb("srccol", [P, TILES], I32), sb("dstcol", [P, TILES], I32)
        srcg = sb("srcg", [P, TILES], I32)
        dlcol, slcol = sb("dlcol", [P, TILES], I32), sb("slcol", [P, TILES], I32)
        lastcol = sb("lastcol", [P, TILES], I32)
        flags = sb("flags", [D, EP], BF16)
        w_conv = [sb(f"w_conv{i}", [P, D]) for i in range(2)]
        w_root = [sb(f"w_root{i}", [D + 1, D]) for i in range(2)]
        w_gcn = sb("w_gcn", [D, D])
        w_h = sb("w_h", [P, D])
        w_2 = sb("w_2", [D + 1, D])
        w_s = sb("w_s", [D + 1, D])
        w_n = sb("w_n", [D, D])
        bias_gcn = sb("bias_gcn", [P, D])
        eps = sb("eps", [P, 1])
        zero = sb("zero", [P, J * D])
        s_z = keep.enter_context(nc.semaphore("sums_zeroed"))
        rs_id, rs_od, rs_ida, rs_odb, fac, last_n = (
            sb(k, [P, BLOCKS + 1, J]) for k in ("rs_id", "rs_od", "rs_ida", "rs_odb", "fac", "last_n"))

        with Phase(nc, "setup") as ph:
            i32a = ph.sb("i32a", [P, NB], I32)
            wt = ph.sb("wt", [D, 5, D])
            brow = ph.sb("brow", [1, 3, D])
            sF, dF, prv, nxt = (ph.sb(k, [P, TILES], I32) for k in ("sF", "dF", "prv", "nxt"))
            fl = ph.sb("fl", [P, TILES])
            lf = ph.sb("lf", [P, TILES])
            flb, li = ph.sb("flb", [P, TILES], BF16), ph.sb("li", [P, TILES], I32)
            pT = ph.ps("pT", [P, 4, P])
            s_c, s_v, s_ld, s_e, s_t, s_cp, s_st, s_b = (ph.sem(k) for k in (
                "iota", "dve", "weights_in", "edges_in", "turned", "copied", "stored", "bias_sum"))
            full, tail = (P - 1) * TILES, E - (P - 1) * TILES
            with nc.Block() as block:
                @block.gpsimd
                def _(pool):
                    nc.gpsimd.iota(i32a[:, :], pattern=[[1, NB]], base=0, channel_multiplier=0).then_inc(s_c, 1)
                    nc.gpsimd.memset(ones[:, :], 1.0).then_inc(s_c, 1)
                    pool.wait_ge(s_c, 2)
                    nc.gpsimd.affine_select(out=ident[:, :], in_=ones[:, :], compare_op=ALU.is_equal, fill=0.0,
                                            base=0, pattern=[[-1, P]], channel_multiplier=1).then_inc(s_c, 1)
                    nc.gpsimd.affine_select(out=tri[:, :], in_=ones[:, :], compare_op=ALU.is_gt, fill=0.0,
                                            base=0, pattern=[[1, P]], channel_multiplier=-1).then_inc(s_c, 1)

                @block.vector
                def _(dve):
                    nc.vector.memset(zero[:, :], 0.0)
                    nc.vector.memset(eps[:, :], EPS)
                    nc.vector.memset(w_h[:, :], 0.0)
                    nc.vector.memset(window[:, :], 0.0)
                    for x_ in (sF, dF):
                        nc.vector.memset(x_[:, :], PADKEY)
                    nc.vector.memset(nxt[:, :], PADKEY)
                    nc.vector.memset(prv[:, :], -1).then_inc(s_v, 1)
                    dve.wait_ge(s_v, 1)
                    nc.vector.memset(window[:, HALF - 1:HALF], 1.0)
                    dve.wait_ge(s_c, 4)
                    nc.vector.tensor_copy(iota[:, :], i32a[:, :])
                    nc.vector.tensor_copy(identb[:, :], ident[:, :])
                    nc.vector.tensor_copy(trib[:, :], tri[:, :])
                    nc.vector.tensor_copy(onesb[:, :], ones[:, :])
                    nc.vector.tensor_scalar(ident256[:, :], ident[:, :], float(NB), None, ALU.mult)
                    dve.wait_ge(s_e, 16 * 10)
                    nc.vector.tensor_tensor(fl[:, :], dF[:, :], prv[:, :], ALU.not_equal)
                    nc.vector.tensor_tensor(lf[:, :], dF[:, :], nxt[:, :], ALU.is_equal).then_inc(s_v, 1)
                    dve.wait_ge(s_v, 2)
                    nc.vector.tensor_scalar(flb[:, :], fl[:, :], NEG, None, ALU.mult)
                    nc.vector.scalar_tensor_tensor(lf[:, :], lf[:, :], 2.0 * PADKEY, dF[:, :], ALU.mult, ALU.add).then_inc(s_v, 1)
                    dve.wait_ge(s_v, 3)
                    nc.vector.tensor_scalar(li[:, :], lf[:, :], SKIP, None, ALU.min).then_inc(s_v, 1)
                    dve.wait_ge(s_t, 1)
                    nc.vector.tensor_copy(w_2[0:D, :], pT[0:D, 0, 0:D])
                    nc.vector.tensor_copy(w_s[0:D, :], pT[0:D, 1, 0:D])
                    nc.vector.tensor_copy(w_n[:, :], pT[0:D, 2, 0:D])
                    dve.wait_ge(s_ld, 16 * 17)
                    nc.vector.tensor_tensor(brow[:, 2, :], brow[:, 0, :], brow[:, 1, :], ALU.add).then_inc(s_v, 1)

                @block.tensor
                def _(pe):
                    pe.wait_ge(s_ld, 16 * 17)
                    pe.wait_ge(s_c, 4)
                    for n in range(3):
                        last = nc.tensor.transpose(pT[0:D, n, 0:D], wt[:, n, :], ident[0:D, 0:D])
                    last.then_inc(s_t, 1)

                @block.sync
                def _(sp):
                    sp.wait_ge(s_v, 1)
                    for flat, t in ((a["src"], sF), (a["dst"], dF)):
                        sp.dma_start(t[0:P - 1, :], flat[0:full].rearrange("(p j) -> p j", j=TILES)).then_inc(s_e, 16)
                        sp.dma_start(t[P - 1:P, 0:tail], flat[full:E].rearrange("(p j) -> p j", p=1)).then_inc(s_e, 16)
                    d = a["dst"]
                    sp.dma_start(prv[0:1, 1:TILES], d[0:TILES - 1].rearrange("(p j) -> p j", p=1)).then_inc(s_e, 16)
                    sp.dma_start(prv[1:P - 1, :], d[TILES - 1:full - 1].rearrange("(p j) -> p j", j=TILES)).then_inc(s_e, 16)
                    sp.dma_start(prv[P - 1:P, 0:tail + 1], d[full - 1:E].rearrange("(p j) -> p j", p=1)).then_inc(s_e, 16)
                    sp.dma_start(nxt[0:P - 1, :], d[1:full + 1].rearrange("(p j) -> p j", j=TILES)).then_inc(s_e, 16)
                    sp.dma_start(nxt[P - 1:P, 0:tail - 1], d[full + 1:E].rearrange("(p j) -> p j", p=1)).then_inc(s_e, 16)
                    sp.dma_start(bias_gcn[:, :], a["L2_gnn_bias"].rearrange("(p d) -> p d", p=1).broadcast_to([P, D])
                                 ).then_inc(s_e, 16)
                    sp.wait_ge(s_e, 16 * 10)
                    for flat, t in ((srcp, sF), (dstp, dF)):
                        sp.dma_start(flat.rearrange("(p j) -> p j", p=P), t[:, :]).then_inc(s_st, 16)
                    sp.wait_ge(s_v, 4)
                    sp.dma_start(dflag.rearrange("(p j) -> p j", p=P), flb[:, :]).then_inc(s_st, 16)
                    sp.dma_start(dlast.rearrange("(p j) -> p j", p=P), li[:, :]).then_inc(s_st, 16)
                    sp.wait_ge(s_v, 5)
                    sp.dma_start(w_s[D:D + 1, :], brow[:, 2, :]).then_inc(s_st, 16)
                    sp.wait_ge(s_st, 16 * 5)
                    sp.dma_start(flags[:, :], dflag.rearrange("(p e) -> p e", p=1).broadcast_to([D, EP])).then_inc(s_b, 16)
                    sp.wait_ge(s_b, 16)

                @block.scalar
                def _(act):
                    act.wait_ge(s_v, 1)
                    row = lambda v: v.rearrange("(p d) -> p d", p=1)
                    for i in range(2):
                        act.dma_start(w_conv[i][0:D, :], a[f"L0_gnn_W{i + 1}_msg"]).then_inc(s_ld, 16)
                        act.dma_start(w_conv[i][D:P, :], a[f"L0_gnn_W{i + 1}_edge"]).then_inc(s_ld, 16)
                        act.dma_start(w_root[i][0:D, :], a[f"L0_gnn_W{i + 1}_root"]).then_inc(s_ld, 16)
                        act.dma_start(w_root[i][D:D + 1, :], row(a[f"L0_gnn_b{i + 1}"])).then_inc(s_ld, 16)
                    act.dma_start(w_gcn[:, :], a["L2_gnn_weight"]).then_inc(s_ld, 16)
                    act.dma_start(wt[:, 0, :], a["L3_gnn_W2"]).then_inc(s_ld, 16)
                    act.dma_start(wt[:, 1, :], a["L3_gnn_Ws"]).then_inc(s_ld, 16)
                    act.dma_start(wt[:, 2, :], a["L3_gnn_Wn"]).then_inc(s_ld, 16)
                    act.dma_start(w_2[D:D + 1, :], row(a["L3_gnn_b2"])).then_inc(s_ld, 16)
                    act.dma_start(brow[:, 0, :], row(a["L3_gnn_bs"])).then_inc(s_ld, 16)
                    act.dma_start(brow[:, 1, :], row(a["L3_gnn_bn"])).then_inc(s_ld, 16)
                    act.dma_start(w_h[D:D + DE17, :], a["L3_gnn_W1"].rearrange("o k -> k o"), allow_slow_non_contiguous=True).then_inc(s_ld, 16)
                    act.dma_start(w_h[D + DE17:D + DE17 + 1, :], row(a["L3_gnn_b1"])).then_inc(s_ld, 16)
                    act.wait_ge(s_ld, 16 * 17)
        def columns(name, src, words, outs, convert=None):
            with Phase(nc, name) as ph:
                raw, rawf = ph.sb("raw", [HALF, 2, P * words], I32), ph.sb("rawf", [HALF, 2, P * words])
                pt = ph.ps("pt", [P, 2 * words, P])
                s_in, s_f, s_t, s_o = (ph.sem(k) for k in ("rows_in", "as_float", "turned", "cols"))
                with nc.Block() as block:
                    @block.sync
                    def _(sp):
                        for h in range(2):
                            sp.dma_start(raw[:, h, :], src.rearrange("(h q n) -> h q n", h=2, q=HALF)[h]).then_inc(s_in, 16)

                    @block.vector
                    def _(dve):
                        dve.wait_ge(s_in, 32)
                        nc.vector.tensor_copy(rawf[:, :, :], raw[:, :, :]).then_inc(s_f, 1)
                        dve.wait_ge(s_t, 1)
                        for h in range(2):
                            for w in range(words):
                                nc.vector.tensor_copy(outs[w][:, h * HALF:(h + 1) * HALF], pt[:, h * words + w, 0:HALF])

                    @block.tensor
                    def _(pe):
                        pe.wait_ge(s_f, 1)
                        for h in range(2):
                            v = rawf[:, h, :].rearrange("q (n w) -> q w n", w=words)
                            for w in range(words):
                                last = nc.tensor.transpose(pt[:, h * words + w, 0:HALF], v[:, w, :], ident[0:HALF, 0:HALF])
                        last.then_inc(s_t, 1)

        columns("colsrc", srcp, 1, [srccol])
        columns("coldst", dstp, 1, [dstcol])
        columns("collast", dlast, 1, [dlcol])

        def edge_phase(name, mode, gidx=None, table=None, attr=None, de=0, sidx=None, target=None,
                       weight=None, hh=None, faccol=None, wr=None, zeroed=None):
            turn_w = P if mode in ("conv", "edge") else D
            scatter = sidx is not None
            with Phase(nc, name) as ph:
                g = [ph.sb(f"g{u}", [P, CH, P]) for u in range(GR)]
                f = [ph.sb(f"f{u}", [P, CH, D]) for u in range(2)] if mode == "prop" else None
                ts = [ph.sb(f"ts{u}", [P, CW]) for u in range(2)]
                sc = [ph.sb(f"sc{u}", [D, CW]) for u in range(2)]
                rows = [ph.sb(f"rows{u}", [P, CH, D]) for u in range(2)]
                gslot = [ph.sb(f"gslot{u}", [P, CH], I32) for u in range(GR)]
                sslot = [ph.sb(f"sslot{u}", [P, CH], I32) for u in range(2)]
                pt = [ph.ps(f"pt{u}", [P, CW]) for u in range(2)]
                pr = [ph.ps(f"pr{u}", [P, CW]) for u in range(2)]
                pm = [ph.ps(f"pm{u}", [P, CW]) for u in range(2)]
                if mode == "edge":
                    ph_ = ph.ps("phid", [P, CW])
                    pw_ = ph.ps("pw", [P, CW])
                    hs = ph.sb("hs", [D + 1, CW])
                    msg = ph.sb("msg", [D, CW])
                s_g = [ph.sem(f"gathered{u}") for u in range(GR)]
                s_at = [ph.sem(f"attr_in{u}") for u in range(GR)]
                s_out = [ph.sem(f"out{u}") for u in range(2)]
                s_ready, s_slot, s_f, s_turn, s_te, s_mm, s_scan, s_back, s_rows, s_tick, s_hid, s_relu, s_w, s_msg, s_one = (
                    ph.sem(k) for k in ("buffers_ready", "slots", "formed", "turned", "turned_copied", "product",
                                        "scanned", "back", "rows", "tick", "hidden", "relu", "edge_weight", "message", "ones_row"))
                gw = T1W if mode == "init" else D

                with nc.Block() as block:
                    @block.gpsimd
                    def _(pool):
                        def put(c, u):
                            pool.wait_ge(s_rows, c + 1)
                            held(pool, s_tick)
                            for j in range(CH):
                                nc.gpsimd.indirect_dma_start(
                                    target[:, :], bass.IndirectOffsetOnAxis(ap=sslot[u][:, j:j + 1], axis=0),
                                    rows[u][:, j, :], None, bounds_check=N - 1, oob_is_err=False).then_inc(s_out[u], 16)

                        def step(r, u):
                            c = GR * r + u
                            pool.wait_ge(s_slot, c + 1)
                            if not (isinstance(r, int) and r == 0):
                                pool.wait_ge(s_f if mode in ("prop", "init") else s_turn, c + 1 - GR)
                                if mode == "init":
                                    pool.wait_ge(s_turn, c + 1 - GR)
                            held(pool, s_tick)
                            for j in range(CH):
                                nc.gpsimd.indirect_dma_start(
                                    g[u][:, j, 0:gw], None, table[:, :],
                                    bass.IndirectOffsetOnAxis(ap=gslot[u][:, j:j + 1], axis=0)).then_inc(s_g[u], 16)
                            if scatter and not (isinstance(c, int) and c < 2):
                                put(c - 2, u % 2)

                        if zeroed is not None:
                            pool.wait_ge(*zeroed)
                        if mode in ("conv", "edge"):
                            for u in range(GR):
                                nc.gpsimd.memset(g[u][:, :, :], 1.0).then_inc(s_ready, 1)
                            pool.wait_ge(s_ready, GR)
                        sweep(pool, CHUNKS, GR, step)
                        if scatter:
                            put(CHUNKS - 2, (CHUNKS - 2) % 2)
                            put(CHUNKS - 1, (CHUNKS - 1) % 2)
                            pool.wait_ge(s_out[0], 64 * ((CHUNKS + 1) // 2))
                            pool.wait_ge(s_out[1], 64 * (CHUNKS // 2))
                        for u in range(GR):
                            pool.wait_ge(s_g[u], 64 * -(-(CHUNKS - u) // GR))

                    @block.sync
                    def _(sp):
                        if attr is not None:
                            def load(r, u):
                                c = GR * r + u
                                if isinstance(r, int) and r == 0:
                                    sp.wait_ge(s_ready, GR)
                                else:
                                    sp.wait_ge(s_turn, c + 1 - GR)
                                if isinstance(c, int) and c == CHUNKS - 1:
                                    left = E - c * CW
                                    nt = left // P
                                    sp.dma_start(g[u][:, 0:nt, D:D + de],
                                                 attr[c * CW:c * CW + nt * P, :].rearrange("(j p) d -> p j d", p=P)
                                                 ).then_inc(s_at[u], 16)
                                    sp.dma_start(g[u][0:left - nt * P, nt, D:D + de], attr[c * CW + nt * P:E, :]
                                                 ).then_inc(s_at[u], 16)
                                else:
                                    sp.dma_start(g[u][:, :, D:D + de],
                                                 attr[bass.ds(c * CW, CW), :].rearrange("(j p) d -> p j d", p=P)
                                                 ).then_inc(s_at[u], 16)
                            sweep(sp, CHUNKS, GR, load)
                        if wr is not None:
                            def store(r, u):
                                c = 2 * r + u
                                sp.wait_ge(s_rows, c + 1)
                                sp.dma_start(wr[bass.ds(c * CW, CW), :].rearrange("(j p) d -> p j d", p=P),
                                             rows[u][:, :, :]).then_inc(s_out[u], 16)
                            sweep(sp, CHUNKS, 2, store)
                            sp.wait_ge(s_out[0], 16 * ((CHUNKS + 1) // 2))
                            sp.wait_ge(s_out[1], 16 * (CHUNKS // 2))

                    @block.scalar
                    def _(act):
                        def slot(r, u):
                            c = GR * r + u
                            if not (isinstance(r, int) and r == 0):
                                act.wait_ge(s_g[u], 64 * r)
                            nc.scalar.copy(gslot[u][:, :], gidx[:, bass.ds(c * CH, CH)]).then_inc(s_slot, 1)

                        def evict(r, u):
                            c = 2 * r + u
                            if not (isinstance(r, int) and r == 0):
                                act.wait_ge(s_out[u], (64 if scatter else 16) * r)
                            act.wait_ge(s_back, c + 1)
                            if scatter:
                                nc.scalar.copy(sslot[u][:, :], sidx[:, bass.ds(c * CH, CH)])
                            nc.scalar.copy(rows[u][:, :, :], pr[u][:, 0:CH * D].rearrange("p (j d) -> p j d", d=D)
                                           ).then_inc(s_rows, 1)

                        def step(r, u):
                            c = GR * r + u
                            static = isinstance(c, int)
                            v, first = u % 2, static and c < 2
                            if not (static and c >= CHUNKS - 2):
                                slot(r + (u + 2) // GR, (u + 2) % GR)
                            if mode == "init":
                                act.wait_ge(s_g[u], 64 * (r + 1))
                                nc.scalar.copy(hh[:, bass.ds(c * CH, CH), :], g[u][:, :, 0:D])
                                nc.scalar.copy(faccol[:, bass.ds(c * CH, CH)], g[u][:, :, D])
                                nc.scalar.copy(lastcol[:, bass.ds(c * CH, CH)], g[u][:, :, D + 1]).then_inc(s_f, 1)
                            if mode != "prop":
                                act.wait_ge(s_turn, c + 1)
                                if not first:
                                    act.wait_ge({"conv": s_mm, "edge": s_msg}.get(mode, s_scan), c - 1)
                                if mode == "init":
                                    nc.scalar.mul(ts[v][0:D, :], pt[v][0:D, :], 1.0 / ALPHA).then_inc(s_te, 1)
                                else:
                                    nc.scalar.copy(ts[v][0:turn_w, :], pt[v][0:turn_w, :]).then_inc(s_te, 1)
                            if mode == "edge":
                                act.wait_ge(s_hid, c + 1)
                                if not (static and c == 0):
                                    act.wait_ge(s_w, c)
                                nc.scalar.activation(hs[0:D, :], ph_[0:D, :], ACT.Relu).then_inc(s_relu, 1)
                            if not (static and c == 0):
                                evict(2 * r + (u - 1) // 2, 1 - v)

                        slot(0, 0)
                        slot(0, 1)
                        sweep(act, CHUNKS, GR, step, tail=2)
                        evict((CHUNKS - 1) // 2, (CHUNKS - 1) % 2)

                    @block.tensor
                    def _(pe):
                        def back(r, u):
                            c = 2 * r + u
                            pe.wait_ge(s_scan, c + 1)
                            if not (isinstance(r, int) and r == 0):
                                pe.wait_ge(s_rows, c - 1)
                            for j in range(CH):
                                last = nc.tensor.matmul(pr[u][:, j * D:(j + 1) * D], sc[u][:, j * P:(j + 1) * P],
                                                        weight if weight is not None else ident[0:D, 0:D],
                                                        start=True, stop=True)
                            last.then_inc(s_back, 1)

                        def step(r, u):
                            c = GR * r + u
                            static = isinstance(c, int)
                            v, first = u % 2, static and c < 2
                            if mode == "prop":
                                pe.wait_ge(s_f, c + 1)
                                if not first:
                                    pe.wait_ge(s_scan, c - 1)
                            else:
                                pe.wait_ge(s_g[u], 64 * (r + 1))
                                if attr is not None:
                                    n_last = 32 if static and c == CHUNKS - 1 else 16
                                    pe.wait_ge(s_at[u], 16 * r + n_last)
                                if not first:
                                    pe.wait_ge(s_te, c - 1)
                            for j in range(CH):
                                last = nc.tensor.transpose(pt[v][0:turn_w, j * P:(j + 1) * P],
                                                           (f[v] if f else g[u])[:, j, 0:turn_w], ident[:, :])
                            last.then_inc(s_turn, 1)
                            if mode == "conv":
                                pe.wait_ge(s_te, c + 1)
                                if not first:
                                    pe.wait_ge(s_scan, c - 1)
                                nc.tensor.matmul(pm[v][0:D, :], w_conv_used, ts[v][:, :], start=True, stop=True
                                                 ).then_inc(s_mm, 1)
                            if mode == "edge":
                                pe.wait_ge(s_te, c + 1)
                                if not (static and c == 0):
                                    pe.wait_ge(s_relu, c)
                                nc.tensor.matmul(ph_[0:D, :], w_h[:, :], ts[v][:, :], start=True, stop=True
                                                 ).then_inc(s_hid, 1)
                                pe.wait_ge(s_relu, c + 1)
                                if static and c == 0:
                                    pe.wait_ge(s_one, 1)
                                else:
                                    pe.wait_ge(s_msg, c)
                                nc.tensor.matmul(pw_[0:D, :], w_2[:, :], hs[:, :], start=True, stop=True
                                                 ).then_inc(s_w, 1)
                            if not (static and c == 0):
                                back(2 * r + (u - 1) // 2, 1 - v)

                        sweep(pe, CHUNKS, GR, step)
                        back((CHUNKS - 1) // 2, (CHUNKS - 1) % 2)

                    @block.vector
                    def _(dve):
                        if mode == "edge":
                            nc.vector.memset(hs[D:D + 1, :], 1.0).then_inc(s_one, 1)

                        def form(r, u):
                            c = GR * r + u
                            dve.wait_ge(s_g[u], 64 * (r + 1))
                            if not (isinstance(c, int) and c < 2):
                                dve.wait_ge(s_turn, c - 1)
                            for j in range(CH):
                                last = nc.vector.scalar_tensor_tensor(
                                    f[u % 2][:, j, :], g[u][:, j, 0:D], faccol[:, bass.ds(c * CH + j, 1)],
                                    hh[:, bass.ds(c * CH + j, 1), :].rearrange("p o d -> p (o d)"), ALU.mult, ALU.add)
                            last.then_inc(s_f, 1)

                        def step(r, u):
                            c = GR * r + u
                            static = isinstance(c, int)
                            v, first = u % 2, static and c < 2
                            if mode == "edge":
                                dve.wait_ge(s_w, c + 1)
                                if not (static and c == 0):
                                    dve.wait_ge(s_scan, c)
                                nc.vector.tensor_tensor(msg[:, :], pw_[0:D, :], ts[v][0:D, :], ALU.mult
                                                        ).then_inc(s_msg, 1)
                                dve.wait_ge(s_msg, c + 1)
                                data = msg[:, :]
                            elif mode == "conv":
                                dve.wait_ge(s_mm, c + 1)
                                data = pm[v][0:D, :]
                            elif mode == "prop":
                                if static and c == 0:
                                    form(0, 0)
                                if not (static and c == CHUNKS - 1):
                                    form(r + (u + 1) // GR, (u + 1) % GR)
                                dve.wait_ge(s_turn, c + 1)
                                data = pt[v][0:D, :]
                            else:
                                dve.wait_ge(s_te, c + 1)
                                data = ts[v][0:D, :]
                            if not first:
                                dve.wait_ge(s_back, c - 1)
                            if not (static and c == 0):
                                dve.wait_ge(s_scan, c)
                            nc.vector.tensor_tensor_scan(
                                sc[v][:, :], flags[:, bass.ds(c * CW, CW)], data,
                                (0.0 if mode != "conv" else NEG) if static and c == 0 else sc[1 - v][:, CW - 1:CW],
                                ALU.add if mode == "conv" else ALU.mult,
                                ALU.max if mode == "conv" else ALU.add).then_inc(s_scan, 1)

                        sweep(dve, CHUNKS, GR, step)

        with Phase(nc, "clamp") as ph:
            with nc.Block() as block:
                @block.vector
                def _(dve):
                    nc.vector.tensor_scalar(srcg[:, :], srccol[:, :], float(N - 1), None, ALU.min)

        def dense_phase(name, mode):
            R = 4
            with Phase(nc, name) as ph:
                kinds = {"conv1": ["x", "aggd"], "conv2": ["c1", "aggd", "x"], "prop": ["x1", "aggs"],
                         "gcn": ["x2", "aggd"], "edge": ["x3", "aggd"]}[mode]
                product = mode in ("conv1", "conv2", "edge")
                norm = mode != "conv1"
                wgt = {"conv1": w_root[0], "conv2": w_root[1], "edge": w_s}.get(mode)
                tabs = dict(dram, x=a["x"])
                bufs = [[ph.sb(f"in_{k}{u}", [P, J, D]) for k in kinds] for u in range(R)]
                z = [ph.sb(f"z{u}", [P, J, D]) for u in range(R)]
                res = [ph.sb(f"res{u}", [P, J, D]) for u in range(R)]
                extra_w = {"conv2": T1W, "prop": D}.get(mode)
                ext = [ph.sb(f"ext{u}", [P, J, extra_w]) for u in range(R)] if extra_w else None
                bst = [ph.sb(f"bst{u}", [P, J, 6]) for u in range(R)]
                st = [ph.sb(f"st{u}", [P, 8, J]) for u in range(R)]
                if product:
                    xt = [ph.sb(f"xt{u}", [D + 1, J, P]) for u in range(2)]
                    pt = [ph.ps(f"pt{i}", [P, 4, P]) for i in range(3)]
                    py = [[ph.ps(f"py{u}{i}", [P, 512]) for i in range(2)] for u in range(2)]
                s_in = [ph.sem(f"in{u}") for u in range(R)]
                s_st = [ph.sem(f"stored{u}") for u in range(R)]
                s_turn, s_xt, s_y, s_add, s_pre, s_prel, s_var, s_std, s_nmr, s_fin, s_ext, s_one = (
                    ph.sem(k) for k in ("turned", "xt", "product", "added", "scaled", "scaled_half",
                                        "variance", "std", "shift", "result", "second", "ones"))
                s_chain, s_chain2, s_inv = (ph.sem(k) for k in ("norm_chain", "relu_chain", "inverse"))
                n_in, n_out = len(kinds), 1 + (ext is not None)
                out_t = {"conv1": c1, "conv2": x1, "prop": x2, "gcn": x3, "edge": out}[mode]
                ext_t = {"conv2": t1, "prop": fn}.get(mode)
                lag_n = 1
                s_free = s_var if norm else s_fin
                total = BLOCKS + 1

                def shape(c):
                    return (REST, 1) if isinstance(c, int) and c == BLOCKS else (P, J)

                def view(t, c):
                    p, j = shape(c)
                    return t[bass.ds(c * BN, p * j), :].rearrange("(p j) d -> p j d", j=j)

                def at(eng, sem, c, back=0):
                    if isinstance(c, int) and c + 1 - back <= 0:
                        return
                    eng.wait_ge(sem, c + 1 - back)

                def landed(eng, sem, n, c, u, r4):
                    eng.wait_ge(sem[u], 16 * n * (r4 + 1))

                def stages(eng, *listed):
                    def run(r, u):
                        for lag, stage in listed:
                            c = R * r + (u - lag)
                            if isinstance(c, int) and not 0 <= c < total:
                                continue
                            stage(c, (u - lag) % R, r + (u - lag) // R)
                    deepest = max(lag for lag, _ in listed)
                    rounds = BLOCKS // R
                    for s in range(2 * R):
                        run(s // R, s % R)
                    with eng.Fori(2, rounds) as r:
                        for u in range(R):
                            run(r, u)
                    for s in range(rounds * R, total + deepest):
                        run(s // R, s % R)

                with nc.Block() as block:
                    @block.sync
                    def _(sp):
                        def load(c, u, r4):
                            p, j = shape(c)
                            at(sp, s_free, c, R)
                            for k, b in zip(kinds, bufs[u]):
                                sp.dma_start(b[0:p, 0:j, :], view(tabs[k], c)).then_inc(s_in[u], 16)

                        def store(c, u, r4):
                            p, j = shape(c)
                            at(sp, s_fin, c)
                            sp.dma_start(view(out_t, c), res[u][0:p, 0:j, :]).then_inc(s_st[u], 16)
                            if ext is not None:
                                at(sp, s_ext, c)
                                sp.dma_start(view(ext_t, c), ext[u][0:p, 0:j, :]).then_inc(s_st[u], 16)
                        stages(sp, (0, load), (lag_n + 4 if norm else 2, store))
                        for u in range(R):
                            sp.wait_ge(s_st[u], 16 * n_out * (total // R))

                    @block.gpsimd
                    def _(pool):
                        wide = lambda t, c, p, j: t[0:p, bass.ds(c, 1), 0:j].rearrange("p c j -> p (c j)").rearrange(
                            "p (j o) -> p j o", o=1).broadcast_to([p, j, D])

                        def scale_in(c, u, r4):
                            p, j = shape(c)
                            v = bufs[u][1][0:p, 0:j, :]
                            landed(pool, s_in, n_in, c, u, r4)
                            t = rs_odb if mode == "prop" else rs_id
                            if mode == "prop":
                                nc.gpsimd.tensor_tensor(v, v, wide(t, c, p, j), ALU.mult).then_inc(s_pre, 1)
                            else:
                                nc.gpsimd.tensor_tensor(v, v, wide(t, c, p, j), ALU.mult).then_inc(s_prel, 1)
                                at(pool, s_prel, c)
                                nc.gpsimd.tensor_tensor(
                                    v, v, bias_gcn[0:p, :].rearrange("p (o d) -> p o d", o=1).broadcast_to([p, j, D]),
                                    ALU.add).then_inc(s_pre, 1)

                        def second(c, u, r4):
                            p, j = shape(c)
                            at(pool, s_fin, c)
                            if not (isinstance(c, int) and c < R):
                                pool.wait_ge(s_st[u], 16 * n_out * r4)
                            if mode == "conv2":
                                for n, t in ((D, fac), (D + 1, last_n)):
                                    nc.gpsimd.tensor_copy(
                                        ext[u][0:p, 0:j, n], t[0:p, bass.ds(c, 1), 0:j].rearrange("p c j -> p (c j)"))
                            nc.gpsimd.tensor_tensor(ext[u][0:p, 0:j, 0:D], res[u][0:p, 0:j, :],
                                                    wide(rs_ida if mode == "conv2" else rs_od, c, p, j), ALU.mult
                                                    ).then_inc(s_ext, 1)
                        todo = []
                        if mode in ("prop", "gcn"):
                            todo.append((0, scale_in))
                        if ext is not None:
                            todo.append((lag_n + 3, second))
                        if todo:
                            stages(pool, *todo)

                    @block.tensor
                    def _(pe):
                        def turn(c, u, r4):
                            p, jn = shape(c)
                            landed(pe, s_in, n_in, c, u, r4)
                            at(pe, s_xt, c, 1)
                            for j in range(jn):
                                last = nc.tensor.transpose(pt[j // 4][0:D, j % 4, 0:p], bufs[u][0][0:p, j, :],
                                                           ident[0:p, 0:p])
                            last.then_inc(s_turn, 1)

                        def root(c, u, r4):
                            p, jn = shape(c)
                            at(pe, s_xt, c)
                            if isinstance(c, int) and c == 0:
                                pe.wait_ge(s_one, 1)
                            at(pe, s_add, c, 2)
                            for j in range(jn):
                                last = nc.tensor.matmul(py[u % 2][j // 5][0:p, (j % 5) * D:(j % 5 + 1) * D],
                                                        xt[u % 2][:, j, 0:p], wgt[:, :], start=True, stop=True)
                            last.then_inc(s_y, 1)
                        if product:
                            stages(pe, (0, turn), (1, root))

                    @block.scalar
                    def _(act):
                        def turned(c, u, r4):
                            p, jn = shape(c)
                            at(act, s_turn, c)
                            at(act, s_y, c, 2)
                            for i in range(-(-jn // 4)):
                                w = min(4, jn - 4 * i)
                                last = nc.scalar.copy(xt[u % 2][0:D, 4 * i:4 * i + w, 0:p], pt[i][0:D, 0:w, 0:p])
                            last.then_inc(s_xt, 1)

                        def std(c, u, r4):
                            p, jn = shape(c)
                            at(act, s_var, c)
                            nc.scalar.activation(st[u][0:p, 4, 0:jn], st[u][0:p, 3, 0:jn], ACT.Sqrt, bias=eps[0:p, :],
                                                 scale=1.0 / D).then_inc(s_std, 1)

                        def final(c, u, r4):
                            p, jn = shape(c)
                            at(act, s_nmr, c)
                            if not (isinstance(c, int) and c < R):
                                act.wait_ge(s_st[u], 16 * n_out * r4)
                            for j in range(jn):
                                last = nc.scalar.activation(res[u][0:p, j, :], z[u][0:p, j, :], ACT.Identity,
                                                            scale=st[u][0:p, 5, j:j + 1], bias=st[u][0:p, 6, j:j + 1])
                            last.then_inc(s_fin, 1)
                        todo = []
                        if product:
                            todo.append((0, turned))
                        if norm:
                            todo += [(lag_n + 1, std), (lag_n + 2, final)]
                        stages(act, *todo)

                    @block.vector
                    def _(dve):
                        if product:
                            for u in range(2):
                                last = nc.vector.memset(xt[u][D:D + 1, :, :], 1.0)
                            last.then_inc(s_one, 1)

                        def add(c, u, r4):
                            p, jn = shape(c)
                            landed(dve, s_in, n_in, c, u, r4)
                            at(dve, s_y, c)
                            if norm:
                                at(dve, s_fin, c, R)
                            for i in range(-(-jn // 5)):
                                w = min(5, jn - 5 * i)
                                last = nc.vector.tensor_tensor(
                                    z[u][0:p, 5 * i:5 * i + w, :],
                                    py[u % 2][i][0:p, 0:w * D].rearrange("p (j d) -> p j d", d=D),
                                    bufs[u][1][0:p, 5 * i:5 * i + w, :], ALU.add)
                            last.then_inc(s_add, 1)
                            v = z[u][0:p, 0:jn, :]
                            if mode == "conv1":
                                at(dve, s_add, c)
                                if not (isinstance(c, int) and c < R):
                                    dve.wait_ge(s_st[u], 16 * n_out * r4)
                                nc.vector.scalar_tensor_tensor(res[u][0:p, 0:jn, :], v, 0.01, v, ALU.mult, ALU.max
                                                               ).then_inc(s_fin, 1)

                        def stats(c, u, r4):
                            p, jn = shape(c)
                            v = z[u][0:p, 0:jn, :]
                            B = [b[0:p, 0:jn, :] for b in bufs[u]]
                            n_chain = 5 if mode == "conv2" else 4
                            done = [0]

                            def link(ins):
                                done[0] += 1
                                ins.then_inc(s_chain, 1)
                                dve.wait_ge(s_chain, c * n_chain + done[0])

                            if mode == "conv2":
                                at(dve, s_add, c)
                                link(nc.vector.scalar_tensor_tensor(v, v, 0.01, v, ALU.mult, ALU.max))
                                link(nc.vector.tensor_tensor(v, v, B[2], ALU.add))
                            elif mode == "edge":
                                at(dve, s_add, c)
                                link(nc.vector.scalar_tensor_tensor(v, v, 0.0, B[0], ALU.max, ALU.add))
                            else:
                                at(dve, s_pre, c)
                                at(dve, s_fin, c, R)
                                if mode == "prop":
                                    link(nc.vector.scalar_tensor_tensor(v, B[0], 1.0 + ALPHA / THETA, B[1], ALU.mult, ALU.add))
                                else:
                                    link(nc.vector.tensor_tensor(v, B[0], B[1], ALU.add))
                            for j in range(jn):
                                last = nc.vector.bn_stats(bst[u][0:p, j, :], z[u][0:p, j, :])
                            link(last)
                            b = bst[u][0:p, 0:jn, :]
                            s_ = lambda i: st[u][0:p, i, 0:jn]
                            nc.vector.tensor_tensor(s_(1), b[:, :, 2], b[:, :, 5], ALU.add)
                            nc.vector.tensor_tensor(s_(0), b[:, :, 1], b[:, :, 4], ALU.add)
                            link(nc.vector.tensor_tensor(s_(2), b[:, :, 1], b[:, :, 4], ALU.subtract))
                            link(nc.vector.tensor_tensor(s_(2), s_(2), s_(2), ALU.mult))
                            nc.vector.scalar_tensor_tensor(s_(3), s_(2), D / 4.0, s_(1), ALU.mult, ALU.add).then_inc(s_var, 1)

                        def shift(c, u, r4):
                            p, jn = shape(c)
                            s_ = lambda i: st[u][0:p, i, 0:jn]
                            at(dve, s_std, c)
                            nc.vector.reciprocal(s_(5), s_(4)).then_inc(s_inv, 1)
                            at(dve, s_inv, c)
                            nc.vector.scalar_tensor_tensor(s_(6), s_(0), -0.5, s_(5), ALU.mult, ALU.mult).then_inc(s_nmr, 1)
                        todo = []
                        if product:
                            todo.append((1, add))
                        if norm:
                            todo += [(lag_n, stats), (lag_n + 1, shift)]
                        stages(dve, *todo)

        def histogram(name, cols, table, last_table=None, zeroing=False):
            with Phase(nc, name) as ph:
                lo, hi = ph.sb("lo", [P, TILES]), ph.sb("hi", [P, TILES])
                loi, hii = ph.sb("loi", [P, TILES], I32), ph.sb("hii", [P, TILES], I32)
                ohl = [ph.sb(f"ohl{u}", [P, CH, NB], BF16) for u in range(2)]
                ohh = [ph.sb(f"ohh{u}", [P, CH, 2 * NH], BF16) for u in range(2)]
                hist, run = ph.sb("hist", [NH, 2, NB]), ph.sb("run", [NH, 2, NB])
                ones_row = ph.sb("ones_row", [NH, NB])
                off = ph.sb("off", [NH, 2])
                acc = [ph.ps(f"acc{h}", [P, 512]) for h in range(2)]
                po = ph.ps("po", [P, 512])
                po2 = ph.ps("po2", [P, 512])
                s_oh, s_mm, s_h, s_r, s_o, s_st, s_v = (ph.sem(k) for k in (
                    "onehots", "added", "hist", "run", "offsets", "stored", "dve"))
                with nc.Block() as block:
                    @block.vector
                    def _(dve):
                        nc.vector.memset(ones_row[:, :], 1.0)
                        nc.vector.tensor_scalar(hii[:, :], cols[:, :], 8, None, ALU.arith_shift_right)
                        nc.vector.tensor_scalar(loi[:, :], cols[:, :], NB - 1, None, ALU.bitwise_and).then_inc(s_v, 1)
                        dve.wait_ge(s_v, 1)
                        nc.vector.tensor_copy(hi[:, :], hii[:, :])
                        nc.vector.tensor_copy(lo[:, :], loi[:, :]).then_inc(s_v, 1)
                        dve.wait_ge(s_v, 2)

                        def step(r, u):
                            c = 2 * r + u
                            if not (isinstance(r, int) and r == 0):
                                dve.wait_ge(s_mm, c - 1)
                            for j in range(CH):
                                nc.vector.tensor_scalar(ohl[u][:, j, :], iota[:, :], lo[:, bass.ds(c * CH + j, 1)], None, ALU.is_equal)
                                last = nc.vector.tensor_scalar(ohh[u][:, j, :], iota[:, 0:2 * NH], hi[:, bass.ds(c * CH + j, 1)],
                                                               None, ALU.is_equal)
                            last.then_inc(s_oh, 1)
                        sweep(dve, CHUNKS, 2, step)
                        dve.wait_ge(s_mm, CHUNKS)
                        nc.vector.tensor_copy(hist[:, 0, :], acc[0][0:NH, 0:NB])
                        nc.vector.tensor_copy(hist[:, 1, :], acc[1][0:NH, 0:NB]).then_inc(s_h, 1)
                        if last_table is not None:
                            dve.wait_ge(s_h, 1)
                            for h in range(2):
                                last = nc.vector.tensor_tensor_scan(run[:, h, :], ones_row[:, :], hist[:, h, :], 0.0,
                                                                    ALU.mult, ALU.add)
                            last.then_inc(s_r, 1)
                            dve.wait_ge(s_o, 1)
                            nc.vector.tensor_copy(off[:, 0:1], po[0:NH, 0:1])
                            nc.vector.tensor_copy(off[:, 1:2], po2[0:NH, 0:1]).then_inc(s_v, 1)
                            dve.wait_ge(s_v, 3)
                            dve.wait_ge(s_r, 1)
                            for h in range(2):
                                last = nc.vector.tensor_scalar(run[:, h, :], run[:, h, :], off[:, h:h + 1], -1.0, ALU.add, ALU.add)
                            last.then_inc(s_r, 1)
                            dve.wait_ge(s_r, 2)
                            nc.vector.tensor_scalar(run[:, :, :], run[:, :, :], 0.0, None, ALU.max).then_inc(s_r, 1)

                    @block.tensor
                    def _(pe):
                        def step(r, u):
                            c = 2 * r + u
                            static = isinstance(c, int)
                            pe.wait_ge(s_oh, c + 1)
                            for j in range(CH):
                                for h in range(2):
                                    last = nc.tensor.matmul(acc[h][0:NH, 0:NB], ohh[u][:, j, h * NH:(h + 1) * NH], ohl[u][:, j, :],
                                                            start=static and c == 0 and j == 0,
                                                            stop=static and c == CHUNKS - 1 and j == CH - 1)
                            last.then_inc(s_mm, 1)
                        sweep(pe, CHUNKS, 2, step)
                        if last_table is not None:
                            pe.wait_ge(s_r, 1)
                            nc.tensor.matmul(po[0:NH, 0:1], tri[0:NH, 0:NH], run[:, 0, NB - 1:NB], start=True, stop=True)
                            nc.tensor.matmul(po2[0:NH, 0:1], tri[0:NH, 0:NH], run[:, 1, NB - 1:NB], start=True, stop=False)
                            nc.tensor.matmul(po2[0:NH, 0:1], ones[0:NH, 0:NH], run[:, 0, NB - 1:NB], start=False, stop=True
                                             ).then_inc(s_o, 1)

                    @block.sync
                    def _(sp):
                        view = lambda t: t.rearrange("(h q n) -> q h n", h=2, q=NH)
                        sp.wait_ge(s_h, 1)
                        sp.dma_start(view(table), hist[:, :, :]).then_inc(s_st, 16)
                        if last_table is not None:
                            sp.wait_ge(s_r, 3)
                            sp.dma_start(view(last_table), run[:, :, :]).then_inc(s_st, 16)
                        sp.wait_ge(s_st, 32 if last_table is not None else 16)

                    @block.scalar
                    def _(act):
                        if zeroing:
                            for t in (aggd, aggs):
                                v = t[0:BLOCKS * BN, :].rearrange("(c p j) d -> c p (j d)", p=P, j=J)
                                for c in range(BLOCKS):
                                    act.dma_start(v[c], zero[:, :]).then_inc(s_z, 16)
                                act.dma_start(t[BLOCKS * BN:N, :], zero[0:REST, 0:D]).then_inc(s_z, 16)

        def radix_pass(name, keys, vals, shift, target):
            with Phase(nc, name) as ph:
                dig, digi = ph.sb("dig", [P, TILES]), ph.sb("digi", [P, TILES], I32)
                oh = [ph.sb(f"oh{u}", [P, CH, NB], BF16) for u in range(2)]
                junk = ph.sb("junk", [P, NB])
                cnt = [ph.sb(f"cnt{h}", [HALF, NB], BF16) for h in range(2)]
                cntf = ph.sb("cntf", [HALF, NB])
                base = ph.sb("base", [HALF, NB + 1])
                tot = ph.sb("tot", [HALF, NB])
                ones_row = ph.sb("ones_row", [HALF, NB])
                rf = [ph.sb(f"rf{h}", [HALF, NB]) for h in range(2)]
                ri = [ph.sb(f"ri{h}", [HALF, NB], I32) for h in range(2)]
                rhi_i, rlo_i = ([ph.sb(f"{k}{h}", [HALF, NB], I32) for h in range(2)] for k in ("rhi_i", "rlo_i"))
                rhi, rlo = ([ph.sb(f"{k}{h}", [HALF, NB], BF16) for h in range(2)] for k in ("rhi", "rlo"))
                posf = [ph.sb(f"posf{u}", [P, CH]) for u in range(2)]
                pos = [ph.sb(f"pos{u}", [P, CH], I32) for u in range(2)]
                pay = [ph.sb(f"pay{u}", [P, CH, 2], I32) for u in range(2)]
                acc = [ph.ps(f"acc{h}", [P, 512]) for h in range(2)]
                pp = [ph.ps(f"pp{u}", [P, CH, NB]) for u in range(2)]
                s_v, s_oh, s_cnt, s_c, s_pre, s_r, s_oh2, s_pos, s_rank, s_pay, s_tick = (ph.sem(k) for k in (
                    "dve", "onehots", "counted", "counts", "prefixes", "bases", "onehots2", "positions", "ranked", "payload", "tick"))
                s_sc = [ph.sem(f"scattered{u}") for u in range(2)]
                with nc.Block() as block:
                    @block.vector
                    def _(dve):
                        at = [0]

                        def link(ins):
                            at[0] += 1
                            ins.then_inc(s_v, 1)
                            dve.wait_ge(s_v, at[0])

                        nc.vector.memset(ones_row[:, :], 1.0)
                        if shift:
                            link(nc.vector.tensor_scalar(digi[:, :], keys[:, :], shift, None, ALU.arith_shift_right))
                        else:
                            link(nc.vector.tensor_scalar(digi[:, :], keys[:, :], NB - 1, None, ALU.bitwise_and))
                        link(nc.vector.tensor_copy(dig[:, :], digi[:, :]))

                        def onehots(c, u, sem):
                            for j in range(CH):
                                last = nc.vector.tensor_scalar(oh[u][:, j, :], iota[:, :], dig[:, bass.ds(c * CH + j, 1)],
                                                               None, ALU.is_equal)
                            last.then_inc(sem, 1)

                        def count(r, u):
                            if not (isinstance(r, int) and r == 0):
                                dve.wait_ge(s_cnt, 2 * r + u - 1)
                            onehots(2 * r + u, u, s_oh)
                        sweep(dve, CHUNKS, 2, count)
                        dve.wait_ge(s_cnt, CHUNKS)
                        nc.vector.tensor_copy(cntf[:, :], acc[0][0:HALF, 0:NB])
                        nc.vector.tensor_copy(cnt[0][:, :], acc[0][0:HALF, 0:NB])
                        nc.vector.tensor_copy(cnt[1][:, :], acc[1][0:HALF, 0:NB]).then_inc(s_c, 1)
                        dve.wait_ge(s_pre, 1)
                        nc.vector.memset(base[:, 0:1], 0.0)
                        link(nc.vector.tensor_copy(tot[:, :], acc[1][0:HALF, 0:NB]))
                        link(nc.vector.tensor_tensor_scan(base[:, 1:NB + 1], ones_row[:, :], tot[:, :], 0.0, ALU.mult, ALU.add))
                        link(nc.vector.tensor_tensor(rf[0][:, :], acc[0][0:HALF, 0:NB], base[:, 0:NB], ALU.add))
                        link(nc.vector.tensor_tensor(rf[1][:, :], rf[0][:, :], cntf[:, :], ALU.add))
                        for h in range(2):
                            link(nc.vector.tensor_copy(ri[h][:, :], rf[h][:, :]))
                            nc.vector.tensor_scalar(rhi_i[h][:, :], ri[h][:, :], 8, None, ALU.arith_shift_right)
                            link(nc.vector.tensor_scalar(rlo_i[h][:, :], ri[h][:, :], NB - 1, None, ALU.bitwise_and))
                            nc.vector.tensor_copy(rhi[h][:, :], rhi_i[h][:, :])
                            last = nc.vector.tensor_copy(rlo[h][:, :], rlo_i[h][:, :])
                        last.then_inc(s_r, 1)

                        def ready(r, u):
                            if not (isinstance(r, int) and r == 0):
                                dve.wait_ge(s_rank, 2 * r + u - 1)
                            onehots(2 * r + u, u, s_oh2)

                        def rank(r, u):
                            c = 2 * r + u
                            static = isinstance(c, int)
                            if static and c == 0:
                                ready(0, 0)
                            if not (static and c == CHUNKS - 1):
                                ready(r + u, 1 - u)
                            dve.wait_ge(s_pos, c + 1)
                            if not (isinstance(r, int) and r == 0):
                                dve.wait_ge(s_sc[u], 64 * r)
                            for j in range(CH):
                                if not (static and c == 0 and j == 0):
                                    dve.wait_ge(s_v, v0 + CH * c + j)
                                nc.vector.tensor_tensor_reduce(out=junk[:, :], in0=oh[u][:, j, :], in1=pp[u][:, j, :],
                                                               scale=1.0, scalar=0.0, op0=ALU.mult, op1=ALU.add,
                                                               accum_out=posf[u][:, j:j + 1]).then_inc(s_v, 1)
                            dve.wait_ge(s_v, v0 + CH * c + CH)
                            nc.vector.tensor_copy(pos[u][:, :], posf[u][:, :]).then_inc(s_rank, 1)
                        v0 = at[0]
                        dve.wait_ge(s_cnt, CHUNKS)
                        sweep(dve, CHUNKS, 2, rank)

                    @block.tensor
                    def _(pe):
                        def count(r, u):
                            c = 2 * r + u
                            static = isinstance(c, int)
                            pe.wait_ge(s_oh, c + 1)
                            for j in range(CH):
                                last = nc.tensor.matmul(acc[j % 2][0:HALF, 0:NB],
                                                        window[:, bass.ds(HALF - 1 - (2 * c + j // 2), HALF)], oh[u][:, j, :],
                                                        start=static and c == 0 and j < 2,
                                                        stop=static and c == CHUNKS - 1 and j >= 2)
                            last.then_inc(s_cnt, 1)
                        sweep(pe, CHUNKS, 2, count)
                        pe.wait_ge(s_c, 1)
                        nc.tensor.matmul(acc[0][0:HALF, 0:NB], trib[0:HALF, 0:HALF], cnt[0][:, :], start=True, stop=False)
                        nc.tensor.matmul(acc[0][0:HALF, 0:NB], trib[0:HALF, 0:HALF], cnt[1][:, :], start=False, stop=True)
                        nc.tensor.matmul(acc[1][0:HALF, 0:NB], onesb[0:HALF, 0:HALF], cnt[0][:, :], start=True, stop=False)
                        nc.tensor.matmul(acc[1][0:HALF, 0:NB], onesb[0:HALF, 0:HALF], cnt[1][:, :], start=False, stop=True
                                         ).then_inc(s_pre, 1)
                        pe.wait_ge(s_r, 1)

                        def place(r, u):
                            c = 2 * r + u
                            pe.wait_ge(s_oh2, c + 1)
                            if not (isinstance(r, int) and r == 0):
                                pe.wait_ge(s_rank, c - 1)
                            for j in range(CH):
                                nc.tensor.matmul(pp[u][:, j, :], trib[:, :], oh[u][:, j, :], start=True, stop=False)
                                for idn, rr in ((ident256, rhi), (identb, rlo)):
                                    last = nc.tensor.matmul(
                                        pp[u][:, j, :],
                                        idn[0:HALF, bass.ds(2 * c + j // 2, 1)].broadcast_to([HALF, P]),
                                        rr[j % 2][:, :], start=False, stop=rr is rlo)
                            last.then_inc(s_pos, 1)
                        sweep(pe, CHUNKS, 2, place)

                    @block.scalar
                    def _(act):
                        def step(r, u):
                            c = 2 * r + u
                            if not (isinstance(r, int) and r == 0):
                                act.wait_ge(s_sc[u], 64 * r)
                            nc.scalar.copy(pay[u][:, :, 0], keys[:, bass.ds(c * CH, CH)])
                            nc.scalar.copy(pay[u][:, :, 1], vals[:, bass.ds(c * CH, CH)]).then_inc(s_pay, 1)
                        sweep(act, CHUNKS, 2, step)

                    @block.gpsimd
                    def _(pool):
                        def step(r, u):
                            c = 2 * r + u
                            pool.wait_ge(s_pay, c + 1)
                            pool.wait_ge(s_rank, c + 1)
                            held(pool, s_tick)
                            for j in range(CH):
                                nc.gpsimd.indirect_dma_start(
                                    target[:, :], bass.IndirectOffsetOnAxis(ap=pos[u][:, j:j + 1], axis=0),
                                    pay[u][:, j, :], None).then_inc(s_sc[u], 16)
                        sweep(pool, CHUNKS, 2, step)
                        pool.wait_ge(s_sc[0], 64 * ((CHUNKS + 1) // 2))
                        pool.wait_ge(s_sc[1], 64 * (CHUNKS // 2))

        histogram("hin", dstcol, ideg, zeroing=True)
        histogram("hout", srccol, odeg, olast)

        w_conv_used = w_conv[0][:, :]
        edge_phase("conv1", "conv", gidx=srcg, table=a["x"], attr=a["edge_attr_32"], de=DE32, sidx=dlcol, target=aggd,
                   zeroed=(s_z, 16 * 2 * (BLOCKS + 1)))
        dense_phase("node1", "conv1")
        w_conv_used = w_conv[1][:, :]
        edge_phase("conv2", "conv", gidx=srcg, table=c1, attr=a["edge_attr_32"], de=DE32, sidx=dlcol, target=aggd)

        with Phase(nc, "factors") as ph:
            od = ph.sb("od", [P, BLOCKS + 1, J])
            has = ph.sb("has", [P, BLOCKS + 1, J])
            s_in, s_m, s_v, s_a = (ph.sem(k) for k in ("tables_in", "cleared", "dve", "act"))
            with nc.Block() as block:
                @block.sync
                def _(sp):
                    sp.wait_ge(s_m, 1)
                    for t, dst in ((odeg, od), (ideg, rs_id), (olast, last_n)):
                        sp.dma_start(dst[:, 0:BLOCKS, :], t[0:BLOCKS * BN].rearrange("(c p j) -> p c j", p=P, j=J)).then_inc(s_in, 16)
                        sp.dma_start(dst[0:REST, BLOCKS, 0:1], t[BLOCKS * BN:N].rearrange("(p j) -> p j", j=1)).then_inc(s_in, 16)

                @block.vector
                def _(dve):
                    for t in (od, rs_id, last_n):
                        last = nc.vector.memset(t[:, :, :], 1.0)
                    last.then_inc(s_m, 1)
                    dve.wait_ge(s_in, 96)
                    nc.vector.tensor_scalar(has[:, :, :], od[:, :, :], 0.0, BETA, ALU.is_gt, ALU.mult)
                    nc.vector.tensor_scalar(rs_od[:, :, :], od[:, :, :], 1.0, None, ALU.max)
                    nc.vector.tensor_scalar(rs_id[:, :, :], rs_id[:, :, :], 1.0, None, ALU.max).then_inc(s_v, 1)
                    dve.wait_ge(s_a, 1)
                    nc.vector.reciprocal(rs_od[:, :, :], rs_od[:, :, :])
                    nc.vector.reciprocal(rs_id[:, :, :], rs_id[:, :, :]).then_inc(s_v, 1)
                    dve.wait_ge(s_v, 2)
                    nc.vector.tensor_scalar(rs_ida[:, :, :], rs_id[:, :, :], ALPHA, None, ALU.mult)
                    nc.vector.tensor_scalar(rs_odb[:, :, :], rs_od[:, :, :], BETA / THETA, None, ALU.mult)
                    nc.vector.tensor_tensor(fac[:, :, :], rs_od[:, :, :], rs_id[:, :, :], ALU.mult).then_inc(s_v, 1)
                    dve.wait_ge(s_v, 3)
                    nc.vector.tensor_tensor(fac[:, :, :], fac[:, :, :], has[:, :, :], ALU.mult)

                @block.scalar
                def _(act):
                    act.wait_ge(s_v, 1)
                    nc.scalar.activation(rs_od[:, :, :], rs_od[:, :, :], ACT.Sqrt)
                    nc.scalar.activation(rs_id[:, :, :], rs_id[:, :, :], ACT.Sqrt).then_inc(s_a, 1)

        dense_phase("node2", "conv2")

        radix_pass("radix1", srccol, dstcol, 0, sorted1)
        k1, v1 = sb("k1", [P, TILES], I32), sb("v1", [P, TILES], I32)
        columns("colsort1", sorted1.rearrange("e w -> (e w)"), 2, [k1, v1])
        radix_pass("radix2", k1, v1, 8, sorted2)
        columns("colsort2", sorted2.rearrange("e w -> (e w)"), 2, [k1, v1])

        def order_flags():
            with Phase(nc, "runs") as ph:
                pair = ph.sb("pair", [P, TILES, 2], I32)
                prv, nxt = ph.sb("prv", [P, TILES, 2], I32), ph.sb("nxt", [P, TILES, 2], I32)
                fl, lf = ph.sb("fl", [P, TILES]), ph.sb("lf", [P, TILES])
                flb, li = ph.sb("flb", [P, TILES], BF16), ph.sb("li", [P, TILES], I32)
                s_m, s_in, s_v, s_st, s_b = (ph.sem(k) for k in ("cleared", "in", "dve", "stored", "broadcast"))
                rows2 = sorted2.rearrange("(p j) w -> p j w", p=P)
                flat2 = sorted2
                with nc.Block() as block:
                    @block.vector
                    def _(dve):
                        nc.vector.memset(prv[:, :, :], -1)
                        nc.vector.memset(nxt[:, :, :], -1).then_inc(s_m, 1)
                        nc.vector.tensor_scalar(v1[:, :], v1[:, :], float(N - 1), None, ALU.min)
                        dve.wait_ge(s_in, 16 * 5)
                        nc.vector.tensor_tensor(fl[:, :], pair[:, :, 0], prv[:, :, 0], ALU.is_equal)
                        nc.vector.tensor_tensor(lf[:, :], pair[:, :, 0], nxt[:, :, 0], ALU.is_equal).then_inc(s_v, 1)
                        dve.wait_ge(s_v, 1)
                        nc.vector.tensor_copy(flb[:, :], fl[:, :])
                        nc.vector.scalar_tensor_tensor(lf[:, :], lf[:, :], 2.0 * PADKEY, pair[:, :, 0], ALU.mult, ALU.add).then_inc(s_v, 1)
                        dve.wait_ge(s_v, 2)
                        nc.vector.tensor_scalar(li[:, :], lf[:, :], SKIP, None, ALU.min).then_inc(s_v, 1)

                    @block.sync
                    def _(sp):
                        sp.wait_ge(s_m, 1)
                        sp.dma_start(pair[:, :, :], rows2).then_inc(s_in, 16)
                        sp.dma_start(prv[0:1, 1:TILES, :], flat2[0:TILES - 1, :].rearrange("(p j) w -> p j w", p=1)).then_inc(s_in, 16)
                        sp.dma_start(prv[1:P, :, :], flat2[TILES - 1:EP - 1, :].rearrange("(p j) w -> p j w", j=TILES)).then_inc(s_in, 16)
                        sp.dma_start(nxt[0:P - 1, :, :], flat2[1:EP - TILES + 1, :].rearrange("(p j) w -> p j w", j=TILES)).then_inc(s_in, 16)
                        sp.dma_start(nxt[P - 1:P, 0:TILES - 1, :], flat2[EP - TILES + 1:EP, :].rearrange("(p j) w -> p j w", p=1)).then_inc(s_in, 16)
                        sp.wait_ge(s_v, 3)
                        sp.dma_start(sflag.rearrange("(p j) -> p j", p=P), flb[:, :]).then_inc(s_st, 16)
                        sp.dma_start(slast.rearrange("(p j) -> p j", p=P), li[:, :]).then_inc(s_st, 16)
                        sp.wait_ge(s_st, 32)
                        sp.dma_start(flags[:, :], sflag.rearrange("(p e) -> p e", p=1).broadcast_to([D, EP])).then_inc(s_b, 16)
                        sp.wait_ge(s_b, 16)

        order_flags()
        columns("colslast", slast, 1, [slcol])

        prop = ExitStack()
        with prop:
            hh = prop.enter_context(nc.sbuf_tensor("hh", [P, TILES, D], F32))
            faccol = prop.enter_context(nc.sbuf_tensor("faccol", [P, TILES], F32))
            edge_phase("prop0", "init", gidx=v1, table=t1, hh=hh, faccol=faccol, wr=sums[0])
            with nc.Fori(0, (K_ITERS - 2) // 2):
                for n in range(2):
                    edge_phase(f"prop{1 + n}", "prop", gidx=lastcol, table=sums[n], hh=hh, faccol=faccol, wr=sums[1 - n])
            edge_phase("prop9", "prop", gidx=lastcol, table=sums[0], hh=hh, faccol=faccol, sidx=slcol, target=aggs)
        dense_phase("node3", "prop")

        with Phase(nc, "dflags") as ph:
            s_in = ph.sem("in")
            s_v = ph.sem("dve")
            with nc.Block() as block:
                @block.sync
                def _(sp):
                    sp.dma_start(flags[:, :], dflag.rearrange("(p e) -> p e", p=1).broadcast_to([D, EP])).then_inc(s_in, 16)

                @block.vector
                def _(dve):
                    dve.wait_ge(s_in, 16)
                    nc.vector.tensor_scalar(flags[:, :], flags[:, :], -1.0, None, ALU.is_ge)

        edge_phase("gcn", "gcn", gidx=srcg, table=fn, sidx=dlcol, target=aggd, weight=w_gcn[:, :])
        dense_phase("node4", "gcn")
        edge_phase("edge", "edge", gidx=srcg, table=x3, attr=a["edge_attr_17"], de=DE17, sidx=dlcol, target=aggd,
                   weight=w_n[:, :])
        dense_phase("node5", "edge")


_INS = ["x", "src", "dst", "edge_attr_17", "edge_attr_32", "L0_gnn_W1_msg", "L0_gnn_W1_edge", "L0_gnn_W1_root",
        "L0_gnn_b1", "L0_gnn_W2_msg", "L0_gnn_W2_edge", "L0_gnn_W2_root", "L0_gnn_b2", "L2_gnn_weight", "L2_gnn_bias",
        "L3_gnn_W1", "L3_gnn_b1", "L3_gnn_W2", "L3_gnn_b2", "L3_gnn_Ws", "L3_gnn_bs", "L3_gnn_Wn", "L3_gnn_bn"]


def kernel(**inputs):
    import concourse.bacc as _bacc
    from concourse.bass_utils import run_bass_kernel_spmd as _run
    nc = _bacc.Bacc("TRN2", target_bir_lowering=False, num_devices=1)
    arrays, args = {}, {}
    for name in _INS:
        v = np.ascontiguousarray(inputs[name])
        arrays[f"in_{name}"] = v
        args[name] = nc.dram_tensor(f"in_{name}", v.shape, mybir.dt.from_np(v.dtype), kind="ExternalInput").ap()
    out = nc.dram_tensor("out_0", (N, D), F32, kind="ExternalOutput").ap()
    build(nc, args, out)
    r = _run(nc, [arrays], core_ids=[0])
    return r.results[0]["out_0"]
```

```python
import numpy as np
import concourse.bass as bass
from concourse import mybir
from concourse.alu_op_type import AluOpType as ALU
from contextlib import ExitStack

F32 = mybir.dt.float32
BF16 = mybir.dt.bfloat16
I32 = mybir.dt.int32
F16 = mybir.dt.float16
U8 = mybir.dt.uint8
ACT = mybir.ActivationFunctionType

N, E, D, DE32, DE17 = 50000, 25000, 96, 32, 17
P = 128
TILES = -(-E // P)
EP = TILES * P
CH = 4
CW = CH * P
CHUNKS = TILES // CH
GR = 4
RMAX = -(-CHUNKS // GR)
RW = GR * CW
TX = RMAX * GR * CH
EX = TX * P
TC = TX + 2 * CH
INACTIVE = 65536
NB2 = 400
HALF = TILES // 2
PADKEY = 65535
SKIP = 60000.0
NB = 256
NH = HALF
NT = 2 * NH * NB
J = 10
BN = P * J
BLOCKS = N // BN
REST = N - BLOCKS * BN
NEG = -3.0e38
K_ITERS, ALPHA, BETA = 10, 0.1, 0.9
THETA = BETA ** K_ITERS + ALPHA * sum(BETA ** i for i in range(K_ITERS))
EPS = 1e-5
ZERO_ROWS = {N: 8, EX: 4}
T1W = D + 4
T2W = D + 1


def sweep(eng, count, unroll, body, peel=1, tail=1):
    rounds = (count - tail) // unroll
    for c in range(peel * unroll):
        body(c // unroll, c % unroll)
    with eng.Fori(peel, rounds) as r:
        for u in range(unroll):
            body(r, u)
    for c in range(rounds * unroll, count):
        body(c // unroll, c % unroll)


class Phase:

    def __init__(self, nc, name):
        self.nc, self.name, self.ctx, self.sems = nc, name, ExitStack(), []

    def __enter__(self):
        return self

    def sb(self, name, shape, dt=F32):
        return self.ctx.enter_context(self.nc.sbuf_tensor(f"{self.name}_{name}", shape, dt))

    def ps(self, name, shape, dt=F32):
        return self.ctx.enter_context(self.nc.psum_tensor(f"{self.name}_{name}", shape, dt))

    def sem(self, name):
        s = self.ctx.enter_context(self.nc.semaphore(f"{self.name}_{name}"))
        self.sems.append(s)
        return s

    def __exit__(self, *exc):
        if exc[0] is None:
            self.nc.gpsimd.dma_reset()
            for s in self.sems:
                self.nc.gpsimd.sem_clear(s)
            self.nc.all_engine_barrier()
        self.ctx.close()


def held(eng, tick):
    eng.sem_inc(tick, 1)


def build(nc, a, out):
    dram = {}

    def scratch(name, shape, dt=F32):
        dram[name] = nc.dram_tensor(f"scr_{name}", shape, dt, kind="Internal").ap()
        return dram[name]

    srcp, dstp, dlast = scratch("srcp", (EP,), I32), scratch("dstp", (EP,), I32), scratch("dlast", (EP,), I32)
    slast, ilast = scratch("slast", (EP,), I32), scratch("ilast", (EP,), I32)
    dflag, dsame, ssame = scratch("dflag", (EP,), BF16), scratch("dsame", (EP,), U8), scratch("ssame", (EP,), U8)
    agga = scratch("agga", (N, D))
    sorted1, sorted2 = scratch("sorted1", (EP, 2), I32), scratch("sorted2", (EP, 2), I32)
    odeg, ideg, adeg, alast = (scratch(k, (NT,)) for k in ("odeg", "ideg", "adeg", "alast"))
    aggd, aggs = scratch("aggd", (N, D)), scratch("aggs", (N, D))
    c1, x3 = scratch("c1", (N, D)), scratch("x3", (N, D))
    x1, x2 = scratch("x1", (N, T1W)), scratch("x2", (N, T2W))
    sums = [scratch("sums0", (EX, D)), scratch("sums1", (EX, D))]

    keep = ExitStack()

    def sb(name, shape, dt=F32):
        return keep.enter_context(nc.sbuf_tensor(name, shape, dt))

    with keep:
        ident = sb("ident", [P, P])
        identb = sb("identb", [P, P], BF16)
        ident256 = sb("ident256", [P, P], BF16)
        tri = sb("tri", [P, P])
        trib = sb("trib", [P, P], BF16)
        ones = sb("ones", [P, P])
        onesb = sb("onesb", [P, P], BF16)
        iota = sb("iota", [P, NB2], F16)
        window = sb("window", [P, 2 * HALF - 1], BF16)
        srccol, dstcol = sb("srccol", [P, TILES], I32), sb("dstcol", [P, TILES], I32)
        srcg = sb("srcg", [P, TILES], I32)
        dlcol, slcol, ilcol = sb("dlcol", [P, TILES], I32), sb("slcol", [P, TC], I32), sb("ilcol", [P, TC], I32)
        active = sb("active", [P, TILES])
        cnt = sb("cnt", [HALF, 2, NB2], BF16)
        k1, v1 = sb("k1", [P, TILES], I32), sb("v1", [P, TC], I32)
        rounds = sb("rounds", [1, 3], I32)
        lastcol = sb("lastcol", [P, TC], I32)
        w_conv = [sb(f"w_conv{i}", [P, D]) for i in range(2)]
        w_root = [sb(f"w_root{i}", [D + 1, D]) for i in range(2)]
        w_gcn = sb("w_gcn", [D, D])
        w_h = sb("w_h", [P, D])
        w_2 = sb("w_2", [D + 1, D])
        w_s = sb("w_s", [D + 1, D])
        w_n = sb("w_n", [D, D])
        bias_gcn = sb("bias_gcn", [P, D])
        eps = sb("eps", [P, 1])
        zero = sb("zero", [P, J * D])
        s_z0 = keep.enter_context(nc.semaphore("first_zeros"))
        s_z = keep.enter_context(nc.semaphore("zeros"))
        rs_id, rs_od, rs_ida, rs_odb, fac, fac_a, last_n = (
            sb(k, [P, BLOCKS + 1, J]) for k in ("rs_id", "rs_od", "rs_ida", "rs_odb", "fac", "fac_a", "last_n"))

        def put_zeros(eng, sem, t, first, rows, per):
            eng.dma_start(t[bass.ds(first, rows), :].rearrange("(p j) d -> p (j d)", j=per),
                          zero[0:rows // per, 0:per * D]).then_inc(sem, 16)

        def zeros_of_chunk(eng, sem, t, c):
            per = ZERO_ROWS[t.shape[0]]
            first, rows = c * (P * per), P * per
            if isinstance(c, int) and c == CHUNKS - 1:
                while first < t.shape[0]:
                    put_zeros(eng, sem, t, first, min(rows, t.shape[0] - first), per)
                    first += rows
            else:
                put_zeros(eng, sem, t, first, rows, per)

        def zero_count(*tables):
            return 16 * sum(-(-t.shape[0] // (P * ZERO_ROWS[t.shape[0]])) for t in tables)

        with Phase(nc, "setup") as ph:
            i32a = ph.sb("i32a", [P, NB2], I32)
            wt = ph.sb("wt", [D, 5, D])
            brow = ph.sb("brow", [1, 3, D])
            sF, dF, prv, nxt = (ph.sb(k, [P, TILES], I32) for k in ("sF", "dF", "prv", "nxt"))
            fl = ph.sb("fl", [P, TILES])
            lf = ph.sb("lf", [P, TILES])
            flb, li = ph.sb("flb", [P, TILES], BF16), ph.sb("li", [P, TILES], I32)
            same = ph.sb("same", [P, TILES], U8)
            pT = ph.ps("pT", [P, 4, P])
            s_c, s_v, s_ld, s_e, s_t, s_st = (ph.sem(k) for k in (
                "iota", "dve", "weights_in", "edges_in", "turned", "stored"))
            full, tail = (P - 1) * TILES, E - (P - 1) * TILES
            with nc.Block() as block:
                @block.gpsimd
                def _(pool):
                    nc.gpsimd.iota(i32a[:, :], pattern=[[1, NB2]], base=0, channel_multiplier=0).then_inc(s_c, 1)
                    nc.gpsimd.memset(ones[:, :], 1.0).then_inc(s_c, 1)
                    pool.wait_ge(s_c, 2)
                    nc.gpsimd.affine_select(out=ident[:, :], in_=ones[:, :], compare_op=ALU.is_equal, fill=0.0,
                                            base=0, pattern=[[-1, P]], channel_multiplier=1).then_inc(s_c, 1)
                    nc.gpsimd.affine_select(out=tri[:, :], in_=ones[:, :], compare_op=ALU.is_gt, fill=0.0,
                                            base=0, pattern=[[1, P]], channel_multiplier=-1).then_inc(s_c, 1)

                @block.vector
                def _(dve):
                    nc.vector.memset(zero[:, :], 0.0)
                    nc.vector.memset(eps[:, :], EPS)
                    nc.vector.memset(w_h[:, :], 0.0)
                    nc.vector.memset(window[:, :], 0.0)
                    for x_ in (sF, dF):
                        nc.vector.memset(x_[:, :], PADKEY)
                    nc.vector.memset(nxt[:, :], PADKEY)
                    nc.vector.memset(prv[:, :], -1).then_inc(s_v, 1)
                    dve.wait_ge(s_v, 1)
                    nc.vector.memset(window[:, HALF - 1:HALF], 1.0)
                    dve.wait_ge(s_c, 4)
                    nc.vector.tensor_copy(iota[:, :], i32a[:, :])
                    nc.vector.tensor_copy(identb[:, :], ident[:, :])
                    nc.vector.tensor_copy(trib[:, :], tri[:, :])
                    nc.vector.tensor_copy(onesb[:, :], ones[:, :])
                    nc.vector.tensor_scalar(ident256[:, :], ident[:, :], float(NB), None, ALU.mult)
                    dve.wait_ge(s_e, 16 * 10)
                    nc.vector.tensor_tensor(fl[:, :], dF[:, :], prv[:, :], ALU.not_equal)
                    nc.vector.tensor_tensor(lf[:, :], dF[:, :], nxt[:, :], ALU.is_equal).then_inc(s_v, 1)
                    dve.wait_ge(s_v, 2)
                    nc.vector.tensor_scalar(flb[:, :], fl[:, :], NEG, None, ALU.mult)
                    nc.vector.tensor_scalar(same[:, :], fl[:, :], -1.0, 1.0, ALU.mult, ALU.add)
                    nc.vector.scalar_tensor_tensor(lf[:, :], lf[:, :], 2.0 * PADKEY, dF[:, :], ALU.mult, ALU.add).then_inc(s_v, 1)
                    dve.wait_ge(s_v, 3)
                    nc.vector.tensor_scalar(li[:, :], lf[:, :], SKIP, None, ALU.min).then_inc(s_v, 1)
                    dve.wait_ge(s_t, 1)
                    nc.vector.tensor_copy(w_2[0:D, :], pT[0:D, 0, 0:D])
                    nc.vector.tensor_copy(w_s[0:D, :], pT[0:D, 1, 0:D])
                    nc.vector.tensor_copy(w_n[:, :], pT[0:D, 2, 0:D])
                    dve.wait_ge(s_ld, 16 * 17)
                    nc.vector.tensor_tensor(brow[:, 2, :], brow[:, 0, :], brow[:, 1, :], ALU.add).then_inc(s_v, 1)

                @block.tensor
                def _(pe):
                    pe.wait_ge(s_ld, 16 * 17)
                    pe.wait_ge(s_c, 4)
                    for n in range(3):
                        last = nc.tensor.transpose(pT[0:D, n, 0:D], wt[:, n, :], ident[0:D, 0:D])
                    last.then_inc(s_t, 1)

                @block.sync
                def _(sp):
                    sp.wait_ge(s_v, 1)
                    for flat, t in ((a["src"], sF), (a["dst"], dF)):
                        sp.dma_start(t[0:P - 1, :], flat[0:full].rearrange("(p j) -> p j", j=TILES)).then_inc(s_e, 16)
                        sp.dma_start(t[P - 1:P, 0:tail], flat[full:E].rearrange("(p j) -> p j", p=1)).then_inc(s_e, 16)
                    d = a["dst"]
                    sp.dma_start(prv[0:1, 1:TILES], d[0:TILES - 1].rearrange("(p j) -> p j", p=1)).then_inc(s_e, 16)
                    sp.dma_start(prv[1:P - 1, :], d[TILES - 1:full - 1].rearrange("(p j) -> p j", j=TILES)).then_inc(s_e, 16)
                    sp.dma_start(prv[P - 1:P, 0:tail + 1], d[full - 1:E].rearrange("(p j) -> p j", p=1)).then_inc(s_e, 16)
                    sp.dma_start(nxt[0:P - 1, :], d[1:full + 1].rearrange("(p j) -> p j", j=TILES)).then_inc(s_e, 16)
                    sp.dma_start(nxt[P - 1:P, 0:tail - 1], d[full + 1:E].rearrange("(p j) -> p j", p=1)).then_inc(s_e, 16)
                    sp.dma_start(bias_gcn[:, :], a["L2_gnn_bias"].rearrange("(p d) -> p d", p=1).broadcast_to([P, D])
                                 ).then_inc(s_e, 16)
                    sp.wait_ge(s_e, 16 * 10)
                    for flat, t in ((srcp, sF), (dstp, dF)):
                        sp.dma_start(flat.rearrange("(p j) -> p j", p=P), t[:, :]).then_inc(s_st, 16)
                    sp.wait_ge(s_v, 4)
                    sp.dma_start(dflag.rearrange("(p j) -> p j", p=P), flb[:, :]).then_inc(s_st, 16)
                    sp.dma_start(dsame.rearrange("(p j) -> p j", p=P), same[:, :]).then_inc(s_st, 16)
                    sp.dma_start(dlast.rearrange("(p j) -> p j", p=P), li[:, :]).then_inc(s_st, 16)
                    sp.wait_ge(s_v, 5)
                    sp.dma_start(w_s[D:D + 1, :], brow[:, 2, :]).then_inc(s_st, 16)
                    sp.wait_ge(s_st, 16 * 6)

                @block.scalar
                def _(act):
                    act.wait_ge(s_v, 1)
                    row = lambda v: v.rearrange("(p d) -> p d", p=1)
                    for i in range(2):
                        act.dma_start(w_conv[i][0:D, :], a[f"L0_gnn_W{i + 1}_msg"]).then_inc(s_ld, 16)
                        act.dma_start(w_conv[i][D:P, :], a[f"L0_gnn_W{i + 1}_edge"]).then_inc(s_ld, 16)
                        act.dma_start(w_root[i][0:D, :], a[f"L0_gnn_W{i + 1}_root"]).then_inc(s_ld, 16)
                        act.dma_start(w_root[i][D:D + 1, :], row(a[f"L0_gnn_b{i + 1}"])).then_inc(s_ld, 16)
                    act.dma_start(w_gcn[:, :], a["L2_gnn_weight"]).then_inc(s_ld, 16)
                    act.dma_start(wt[:, 0, :], a["L3_gnn_W2"]).then_inc(s_ld, 16)
                    act.dma_start(wt[:, 1, :], a["L3_gnn_Ws"]).then_inc(s_ld, 16)
                    act.dma_start(wt[:, 2, :], a["L3_gnn_Wn"]).then_inc(s_ld, 16)
                    act.dma_start(w_2[D:D + 1, :], row(a["L3_gnn_b2"])).then_inc(s_ld, 16)
                    act.dma_start(brow[:, 0, :], row(a["L3_gnn_bs"])).then_inc(s_ld, 16)
                    act.dma_start(brow[:, 1, :], row(a["L3_gnn_bn"])).then_inc(s_ld, 16)
                    act.dma_start(w_h[D:D + DE17, :], a["L3_gnn_W1"].rearrange("o k -> k o"), allow_slow_non_contiguous=True).then_inc(s_ld, 16)
                    act.dma_start(w_h[D + DE17:D + DE17 + 1, :], row(a["L3_gnn_b1"])).then_inc(s_ld, 16)
                    for c in range(CHUNKS):
                        zeros_of_chunk(act, s_z0, aggd, c)
                    act.wait_ge(s_ld, 16 * 17)


        def columns(name, src, words, outs):
            with Phase(nc, name) as ph:
                raw, rawf = ph.sb("raw", [HALF, 2, P * words], I32), ph.sb("rawf", [HALF, 2, P * words])
                pt = ph.ps("pt", [P, 2 * words, P])
                s_in, s_f, s_t = (ph.sem(k) for k in ("rows_in", "as_float", "turned"))
                with nc.Block() as block:
                    @block.sync
                    def _(sp):
                        for h in range(2):
                            sp.dma_start(raw[:, h, :], src.rearrange("(h q n) -> h q n", h=2, q=HALF)[h]).then_inc(s_in, 16)

                    @block.vector
                    def _(dve):
                        dve.wait_ge(s_in, 32)
                        nc.vector.tensor_copy(rawf[:, :, :], raw[:, :, :]).then_inc(s_f, 1)
                        dve.wait_ge(s_t, 1)
                        for h in range(2):
                            for w in range(words):
                                nc.vector.tensor_copy(outs[w][:, h * HALF:(h + 1) * HALF], pt[:, h * words + w, 0:HALF])

                    @block.tensor
                    def _(pe):
                        pe.wait_ge(s_f, 1)
                        for h in range(2):
                            v = rawf[:, h, :].rearrange("q (n w) -> q w n", w=words)
                            for w in range(words):
                                last = nc.tensor.transpose(pt[:, h * words + w, 0:HALF], v[:, w, :], ident[0:HALF, 0:HALF])
                        last.then_inc(s_t, 1)

        columns("colsrc", srcp, 1, [srccol])
        columns("coldst", dstp, 1, [dstcol])
        columns("collast", dlast, 1, [dlcol])

        def digits(keys, high, dig, digi, inact, link):
            if high:
                nc.vector.tensor_scalar(inact[:, :], keys[:, 0:TILES], INACTIVE.bit_length() - 1, None, ALU.arith_shift_right)
                link(nc.vector.tensor_scalar(digi[:, :], keys[:, 0:TILES], INACTIVE - 1, NB.bit_length() - 1,
                                             ALU.bitwise_and, ALU.arith_shift_right))
                link(nc.vector.scalar_tensor_tensor(dig[:, :], inact[:, :], float(2 * NH), digi[:, :], ALU.mult, ALU.add))
                link(nc.vector.tensor_scalar(dig[:, :], dig[:, :], float(NB2 - 1), None, ALU.min))
            else:
                link(nc.vector.tensor_scalar(digi[:, :], keys[:, 0:TILES], NB - 1, None, ALU.bitwise_and))
                link(nc.vector.tensor_copy(dig[:, :], digi[:, :]))

        class Histogram:

            def __init__(self, ph, cols, table, last_table=None, found=None, source=None, tiles=None):
                self.tiles = tiles
                self.cols, self.table, self.last_table, self.found, self.source = cols, table, last_table, found, source
                self.lo, self.hi = ph.sb("lo", [P, TILES]), ph.sb("hi", [P, TILES])
                self.loi, self.hii = ph.sb("loi", [P, TILES], I32), ph.sb("hii", [P, TILES], I32)
                self.ohl = [ph.sb(f"ohl{v}", [P, CH, NB], BF16) for v in range(2)]
                self.hw = NB2 if tiles == "high" else 2 * NH
                self.ohh = [ph.sb(f"ohh{v}", [P, CH, self.hw], BF16) for v in range(2)]
                if tiles is not None:
                    self.classes = ph.sb("classes", [P, TILES], I32)
                    self.per_tile = [ph.ps("tile", [P, 2, NB])] if tiles == "low" else [ph.ps(f"tile{h}", [P, 512]) for h in range(2)]
                self.hist = ph.sb("hist", [NH, 2, NB])
                self.acc = ph.ps("acc", [P, 2, NB])
                self.s_digits, self.s_oh, self.s_mm, self.s_h, self.s_stored = (
                    ph.sem(k) for k in ("digits", "onehots", "added", "hist", "hist_stored"))
                if last_table is not None:
                    self.run, self.ones_row = ph.sb("run", [NH, 2, NB]), ph.sb("ones_row", [NH, NB])
                    self.off, self.total = ph.sb("off", [NH, 2]), ph.sb("total", [1, 2], I32)
                    self.po, self.po2, self.po3 = (ph.ps(k, [P, 512]) for k in ("po", "po2", "po3"))
                    self.s_run, self.s_off, self.s_tot = (ph.sem(k) for k in ("run", "offsets", "totals"))
                if found is not None:
                    self.srct, self.has = ph.sb("srct", [NH, 2, NB]), ph.sb("has", [NH, 2, NB], BF16)
                    self.pth = ph.ps("pth", [NH, 2, CH, P], BF16)
                    self.oht = [ph.sb(f"oht{v}", [NH, 2, CH, P], BF16) for v in range(2)]
                    self.pf = ph.ps("pf", [P, CH, NB])
                    self.junk, self.hit = ph.sb("junk", [P, NB]), ph.sb("hit", [P, CH])
                    self.s_src, self.s_has, self.s_ot, self.s_oc, self.s_lk, self.s_ttr, self.s_hit = (
                        ph.sem(k) for k in ("source_in", "has", "onehots_turned", "onehots_copied", "looked_up",
                                            "reduced", "hits"))

            def dve_before(self, dve):
                at = [0]

                def link(ins):
                    at[0] += 1
                    ins.then_inc(self.s_digits, 1)
                    dve.wait_ge(self.s_digits, at[0])

                digits(self.cols, False, self.lo, self.loi, None, link)
                if self.tiles == "high":
                    digits(self.cols, True, self.hi, self.hii, self.classes, link)
                else:
                    link(nc.vector.tensor_scalar(self.hii[:, :], self.cols[:, 0:TILES], NB.bit_length() - 1, None,
                                                 ALU.arith_shift_right))
                    link(nc.vector.tensor_copy(self.hi[:, :], self.hii[:, :]))
                if self.last_table is not None:
                    nc.vector.memset(self.ones_row[:, :], 1.0)
                if self.found is not None:
                    dve.wait_ge(self.s_src, 16)
                    nc.vector.tensor_scalar(self.has[:, :, :], self.srct[:, :, :], 0.0, None, ALU.is_gt).then_inc(self.s_has, 1)

            def look(self, dve, c, v):
                dve.wait_ge(self.s_lk, c + 1)
                for j in range(CH):
                    if not (isinstance(c, int) and c == 0 and j == 0):
                        dve.wait_ge(self.s_ttr, CH * c + j)
                    nc.vector.tensor_tensor_reduce(out=self.junk[:, :], in0=self.ohl[v][:, j, :], in1=self.pf[:, j, :],
                                                   scale=1.0, scalar=0.0, op0=ALU.mult, op1=ALU.add,
                                                   accum_out=self.hit[:, j:j + 1]).then_inc(self.s_ttr, 1)
                dve.wait_ge(self.s_ttr, CH * (c + 1))
                nc.vector.tensor_copy(self.found[:, bass.ds(c * CH, CH)], self.hit[:, :]).then_inc(self.s_hit, 1)

            def dve_step(self, dve, c, v):
                if not (isinstance(c, int) and c < 2):
                    dve.wait_ge(self.s_mm, c - 1)
                    if self.found is not None:
                        self.look(dve, c - 2, v)
                        dve.wait_ge(self.s_hit, c - 1)
                for j in range(CH):
                    nc.vector.tensor_scalar(self.ohl[v][:, j, :], iota[:, 0:NB], self.lo[:, bass.ds(c * CH + j, 1)],
                                            None, ALU.is_equal)
                    last = nc.vector.tensor_scalar(self.ohh[v][:, j, :], iota[:, 0:self.hw],
                                                   self.hi[:, bass.ds(c * CH + j, 1)], None, ALU.is_equal)
                last.then_inc(self.s_oh, 1)

            def dve_after(self, dve):
                if self.found is not None:
                    for c in (CHUNKS - 2, CHUNKS - 1):
                        self.look(dve, c, c % 2)
                dve.wait_ge(self.s_mm, CHUNKS)
                if self.tiles == "low":
                    nc.vector.tensor_copy(cnt[:, :, 0:NB], self.per_tile[0][0:HALF, :, :])
                elif self.tiles == "high":
                    for h in range(2):
                        nc.vector.tensor_copy(cnt[:, h, :], self.per_tile[h][0:HALF, 0:NB2])
                nc.vector.tensor_copy(self.hist[:, :, :], self.acc[0:NH, :, :]).then_inc(self.s_h, 1)
                if self.last_table is None:
                    return
                run, total, off = self.run, self.total, self.off
                dve.wait_ge(self.s_h, 1)
                for h in range(2):
                    last = nc.vector.tensor_tensor_scan(run[:, h, :], self.ones_row[:, :], self.hist[:, h, :], 0.0,
                                                        ALU.mult, ALU.add)
                last.then_inc(self.s_run, 1)
                dve.wait_ge(self.s_off, 1)
                nc.vector.tensor_copy(off[:, 0:1], self.po[0:NH, 0:1])
                nc.vector.tensor_scalar(total[:, 0:1], self.po3[0:1, 0:1], float(RW - 1), None, ALU.add)
                nc.vector.tensor_copy(total[:, 1:2], self.po3[0:1, 0:1])
                nc.vector.tensor_copy(off[:, 1:2], self.po2[0:NH, 0:1]).then_inc(self.s_tot, 1)
                dve.wait_ge(self.s_tot, 1)
                nc.vector.tensor_scalar(total[:, :], total[:, :], RW.bit_length() - 1, None,
                                        ALU.arith_shift_right).then_inc(self.s_tot, 1)
                dve.wait_ge(self.s_tot, 2)
                nc.vector.tensor_scalar(rounds[:, 0:1], total[:, 0:1], 2.0, -2.0, ALU.max, ALU.add)
                nc.vector.tensor_scalar(rounds[:, 2:3], total[:, 1:2], float(RMAX - 2), None, ALU.min).then_inc(self.s_tot, 1)
                dve.wait_ge(self.s_tot, 3)
                nc.vector.tensor_scalar(rounds[:, 1:2], rounds[:, 2:3], -1.0, float(RMAX - 2), ALU.mult, ALU.add)
                dve.wait_ge(self.s_run, 1)
                for h in range(2):
                    last = nc.vector.tensor_scalar(run[:, h, :], run[:, h, :], off[:, h:h + 1], -1.0, ALU.add, ALU.add)
                last.then_inc(self.s_run, 1)
                dve.wait_ge(self.s_run, 2)
                nc.vector.tensor_scalar(run[:, :, :], run[:, :, :], 0.0, None, ALU.max).then_inc(self.s_run, 1)

            def pe_lookup(self, pe, c, v):
                if isinstance(c, int) and c == 0:
                    pe.wait_ge(self.s_has, 1)
                pe.wait_ge(self.s_oc, c + 1)
                if not (isinstance(c, int) and c == 0):
                    pe.wait_ge(self.s_hit, c)
                for j in range(CH):
                    for h in range(2):
                        last = nc.tensor.matmul(self.pf[:, j, :], self.oht[v][:, h, j, :], self.has[:, h, :],
                                                start=h == 0, stop=h == 1)
                last.then_inc(self.s_lk, 1)

            def pe_step(self, pe, c, v):
                static = isinstance(c, int)
                pe.wait_ge(self.s_oh, c + 1)
                if self.found is not None:
                    if not (static and c == 0):
                        pe.wait_ge(self.s_oc, c)
                    for j in range(CH):
                        for h in range(2):
                            last = nc.tensor.transpose(self.pth[:, h, j, :], self.ohh[v][:, j, h * NH:(h + 1) * NH],
                                                       identb[:, :])
                    last.then_inc(self.s_ot, 1)
                for j in range(CH):
                    for h in range(2):
                        last = nc.tensor.matmul(self.acc[0:NH, h, :], self.ohh[v][:, j, h * NH:(h + 1) * NH],
                                                self.ohl[v][:, j, :], start=static and c == 0 and j == 0 and h == 0,
                                                stop=static and c == CHUNKS - 1 and j == CH - 1 and h == 1)
                if self.tiles is not None:
                    for j in range(CH):
                        low = self.tiles == "low"
                        to = self.per_tile[0][0:HALF, j % 2, :] if low else self.per_tile[j % 2][0:HALF, 0:NB2]
                        last = nc.tensor.matmul(to, window[:, bass.ds(HALF - 1 - (2 * c + j // 2), HALF)],
                                                (self.ohl if low else self.ohh)[v][:, j, :],
                                                start=static and c == 0 and j < (1 if low else 2),
                                                stop=static and c == CHUNKS - 1 and j >= (3 if low else 2))
                last.then_inc(self.s_mm, 1)
                if self.found is not None and not (static and c == 0):
                    self.pe_lookup(pe, c - 1, 1 - v)

            def pe_after(self, pe):
                if self.found is not None:
                    self.pe_lookup(pe, CHUNKS - 1, (CHUNKS - 1) % 2)
                if self.last_table is not None:
                    run = self.run
                    pe.wait_ge(self.s_run, 1)
                    nc.tensor.matmul(self.po[0:NH, 0:1], tri[0:NH, 0:NH], run[:, 0, NB - 1:NB], start=True, stop=True)
                    nc.tensor.matmul(self.po2[0:NH, 0:1], tri[0:NH, 0:NH], run[:, 1, NB - 1:NB], start=True, stop=False)
                    nc.tensor.matmul(self.po2[0:NH, 0:1], ones[0:NH, 0:NH], run[:, 0, NB - 1:NB], start=False, stop=True)
                    for h in range(2):
                        last = nc.tensor.matmul(self.po3[0:1, 0:1], ones[0:NH, 0:1], run[:, h, NB - 1:NB],
                                                start=h == 0, stop=h == 1)
                    last.then_inc(self.s_off, 1)

            def act_step(self, act, c, v):
                if self.found is None:
                    return
                act.wait_ge(self.s_ot, c + 1)
                if not (isinstance(c, int) and c < 2):
                    act.wait_ge(self.s_lk, c - 1)
                nc.scalar.copy(self.oht[v][:, :, :, :], self.pth[:, :, :, :]).then_inc(self.s_oc, 1)

            def sp_before(self, sp):
                if self.found is not None:
                    sp.dma_start(self.srct[:, :, :], self.source.rearrange("(h q n) -> q h n", h=2, q=NH)
                                 ).then_inc(self.s_src, 16)

            def sp_after(self, sp):
                view = lambda t: t.rearrange("(h q n) -> q h n", h=2, q=NH)
                sp.wait_ge(self.s_h, 1)
                sp.dma_start(view(self.table), self.hist[:, :, :]).then_inc(self.s_stored, 16)
                if self.last_table is not None:
                    sp.wait_ge(self.s_run, 3)
                    sp.dma_start(view(self.last_table), self.run[:, :, :]).then_inc(self.s_stored, 16)
                sp.wait_ge(self.s_stored, 32 if self.last_table is not None else 16)

        def histogram(name, cols, table, last_table, tiles):
            with Phase(nc, name) as ph:
                h = Histogram(ph, cols, table, last_table, tiles=tiles)
                with nc.Block() as block:
                    @block.vector
                    def _(dve):
                        h.dve_before(dve)
                        sweep(dve, CHUNKS, 2, lambda r, u: h.dve_step(dve, 2 * r + u, u))
                        h.dve_after(dve)

                    @block.tensor
                    def _(pe):
                        sweep(pe, CHUNKS, 2, lambda r, u: h.pe_step(pe, 2 * r + u, u))
                        h.pe_after(pe)

                    @block.sync
                    def _(sp):
                        h.sp_after(sp)

        def edge_phase(name, mode, gidx=None, table=None, attr=None, de=0, sidx=None, target=None,
                       weight=None, hh=None, cols=None, wr=None, zeroed=None, flags=None,
                       gidx2=None, table2=None, rounds_of=None, first_round_of=None,
                       counted=None, zero_also=()):
            turn_w = P if mode in ("conv", "edge") else D
            scatter = sidx is not None
            formed = mode in ("prop", "first")
            scaled = mode in ("init", "gcn")
            LB = 2 if mode == "edge" else 1
            NG = 2 if mode == "first" else 1
            GIN = 64 * NG
            dyn = rounds_of is not None
            with Phase(nc, name) as ph:
                g = [ph.sb(f"g{u}", [P, CH, 2 * D if mode == "first" else P]) for u in range(GR)]
                f = [ph.sb(f"f{u}", [P, CH, D]) for u in range(2)] if formed else None
                ts = [ph.sb(f"ts{u}", [P, CW]) for u in range(2)] if not formed else None
                sc = [ph.sb(f"sc{u}", [D, CW]) for u in range(2)]
                rows = [ph.sb(f"rows{u}", [P, CH, D]) for u in range(2)]
                gslot = [ph.sb(f"gslot{u}", [P, NG, CH], I32) for u in range(GR)]
                sslot = [ph.sb(f"sslot{u}", [P, CH], I32) for u in range(2)]
                pt = [ph.ps(f"pt{u}", [P, CW]) for u in range(2)]
                side = Histogram(ph, *counted) if counted is not None else None
                NP = 1 if side is not None and side.found is not None else 2
                pr = [ph.ps(f"pr{u}", [P, CW]) for u in range(NP)]
                pm = [ph.ps(f"pm{u}", [P, CW]) for u in range(NP)] if mode == "conv" else None
                if mode == "edge":
                    p_hid, p_w = ph.ps("phid", [P, CW]), ph.ps("pw", [P, CW])
                    hs, msg = ph.sb("hs", [D + 1, CW]), ph.sb("msg", [D, CW])
                s_g = [ph.sem(f"gathered{u}") for u in range(GR)]
                s_at = [ph.sem(f"attr_in{u}") for u in range(GR)]
                s_out = [ph.sem(f"out{u}") for u in range(2)]
                s_ready, s_slot, s_f, s_turn, s_te, s_mm, s_scan, s_back, s_rows, s_tick, s_one = (
                    ph.sem(k) for k in ("buffers_ready", "slots", "formed", "turned", "turned_copied", "product",
                                        "scanned", "back", "rows", "tick", "ones_row"))
                s_hid, s_relu, s_w, s_msg, s_half, s_half2, s_cols = (
                    ph.sem(k) for k in ("hidden", "relu", "edge_weight", "message", "first_term", "second_term", "columns"))
                gw = table.shape[1]

                def count(eng):
                    if not dyn:
                        return None, 0
                    n = eng.value_load(rounds_of, min_val=0, max_val=RMAX - 2) + 2
                    o = 0 if first_round_of is None else eng.value_load(first_round_of, min_val=0, max_val=RMAX - 2)
                    return n, o

                def chunks(eng, n, body, tail=1):
                    if n is None:
                        sweep(eng, CHUNKS, GR, body, tail=tail)
                        return
                    for u in range(GR):
                        body(0, u)
                    with eng.Fori(1, n) as r:
                        for u in range(GR):
                            body(r, u)

                def trail(n, k, body):
                    for i in range(k, 0, -1):
                        body(*(divmod(CHUNKS - i, GR) if n is None else (n - 1, GR - i)))

                def behind(r, u, k):
                    return r + (u - k) // GR, (u - k) % GR

                def known(c, least):
                    return isinstance(c, int) and c < least

                with nc.Block() as block:
                    @block.gpsimd
                    def _(pool):
                        n, o = count(pool)

                        def put(r, u):
                            c = GR * r + u
                            pool.wait_ge(s_rows, c + 1)
                            if zeroed is not None and known(c, 1):
                                pool.wait_ge(*zeroed)
                            held(pool, s_tick)
                            for j in range(CH):
                                nc.gpsimd.indirect_dma_start(
                                    target[:, :], bass.IndirectOffsetOnAxis(ap=sslot[u % 2][:, j:j + 1], axis=0),
                                    rows[u % 2][:, j, :], None, bounds_check=N - 1, oob_is_err=False
                                    ).then_inc(s_out[u % 2], 16)

                        def step(r, u):
                            c = GR * r + u
                            pool.wait_ge(s_slot, c + 1)
                            if not known(c, GR):
                                pool.wait_ge(s_f if formed else s_turn, c + 1 - GR)
                                if mode == "init":
                                    pool.wait_ge(s_cols, c + 1 - GR)
                            held(pool, s_tick)
                            for k, t in enumerate([table, table2][:NG]):
                                for j in range(CH):
                                    nc.gpsimd.indirect_dma_start(
                                        g[u][:, j, k * D:k * D + gw], None, t[:, :],
                                        bass.IndirectOffsetOnAxis(ap=gslot[u][:, k, j:j + 1], axis=0)
                                        ).then_inc(s_g[u], 16)
                            if scatter and not known(c, LB + 1):
                                put(*behind(r, u, LB + 1))

                        if mode in ("conv", "edge"):
                            for u in range(GR):
                                nc.gpsimd.memset(g[u][:, :, :], 1.0).then_inc(s_ready, 1)
                            pool.wait_ge(s_ready, GR)
                        chunks(pool, n, step)
                        if scatter:
                            trail(n, LB + 1, put)
                        for u in range(GR):
                            pool.wait_ge(s_g[u], GIN * (-(-(CHUNKS - u) // GR) if n is None else n))
                        if scatter:
                            for u in range(2):
                                pool.wait_ge(s_out[u], 64 * (-(-(CHUNKS - u) // 2) if n is None else 2 * n))
                        held(pool, s_tick)

                    @block.sync
                    def _(sp):
                        n, o = count(sp)
                        if side is not None:
                            side.sp_before(sp)
                        if attr is not None:
                            def load(r, u):
                                c = GR * r + u
                                if known(c, GR):
                                    sp.wait_ge(s_ready, GR)
                                else:
                                    sp.wait_ge(s_turn, c + 1 - GR)
                                if isinstance(c, int) and c == CHUNKS - 1:
                                    left = E - c * CW
                                    nt = left // P
                                    sp.dma_start(g[u][:, 0:nt, D:D + de],
                                                 attr[c * CW:c * CW + nt * P, :].rearrange("(j p) d -> p j d", p=P)
                                                 ).then_inc(s_at[u], 16)
                                    sp.dma_start(g[u][0:left - nt * P, nt, D:D + de], attr[c * CW + nt * P:E, :]
                                                 ).then_inc(s_at[u], 16)
                                else:
                                    sp.dma_start(g[u][:, :, D:D + de],
                                                 attr[bass.ds(c * CW, CW), :].rearrange("(j p) d -> p j d", p=P)
                                                 ).then_inc(s_at[u], 16)
                                for t in zero_also:
                                    zeros_of_chunk(sp, s_z, t, c)
                            chunks(sp, n, load)
                        if wr is not None:
                            def store(r, u):
                                c = GR * r + u
                                sp.wait_ge(s_rows, c + 1)
                                sp.dma_start(wr[bass.ds(c * CW, CW), :].rearrange("(j p) d -> p j d", p=P),
                                             rows[u % 2][:, :, :]).then_inc(s_out[u % 2], 16)
                            chunks(sp, n, store)
                            for u in range(2):
                                sp.wait_ge(s_out[u], 16 * 2 * n)
                            held(sp, s_tick)
                        if side is not None:
                            side.sp_after(sp)

                    @block.scalar
                    def _(act):
                        n, o = count(act)

                        def src_of(c):
                            return c * CH if isinstance(o, int) else nc.s_assert_within(
                                c * CH + o * (GR * CH), 0, TC - CH,
                                skip_runtime_bounds_check_because="rounds and first round add up to RMAX")

                        def slot(r, u):
                            c = GR * r + u
                            if not known(c, GR):
                                act.wait_ge(s_g[u], GIN * r)
                            if mode == "first":
                                nc.scalar.copy(gslot[u][:, 1, :], gidx2[:, bass.ds(src_of(c), CH)])
                            nc.scalar.copy(gslot[u][:, 0, :], gidx[:, bass.ds(src_of(c), CH)]).then_inc(s_slot, 1)

                        def evict(r, u):
                            c = GR * r + u
                            v = u % 2
                            if not known(c, 2):
                                act.wait_ge(s_out[v], (64 if scatter else 16) * (2 * r + u // 2))
                            act.wait_ge(s_back, c + 1)
                            if scatter:
                                nc.scalar.copy(sslot[v][:, :], sidx[:, bass.ds(src_of(c), CH)])
                            nc.scalar.copy(rows[v][:, :, :], pr[v % NP][:, 0:CH * D].rearrange("p (j d) -> p j d", d=D)
                                           ).then_inc(s_rows, 1)

                        def step(r, u):
                            c = GR * r + u
                            v = u % 2
                            if n is not None or not (isinstance(c, int) and c >= CHUNKS - 2):
                                slot(*behind(r, u, -2))
                            if mode == "init":
                                act.wait_ge(s_f, c + 1)
                                nc.scalar.copy(hh[:, bass.ds(c * CH, CH), :], g[u][:, :, 0:D])
                                for k, col in enumerate(cols):
                                    last = nc.scalar.copy(col[:, bass.ds(c * CH, CH)], g[u][:, :, D + 1 + k])
                                last.then_inc(s_cols, 1)
                            if not formed:
                                act.wait_ge(s_turn, c + 1)
                                if not known(c, 2):
                                    act.wait_ge({"conv": s_mm, "edge": s_msg}.get(mode, s_scan), c - 1)
                                if mode == "init":
                                    nc.scalar.mul(ts[v][0:D, :], pt[v][0:D, :], 1.0 / ALPHA).then_inc(s_te, 1)
                                else:
                                    nc.scalar.copy(ts[v][0:turn_w, :], pt[v][0:turn_w, :]).then_inc(s_te, 1)
                            if not known(c, LB):
                                evict(*behind(r, u, LB))
                            if mode == "edge":
                                act.wait_ge(s_hid, c + 1)
                                if not known(c, 1):
                                    act.wait_ge(s_w, c)
                                nc.scalar.activation(hs[0:D, :], p_hid[0:D, :], ACT.Relu).then_inc(s_relu, 1)
                            if side is not None:
                                side.act_step(act, c, v)

                        slot(0, 0)
                        slot(0, 1)
                        chunks(act, n, step, tail=2)
                        trail(n, LB, evict)

                    @block.tensor
                    def _(pe):
                        n, o = count(pe)

                        def back(r, u):
                            c = GR * r + u
                            v = u % 2
                            pe.wait_ge(s_scan, c + 1)
                            if not known(c, NP):
                                pe.wait_ge(s_rows, c + 1 - NP)
                            for j in range(CH):
                                last = nc.tensor.matmul(pr[v % NP][:, j * D:(j + 1) * D], sc[v][:, j * P:(j + 1) * P],
                                                        weight if weight is not None and mode != "conv" else ident[0:D, 0:D],
                                                        start=True, stop=True)
                            last.then_inc(s_back, 1)

                        def edge_weight(r, u):
                            c = GR * r + u
                            pe.wait_ge(s_relu, c + 1)
                            if known(c, 1):
                                pe.wait_ge(s_one, 1)
                            else:
                                pe.wait_ge(s_msg, c)
                            nc.tensor.matmul(p_w[0:D, :], w_2[:, :], hs[:, :], start=True, stop=True).then_inc(s_w, 1)

                        def step(r, u):
                            c = GR * r + u
                            v = u % 2
                            if formed or scaled:
                                pe.wait_ge(s_f, c + 1)
                                if not known(c, 2):
                                    pe.wait_ge(s_scan if formed else s_te, c - 1)
                            else:
                                pe.wait_ge(s_g[u], GIN * (r + 1))
                                if attr is not None:
                                    n_last = 32 if isinstance(c, int) and c == CHUNKS - 1 else 16
                                    pe.wait_ge(s_at[u], 16 * r + n_last)
                                if not known(c, 2):
                                    pe.wait_ge(s_te, c - 1)
                            for j in range(CH):
                                last = nc.tensor.transpose(pt[v][0:turn_w, j * P:(j + 1) * P],
                                                           (f[v] if f else g[u])[:, j, 0:turn_w], ident[:, :])
                            last.then_inc(s_turn, 1)
                            if mode == "conv":
                                pe.wait_ge(s_te, c + 1)
                                if not known(c, NP):
                                    pe.wait_ge(s_scan, c + 1 - NP)
                                nc.tensor.matmul(pm[v % NP][0:D, :], weight, ts[v][:, :], start=True, stop=True
                                                 ).then_inc(s_mm, 1)
                            if mode == "edge":
                                if not known(c, 1):
                                    edge_weight(*behind(r, u, 1))
                                pe.wait_ge(s_te, c + 1)
                                if not known(c, 1):
                                    pe.wait_ge(s_relu, c)
                                nc.tensor.matmul(p_hid[0:D, :], w_h[:, :], ts[v][:, :], start=True, stop=True
                                                 ).then_inc(s_hid, 1)
                            if not known(c, LB):
                                back(*behind(r, u, LB))
                            if side is not None:
                                side.pe_step(pe, c, v)

                        chunks(pe, n, step)
                        if mode == "edge":
                            back(*divmod(CHUNKS - 2, GR))
                            edge_weight(*divmod(CHUNKS - 1, GR))
                            back(*divmod(CHUNKS - 1, GR))
                        else:
                            trail(n, LB, back)
                        if side is not None:
                            side.pe_after(pe)

                    @block.vector
                    def _(dve):
                        n, o = count(dve)
                        if mode == "edge":
                            nc.vector.memset(hs[D:D + 1, :], 1.0).then_inc(s_one, 1)
                        if side is not None:
                            side.dve_before(dve)

                        def form(r, u):
                            c = GR * r + u
                            v = u % 2
                            dve.wait_ge(s_g[u], GIN * (r + 1))
                            if formed and not known(c, 2):
                                dve.wait_ge(s_turn, c - 1)
                            if scaled:
                                for j in range(CH):
                                    last = nc.vector.tensor_scalar(g[u][:, j, 0:D], g[u][:, j, 0:D], g[u][:, j, D:D + 1], None, ALU.mult)
                                last.then_inc(s_f, 1)
                                return
                            tile_ = lambda j: bass.ds(c * CH + j, 1)
                            h_ = lambda j: hh[:, tile_(j), :].rearrange("p o d -> p (o d)")
                            if mode == "first":
                                for j in range(CH):
                                    last = nc.vector.tensor_scalar(g[u][:, j, D:2 * D], g[u][:, j, D:2 * D],
                                                                   cols[0][:, tile_(j)], None, ALU.mult)
                                last.then_inc(s_half, 1)
                                dve.wait_ge(s_half, c + 1)
                                for j in range(CH):
                                    last = nc.vector.scalar_tensor_tensor(f[v][:, j, :], g[u][:, j, D:2 * D], 1.0 / ALPHA,
                                                                          h_(j), ALU.mult, ALU.add)
                                last.then_inc(s_half2, 1)
                                dve.wait_ge(s_half2, c + 1)
                                nc.vector.tensor_tensor(hh[:, bass.ds(c * CH, CH), :], hh[:, bass.ds(c * CH, CH), :],
                                                        g[u][:, :, D:2 * D], ALU.add)
                            for j in range(CH):
                                last = nc.vector.scalar_tensor_tensor(
                                    f[v][:, j, :], g[u][:, j, 0:D], cols[1][:, tile_(j)],
                                    f[v][:, j, :] if mode == "first" else h_(j), ALU.mult, ALU.add)
                            last.then_inc(s_f, 1)

                        def message(r, u):
                            c = GR * r + u
                            dve.wait_ge(s_w, c + 1)
                            if not known(c, 1):
                                dve.wait_ge(s_scan, c)
                            nc.vector.tensor_tensor(msg[:, :], p_w[0:D, :], ts[u % 2][0:D, :], ALU.mult
                                                    ).then_inc(s_msg, 1)
                            dve.wait_ge(s_msg, c + 1)

                        def scan(r, u):
                            c = GR * r + u
                            v = u % 2
                            if mode == "edge":
                                message(r, u)
                                data = msg[:, :]
                            elif mode == "conv":
                                dve.wait_ge(s_mm, c + 1)
                                data = pm[v % NP][0:D, :]
                            elif formed:
                                dve.wait_ge(s_turn, c + 1)
                                data = pt[v][0:D, :]
                            else:
                                dve.wait_ge(s_te, c + 1)
                                data = ts[v][0:D, :]
                            if not known(c, 2):
                                dve.wait_ge(s_back, c - 1)
                            if not known(c, 1):
                                dve.wait_ge(s_scan, c)
                            at_edge = c * CW if isinstance(o, int) else nc.s_assert_within(
                                c * CW + o * RW, 0, EX - CW,
                                skip_runtime_bounds_check_because="rounds and first round add up to RMAX")
                            nc.vector.tensor_tensor_scan(
                                sc[v][:, :], flags[:, bass.ds(at_edge, CW)], data,
                                (0.0 if mode != "conv" else NEG) if known(c, 1) else sc[1 - v][:, CW - 1:CW],
                                ALU.add if mode == "conv" else ALU.mult,
                                ALU.max if mode == "conv" else ALU.add).then_inc(s_scan, 1)

                        def step(r, u):
                            c = GR * r + u
                            form(r, u)
                            if not known(c, 1):
                                scan(*behind(r, u, 1))

                        def counted_scan(r, u):
                            side.dve_step(dve, GR * r + u, u % 2)
                            scan(r, u)

                        chunks(dve, n, step if formed or scaled else scan if side is None else counted_scan)
                        if formed or scaled:
                            trail(n, 1, scan)
                        if side is not None:
                            side.dve_after(dve)

        class Radix:

            def __init__(self, ph, keys, vals, high, target):
                nb = self.nb = NB2 if high else NB
                self.keys, self.vals, self.high, self.target = keys, vals, high, target
                self.dig, self.digi = ph.sb("dig", [P, TILES]), ph.sb("digi", [P, TILES], I32)
                self.inact = ph.sb("inact", [P, TILES], I32)
                self.oh = [ph.sb(f"oh{v}", [P, CH, nb], BF16) for v in range(2)]
                self.junk = [ph.sb(f"junk{j}", [P, nb], BF16) for j in range(CH)]
                self.base = ph.sb("base", [HALF, nb + 1])
                self.tot, self.ones_row, self.rf, self.cntf = (ph.sb(k, [HALF, nb]) for k in (
                    "tot", "ones_row", "rf", "cntf"))
                self.ri, self.rpart = (ph.sb(k, [HALF, nb], I32) for k in ("ri", "rpart"))
                self.rhi, self.rlo = ([ph.sb(f"{k}{h}", [HALF, nb], BF16) for h in range(2)] for k in ("rhi", "rlo"))
                self.posf = [ph.sb(f"posf{v}", [P, CH]) for v in range(GR)]
                self.pos = [ph.sb(f"pos{v}", [P, CH], I32) for v in range(GR)]
                self.pay = [ph.sb(f"pay{v}", [P, CH, 2], I32) for v in range(GR)]
                self.pp = [ph.ps(f"pp{i}", [P, 2, 512]) for i in range(2)]
                self.s_link, self.s_pre, self.s_base, self.s_oh, self.s_pos, self.s_red, self.s_rank, self.s_pay, \
                    self.s_tick = (ph.sem(k) for k in ("base_chain", "prefixes", "bases", "onehots", "positions",
                                                       "reduced", "ranked", "payload", "tick"))
                self.s_sc = [ph.sem(f"scattered{v}") for v in range(GR)]

            def dve_before(self, dve):
                nb, acc = self.nb, self.pp[0]
                at = [0]

                def link(ins):
                    at[0] += 1
                    ins.then_inc(self.s_link, 1)
                    dve.wait_ge(self.s_link, at[0])

                nc.vector.memset(self.ones_row[:, :], 1.0)
                nc.vector.memset(self.base[:, 0:1], 0.0)
                digits(self.keys, self.high, self.dig, self.digi, self.inact, link)
                link(nc.vector.tensor_copy(self.cntf[:, :], cnt[:, 0, 0:nb]))
                dve.wait_ge(self.s_pre, 1)
                link(nc.vector.tensor_copy(self.tot[:, :], acc[0:HALF, 1, 0:nb]))
                link(nc.vector.tensor_tensor_scan(self.base[:, 1:nb + 1], self.ones_row[:, :], self.tot[:, :], 0.0,
                                                  ALU.mult, ALU.add))
                link(nc.vector.tensor_tensor(self.rf[:, :], acc[0:HALF, 0, 0:nb], self.base[:, 0:nb], ALU.add))
                for h in range(2):
                    if h:
                        link(nc.vector.tensor_tensor(self.rf[:, :], self.rf[:, :], self.cntf[:, :], ALU.add))
                    link(nc.vector.tensor_copy(self.ri[:, :], self.rf[:, :]))
                    link(nc.vector.tensor_scalar(self.rpart[:, :], self.ri[:, :], 8, None, ALU.arith_shift_right))
                    link(nc.vector.tensor_copy(self.rhi[h][:, :], self.rpart[:, :]))
                    link(nc.vector.tensor_scalar(self.rpart[:, :], self.ri[:, :], NB - 1, None, ALU.bitwise_and))
                    last = nc.vector.tensor_copy(self.rlo[h][:, :], self.rpart[:, :])
                    if h == 0:
                        link(last)
                last.then_inc(self.s_base, 1)

            def rank(self, dve, c, v, r):
                if not (isinstance(c, int) and c < GR):
                    dve.wait_ge(self.s_sc[v], 64 * r)
                for j in range(CH):
                    if j % 2 == 0:
                        dve.wait_ge(self.s_pos, 2 * c + j // 2 + 1)
                    nc.vector.tensor_tensor_reduce(out=self.junk[j][:, :], in0=self.oh[v % 2][:, j, :],
                                                   in1=self.pp[j // 2][:, j % 2, 0:self.nb],
                                                   scale=1.0, scalar=0.0, op0=ALU.mult, op1=ALU.add,
                                                   accum_out=self.posf[v][:, j:j + 1]).then_inc(self.s_red, 1)
                dve.wait_ge(self.s_red, CH * c + CH)
                nc.vector.tensor_copy(self.pos[v][:, :], self.posf[v][:, :]).then_inc(self.s_rank, 1)

            def dve_step(self, dve, c, v, r):
                if not (isinstance(c, int) and c < 2):
                    dve.wait_ge(self.s_rank, c - 1)
                for j in range(CH):
                    last = nc.vector.tensor_scalar(self.oh[v % 2][:, j, :], iota[:, 0:self.nb],
                                                   self.dig[:, bass.ds(c * CH + j, 1)], None, ALU.is_equal)
                last.then_inc(self.s_oh, 1)
                if not (isinstance(c, int) and c == 0):
                    self.rank(dve, c - 1, (v - 1) % GR, r + (v - 1) // GR)

            def dve_after(self, dve):
                self.rank(dve, CHUNKS - 1, (CHUNKS - 1) % GR, (CHUNKS - 1) // GR)

            def pe_before(self, pe):
                nb, acc = self.nb, self.pp[0]
                for s, t in ((0, trib), (1, onesb)):
                    for h in range(2):
                        last = nc.tensor.matmul(acc[0:HALF, s, 0:nb], t[0:HALF, 0:HALF], cnt[:, h, 0:nb],
                                                start=h == 0, stop=h == 1)
                last.then_inc(self.s_pre, 1)
                pe.wait_ge(self.s_base, 1)

            def pe_step(self, pe, c, v, r):
                pe.wait_ge(self.s_oh, c + 1)
                for j in range(CH):
                    if j % 2 == 0 and not (isinstance(c, int) and c == 0):
                        pe.wait_ge(self.s_red, CH * c + j - 2)
                    to = self.pp[j // 2][:, j % 2, 0:self.nb]
                    nc.tensor.matmul(to, trib[:, :], self.oh[v % 2][:, j, :], start=True, stop=False)
                    for idn, part in ((ident256, self.rhi), (identb, self.rlo)):
                        last = nc.tensor.matmul(to, idn[0:HALF, bass.ds(2 * c + j // 2, 1)].broadcast_to([HALF, P]),
                                                part[j % 2][:, :], start=False, stop=part is self.rlo)
                    if j % 2 == 1:
                        last.then_inc(self.s_pos, 1)

            def act_step(self, act, c, v, r):
                if not (isinstance(c, int) and c < GR):
                    act.wait_ge(self.s_sc[v], 64 * r)
                nc.scalar.copy(self.pay[v][:, :, 0], self.keys[:, bass.ds(c * CH, CH)])
                nc.scalar.copy(self.pay[v][:, :, 1], self.vals[:, bass.ds(c * CH, CH)]).then_inc(self.s_pay, 1)

            def scatter(self, pool, c, v, r):
                pool.wait_ge(self.s_pay, c + 1)
                pool.wait_ge(self.s_rank, c + 1)
                held(pool, self.s_tick)
                for j in range(CH):
                    nc.gpsimd.indirect_dma_start(
                        self.target[:, :], bass.IndirectOffsetOnAxis(ap=self.pos[v][:, j:j + 1], axis=0),
                        self.pay[v][:, j, :], None).then_inc(self.s_sc[v], 16)

            def pool_step(self, pool, c, v, r):
                if not (isinstance(c, int) and c == 0):
                    self.scatter(pool, c - 1, (v - 1) % GR, r + (v - 1) // GR)

            def pool_after(self, pool):
                self.scatter(pool, CHUNKS - 1, (CHUNKS - 1) % GR, (CHUNKS - 1) // GR)
                for v in range(GR):
                    pool.wait_ge(self.s_sc[v], 64 * -(-(CHUNKS - v) // GR))

        with Phase(nc, "clamp") as ph:
            with nc.Block() as block:
                @block.vector
                def _(dve):
                    nc.vector.tensor_scalar(srcg[:, :], srccol[:, :], float(N - 1), None, ALU.min)
                    for t, fill in ((v1, 0), (lastcol, 0), (slcol, int(SKIP)), (ilcol, int(SKIP))):
                        nc.vector.memset(t[:, :], fill)

        def dense_phase(name, mode, sort=None):
            R = 4
            with Phase(nc, name) as ph:
                kinds = {"conv1": ["x", "aggd"], "conv2": ["c1", "aggd", "x"], "prop": ["x1", "aggs", "agga"],
                         "gcn": ["x2", "aggd"], "edge": ["x3", "aggd"]}[mode]
                product = mode in ("conv1", "conv2", "edge")
                norm = mode != "conv1"
                wgt = {"conv1": w_root[0], "conv2": w_root[1], "edge": w_s}.get(mode)
                tabs = dict(dram, x=a["x"])
                bufs = [[ph.sb(f"in_{k}{u}", [P, J, tabs[k].shape[1]]) for k in kinds] for u in range(R)]
                z = [ph.sb(f"z{u}", [P, J, D]) for u in range(R)]
                out_t = {"conv1": c1, "conv2": x1, "prop": x2, "gcn": x3, "edge": out}[mode]
                factors = {"conv2": [rs_ida, fac, fac_a, last_n], "prop": [rs_od]}.get(mode, [])
                res = [ph.sb(f"res{u}", [P, J, D + len(factors)]) for u in range(R)]
                bst = [ph.sb(f"bst{u}", [P, J, 6]) for u in range(R)]
                st = [ph.sb(f"st{u}", [P, 8, J]) for u in range(R)]
                if product:
                    xt = [ph.sb(f"xt{u}", [D + 1, J, P]) for u in range(2)]
                    NPT, NPY = (3, 2) if sort is None else (2, 1)
                    pt = [ph.ps(f"pt{i}", [P, 4, P]) for i in range(NPT)]
                    py = [[ph.ps(f"py{u}{i}", [P, 512]) for i in range(2)] for u in range(NPY)]
                side = Radix(ph, *sort) if sort is not None else None
                s_in = [ph.sem(f"in{u}") for u in range(R)]
                s_st = [ph.sem(f"stored{u}") for u in range(R)]
                s_turn, s_xt, s_y, s_add, s_pre, s_prel, s_var, s_std, s_nmr, s_fin, s_ext, s_one = (
                    ph.sem(k) for k in ("turned", "xt", "product", "added", "scaled", "scaled_half",
                                        "variance", "std", "shift", "result", "second", "ones"))
                s_fin2, s_part = ph.sem("result_rest"), ph.sem("result_rest_half")
                s_half, s_full, s_bn, s_mom, s_sq, s_inv, s_four, s_first = (ph.sem(k) for k in (
                    "activated", "summed", "stats", "moments", "squared", "inverse", "four_turned", "four_copied"))
                n_in = len(kinds)
                JA = 6 if mode == "edge" else J
                L = 2 if product else 1
                s_free = s_full if norm else s_fin
                total = BLOCKS + 1

                def shape(c):
                    return (REST, 1) if isinstance(c, int) and c == BLOCKS else (P, J)

                def view(t, c):
                    p, j = shape(c)
                    return t[bass.ds(c * BN, p * j), :].rearrange("(p j) d -> p j d", j=j)

                def at(eng, sem, c, back=0):
                    if isinstance(c, int) and c + 1 - back <= 0:
                        return
                    eng.wait_ge(sem, c + 1 - back)

                def landed(eng, sem, n, c, u, r4):
                    eng.wait_ge(sem[u], 16 * n * (r4 + 1))

                def stages(eng, *listed):
                    def run(r, u):
                        for lag, stage in listed:
                            if lag is None:
                                if not (isinstance(r, int) and R * r + u >= CHUNKS):
                                    stage(eng, R * r + u, u, r)
                                continue
                            c = R * r + (u - lag)
                            if isinstance(c, int) and not 0 <= c < total:
                                continue
                            stage(c, (u - lag) % R, r + (u - lag) // R)
                    deepest = max([lag for lag, _ in listed if lag is not None], default=0)
                    steps = max(total + deepest, CHUNKS if side is not None else 0)
                    rounds = BLOCKS // R
                    for s in range(2 * R):
                        run(s // R, s % R)
                    with eng.Fori(2, rounds) as r:
                        for u in range(R):
                            run(r, u)
                    for s in range(rounds * R, steps):
                        run(s // R, s % R)

                with nc.Block() as block:
                    @block.sync
                    def _(sp):
                        def load(c, u, r4):
                            p, j = shape(c)
                            at(sp, s_free, c, R)
                            for k, b in zip(kinds, bufs[u]):
                                sp.dma_start(b[0:p, 0:j, :], view(tabs[k], c)).then_inc(s_in[u], 16)

                        def store(c, u, r4):
                            p, j = shape(c)
                            at(sp, s_fin, c)
                            if j > JA:
                                at(sp, s_fin2, c)
                            if factors:
                                at(sp, s_ext, c)
                            sp.dma_start(view(out_t, c), res[u][0:p, 0:j, :]).then_inc(s_st[u], 16)
                        stages(sp, (0, load), (L + 5 if norm else L + 2, store))
                        for u in range(R):
                            sp.wait_ge(s_st[u], 16 * (total // R))

                    @block.gpsimd
                    def _(pool):
                        wide = lambda t, c, p, j: t[0:p, bass.ds(c, 1), 0:j].rearrange("p c j -> p (c j)").rearrange(
                            "p (j o) -> p j o", o=1).broadcast_to([p, j, D])

                        def scale_in(c, u, r4):
                            p, j = shape(c)
                            v = bufs[u][1][0:p, 0:j, :]
                            landed(pool, s_in, n_in, c, u, r4)
                            t = rs_odb if mode == "prop" else rs_id
                            if mode == "prop":
                                v2 = bufs[u][2][0:p, 0:j, :]
                                nc.gpsimd.tensor_tensor(v2, v2, wide(t, c, p, j), ALU.mult)
                                nc.gpsimd.tensor_tensor(v, v, wide(t, c, p, j), ALU.mult).then_inc(s_pre, 1)
                            else:
                                nc.gpsimd.tensor_tensor(v, v, wide(t, c, p, j), ALU.mult).then_inc(s_prel, 1)
                                at(pool, s_prel, c)
                                nc.gpsimd.tensor_tensor(
                                    v, v, bias_gcn[0:p, :].rearrange("p (o d) -> p o d", o=1).broadcast_to([p, j, D]),
                                    ALU.add).then_inc(s_pre, 1)

                        def third_term(c, u, r4):
                            p, j = shape(c)
                            v = z[u][0:p, 0:j, :]
                            at(pool, s_half, c)
                            nc.gpsimd.tensor_tensor(v, v, bufs[u][2][0:p, 0:j, 0:D], ALU.add).then_inc(s_full, 1)

                        def factor_columns(c, u, r4):
                            p, j = shape(c)
                            if not (isinstance(c, int) and c < R):
                                pool.wait_ge(s_st[u], 16 * r4)
                            for k, t in enumerate(factors):
                                last = nc.gpsimd.tensor_copy(
                                    res[u][0:p, 0:j, D + k], t[0:p, bass.ds(c, 1), 0:j].rearrange("p c j -> p (c j)"))
                            last.then_inc(s_ext, 1)
                        def final_rest(c, u, r4):
                            p, j = shape(c)
                            if j <= JA:
                                return
                            at(pool, s_nmr, c)
                            if not (isinstance(c, int) and c < R):
                                pool.wait_ge(s_st[u], 16 * r4)
                            o = res[u][0:p, JA:j, 0:D]
                            row_of = lambda i: st[u][0:p, i, JA:j].rearrange("p (j o) -> p j o", o=1).broadcast_to([p, j - JA, D])
                            nc.gpsimd.tensor_tensor(o, z[u][0:p, JA:j, :], row_of(5), ALU.mult).then_inc(s_part, 1)
                            at(pool, s_part, c)
                            nc.gpsimd.tensor_tensor(o, o, row_of(6), ALU.add).then_inc(s_fin2, 1)

                        todo = []
                        if JA < J:
                            todo.append((L + 3, final_rest))
                        if mode in ("prop", "gcn"):
                            todo.append((0, scale_in))
                        if mode == "conv2":
                            todo.append((L, third_term))
                        if side is not None:
                            todo.append((None, side.pool_step))
                        if factors:
                            todo.append((L + 3, factor_columns))
                        if todo:
                            stages(pool, *todo)
                        if side is not None:
                            side.pool_after(pool)

                    @block.tensor
                    def _(pe):
                        def turn(c, u, r4):
                            p, jn = shape(c)
                            landed(pe, s_in, n_in, c, u, r4)
                            at(pe, s_xt, c, 1)
                            for j in range(jn):
                                if j == 4 * NPT:
                                    pe.wait_ge(s_first, c + 1)
                                last = nc.tensor.transpose(pt[j // 4 % NPT][0:D, j % 4, 0:p], bufs[u][0][0:p, j, 0:D],
                                                           ident[0:p, 0:p])
                                if j == 3 and NPT == 2:
                                    last.then_inc(s_four, 1)
                            last.then_inc(s_turn, 1)

                        def root(c, u, r4):
                            p, jn = shape(c)
                            at(pe, s_xt, c)
                            if isinstance(c, int) and c == 0:
                                pe.wait_ge(s_one, 1)
                            at(pe, s_add, c, NPY)
                            for j in range(jn):
                                last = nc.tensor.matmul(py[u % NPY][j // 5][0:p, (j % 5) * D:(j % 5 + 1) * D],
                                                        xt[u % 2][:, j, 0:p], wgt[:, :], start=True, stop=True)
                            last.then_inc(s_y, 1)
                        if product:
                            if side is not None:
                                side.pe_before(pe)
                            stages(pe, (0, turn), (1, root), *([(None, side.pe_step)] if side is not None else []))

                    @block.scalar
                    def _(act):
                        def turned(c, u, r4):
                            p, jn = shape(c)
                            at(act, s_y, c, 2)
                            for i in range(-(-jn // 4)):
                                if i == 0 and NPT == 2 and jn > 4:
                                    at(act, s_four, c)
                                elif i == (1 if NPT == 2 and jn > 4 else 0):
                                    at(act, s_turn, c)
                                w = min(4, jn - 4 * i)
                                last = nc.scalar.copy(xt[u % 2][0:D, 4 * i:4 * i + w, 0:p], pt[i % NPT][0:D, 0:w, 0:p])
                                if i == 0 and NPT == 2 and jn > 4:
                                    last.then_inc(s_first, 1)
                            last.then_inc(s_xt, 1)

                        def std(c, u, r4):
                            p, jn = shape(c)
                            at(act, s_var, c)
                            nc.scalar.activation(st[u][0:p, 4, 0:jn], st[u][0:p, 3, 0:jn], ACT.Sqrt, bias=eps[0:p, :],
                                                 scale=1.0 / D).then_inc(s_std, 1)

                        def final(c, u, r4):
                            p, jn = shape(c)
                            at(act, s_nmr, c)
                            if not (isinstance(c, int) and c < R):
                                act.wait_ge(s_st[u], 16 * r4)
                            for j in range(min(jn, JA)):
                                last = nc.scalar.activation(res[u][0:p, j, 0:D], z[u][0:p, j, :], ACT.Identity,
                                                            scale=st[u][0:p, 5, j:j + 1], bias=st[u][0:p, 6, j:j + 1])
                            last.then_inc(s_fin, 1)
                        todo = []
                        if side is not None:
                            todo.append((None, side.act_step))
                        if product:
                            todo.append((0, turned))
                        if norm:
                            todo += [(L + 2, std), (L + 3, final)]
                        stages(act, *todo)

                    @block.vector
                    def _(dve):
                        if product:
                            for u in range(2):
                                last = nc.vector.memset(xt[u][D:D + 1, :, :], 1.0)
                            last.then_inc(s_one, 1)
                        if side is not None:
                            side.dve_before(dve)

                        def add(c, u, r4):
                            p, jn = shape(c)
                            landed(dve, s_in, n_in, c, u, r4)
                            at(dve, s_y, c)
                            if norm:
                                at(dve, s_fin, c, R)
                                if jn > JA:
                                    at(dve, s_fin2, c, R)
                            for i in range(-(-jn // 5)):
                                w = min(5, jn - 5 * i)
                                last = nc.vector.tensor_tensor(
                                    z[u][0:p, 5 * i:5 * i + w, :],
                                    py[u % NPY][i][0:p, 0:w * D].rearrange("p (j d) -> p j d", d=D),
                                    bufs[u][1][0:p, 5 * i:5 * i + w, :], ALU.add)
                            last.then_inc(s_add, 1)
                            if mode == "conv1":
                                v = z[u][0:p, 0:jn, :]
                                at(dve, s_add, c)
                                if not (isinstance(c, int) and c < R):
                                    dve.wait_ge(s_st[u], 16 * r4)
                                nc.vector.scalar_tensor_tensor(res[u][0:p, 0:jn, :], v, 0.01, v, ALU.mult, ALU.max
                                                               ).then_inc(s_fin, 1)

                        def activate(c, u, r4):
                            p, jn = shape(c)
                            v = z[u][0:p, 0:jn, :]
                            B = [b[0:p, 0:jn, 0:D] for b in bufs[u]]
                            at(dve, s_add if product else s_pre, c)
                            if not product:
                                at(dve, s_fin, c, R)
                            if mode == "conv2":
                                ins = nc.vector.scalar_tensor_tensor(v, v, 0.01, v, ALU.mult, ALU.max)
                            elif mode == "edge":
                                ins = nc.vector.scalar_tensor_tensor(v, v, 0.0, B[0], ALU.max, ALU.add)
                            elif mode == "prop":
                                ins = nc.vector.scalar_tensor_tensor(v, B[0], 1.0 + ALPHA / THETA, B[1], ALU.mult, ALU.add)
                            else:
                                ins = nc.vector.tensor_tensor(v, B[0], B[1], ALU.add)
                            ins.then_inc(s_half if mode in ("conv2", "prop") else s_full, 1)

                        def third_term(c, u, r4):
                            p, jn = shape(c)
                            v = z[u][0:p, 0:jn, :]
                            at(dve, s_half, c)
                            nc.vector.tensor_tensor(v, v, bufs[u][2][0:p, 0:jn, 0:D], ALU.add).then_inc(s_full, 1)

                        def stats(c, u, r4):
                            p, jn = shape(c)
                            at(dve, s_full, c)
                            for j in range(jn):
                                last = nc.vector.bn_stats(bst[u][0:p, j, :], z[u][0:p, j, :])
                            last.then_inc(s_bn, 1)

                        def moments(c, u, r4):
                            p, jn = shape(c)
                            b = bst[u][0:p, 0:jn, :]
                            s_ = lambda i: st[u][0:p, i, 0:jn]
                            at(dve, s_bn, c)
                            nc.vector.tensor_tensor(s_(1), b[:, :, 2], b[:, :, 5], ALU.add)
                            nc.vector.tensor_tensor(s_(0), b[:, :, 1], b[:, :, 4], ALU.add)
                            nc.vector.tensor_tensor(s_(2), b[:, :, 1], b[:, :, 4], ALU.subtract).then_inc(s_mom, 1)

                        def square(c, u, r4):
                            p, jn = shape(c)
                            s_ = lambda i: st[u][0:p, i, 0:jn]
                            at(dve, s_mom, c)
                            nc.vector.tensor_tensor(s_(2), s_(2), s_(2), ALU.mult).then_inc(s_sq, 1)

                        def variance(c, u, r4):
                            p, jn = shape(c)
                            s_ = lambda i: st[u][0:p, i, 0:jn]
                            at(dve, s_sq, c)
                            nc.vector.scalar_tensor_tensor(s_(3), s_(2), D / 4.0, s_(1), ALU.mult, ALU.add).then_inc(s_var, 1)

                        def inverse(c, u, r4):
                            p, jn = shape(c)
                            at(dve, s_std, c)
                            nc.vector.reciprocal(st[u][0:p, 5, 0:jn], st[u][0:p, 4, 0:jn]).then_inc(s_inv, 1)

                        def shift(c, u, r4):
                            p, jn = shape(c)
                            s_ = lambda i: st[u][0:p, i, 0:jn]
                            at(dve, s_inv, c)
                            nc.vector.scalar_tensor_tensor(s_(6), s_(0), -0.5, s_(5), ALU.mult, ALU.mult).then_inc(s_nmr, 1)
                        todo = [(L, add)] if product else []
                        if norm:
                            todo += [(L + 1, moments), (L, activate), (L + 1, square)]
                            todo += [(L, third_term)] if mode == "prop" else []
                            todo += [(L + 1, variance), (L + 2, inverse), (L + 2, shift)]
                        if side is not None:
                            todo.append((None, side.dve_step))
                        if norm:
                            todo.append((L, stats))
                        stages(dve, *todo)
                        if side is not None:
                            side.dve_after(dve)

        def spread(name, source, flags, width):
            with Phase(nc, name) as ph:
                s_in, s_m = ph.sem("in"), ph.sem("cleared")
                with nc.Block() as block:
                    @block.vector
                    def _(dve):
                        if width > EP:
                            nc.vector.memset(flags[:, EP:width], 0.0).then_inc(s_m, 1)

                    @block.sync
                    def _(sp):
                        sp.dma_start(flags[:, 0:EP], source.rearrange("(p e) -> p e", p=1).broadcast_to([D, EP])
                                     ).then_inc(s_in, 16)
                        sp.wait_ge(s_in, 16)

        conv = ExitStack()
        with conv:
            flags = conv.enter_context(nc.sbuf_tensor("flags_max", [D, EP], BF16))
            spread("flagmax", dflag, flags, EP)
            for i, table in enumerate((a["x"], c1)):
                edge_phase(f"conv{i + 1}", "conv", gidx=srcg, table=table, attr=a["edge_attr_32"], de=DE32, sidx=dlcol, weight=w_conv[i][:, :],
                           target=aggd, flags=flags, zeroed=(s_z0, zero_count(aggd)) if i == 0 else None,
                           zero_also=[aggs, agga] if i == 0 else sums,
                           counted=(srccol, odeg, None, None, None, "low") if i == 0 else (v1, ideg, None, active, odeg, None))
                if i == 0:
                    dense_phase("node1", "conv1", sort=(srccol, dstcol, False, sorted1))
                    columns("colsort1", sorted1.rearrange("e w -> (e w)"), 2, [k1, v1])

        with Phase(nc, "keys") as ph:
            inv, keyf = ph.sb("inv", [P, TILES]), ph.sb("keyf", [P, TILES])
            s_v = ph.sem("dve")
            with nc.Block() as block:
                @block.vector
                def _(dve):
                    nc.vector.tensor_scalar(inv[:, :], active[:, :], 0.0, None, ALU.is_equal).then_inc(s_v, 1)
                    dve.wait_ge(s_v, 1)
                    nc.vector.scalar_tensor_tensor(keyf[:, :], inv[:, :], float(INACTIVE), k1[:, :], ALU.mult, ALU.add
                                                   ).then_inc(s_v, 1)
                    dve.wait_ge(s_v, 2)
                    nc.vector.tensor_copy(k1[:, :], keyf[:, :])
        histogram("hact", k1, adeg, alast, "high")

        with Phase(nc, "factors") as ph:
            od = ph.sb("od", [P, BLOCKS + 1, J])
            has, ad = ph.sb("has", [P, BLOCKS + 1, J]), ph.sb("ad", [P, BLOCKS + 1, J])
            s_in, s_m, s_v, s_a = (ph.sem(k) for k in ("tables_in", "cleared", "dve", "act"))
            with nc.Block() as block:
                @block.sync
                def _(sp):
                    sp.wait_ge(s_m, 1)
                    for t, dst in ((odeg, od), (ideg, rs_id), (alast, last_n), (adeg, ad)):
                        sp.dma_start(dst[:, 0:BLOCKS, :], t[0:BLOCKS * BN].rearrange("(c p j) -> p c j", p=P, j=J)).then_inc(s_in, 16)
                        sp.dma_start(dst[0:REST, BLOCKS, 0:1], t[BLOCKS * BN:N].rearrange("(p j) -> p j", j=1)).then_inc(s_in, 16)

                @block.vector
                def _(dve):
                    for t in (od, rs_id, last_n, ad):
                        last = nc.vector.memset(t[:, :, :], 1.0)
                    last.then_inc(s_m, 1)
                    dve.wait_ge(s_in, 128)
                    nc.vector.tensor_scalar(has[:, :, :], od[:, :, :], 0.0, BETA, ALU.is_gt, ALU.mult)
                    nc.vector.tensor_scalar(ad[:, :, :], ad[:, :, :], 0.0, None, ALU.is_gt)
                    nc.vector.tensor_scalar(rs_od[:, :, :], od[:, :, :], 1.0, None, ALU.max)
                    nc.vector.tensor_scalar(rs_id[:, :, :], rs_id[:, :, :], 1.0, None, ALU.max).then_inc(s_v, 1)
                    dve.wait_ge(s_a, 1)
                    nc.vector.reciprocal(rs_od[:, :, :], rs_od[:, :, :])
                    nc.vector.reciprocal(rs_id[:, :, :], rs_id[:, :, :]).then_inc(s_v, 1)
                    dve.wait_ge(s_v, 2)
                    nc.vector.tensor_scalar(rs_ida[:, :, :], rs_id[:, :, :], ALPHA, None, ALU.mult)
                    nc.vector.tensor_scalar(rs_odb[:, :, :], rs_od[:, :, :], BETA / THETA, None, ALU.mult)
                    nc.vector.tensor_tensor(fac[:, :, :], rs_od[:, :, :], rs_id[:, :, :], ALU.mult).then_inc(s_v, 1)
                    dve.wait_ge(s_v, 3)
                    nc.vector.tensor_tensor(fac[:, :, :], fac[:, :, :], has[:, :, :], ALU.mult).then_inc(s_v, 1)
                    dve.wait_ge(s_v, 4)
                    nc.vector.tensor_tensor(fac_a[:, :, :], fac[:, :, :], ad[:, :, :], ALU.mult)

                @block.scalar
                def _(act):
                    act.wait_ge(s_v, 1)
                    nc.scalar.activation(rs_od[:, :, :], rs_od[:, :, :], ACT.Sqrt)
                    nc.scalar.activation(rs_id[:, :, :], rs_id[:, :, :], ACT.Sqrt).then_inc(s_a, 1)

        dense_phase("node2", "conv2", sort=(k1, v1, True, sorted2))

        columns("colsort2", sorted2.rearrange("e w -> (e w)"), 2, [k1, v1])

        with Phase(nc, "runs") as ph:
            pair = ph.sb("pair", [P, TILES, 2], I32)
            prv, nxt = ph.sb("prv", [P, TILES, 2], I32), ph.sb("nxt", [P, TILES, 2], I32)
            fl, lf = ph.sb("fl", [P, TILES]), ph.sb("lf", [P, TILES])
            flb = ph.sb("flb", [P, TILES], U8)
            li, ii = ph.sb("li", [P, TILES], I32), ph.sb("ii", [P, TILES], I32)
            srci, acti = ph.sb("srci", [P, TILES], I32), ph.sb("acti", [P, TILES], I32)
            base, i_f = ph.sb("base", [P, TILES]), ph.sb("i_f", [P, TILES])
            s_m, s_in, s_v, s_st = (ph.sem(k) for k in ("cleared", "in", "dve", "stored"))
            with nc.Block() as block:
                @block.vector
                def _(dve):
                    nc.vector.memset(prv[:, :, :], -1)
                    nc.vector.memset(nxt[:, :, :], -1).then_inc(s_m, 1)
                    nc.vector.tensor_scalar(v1[:, :], v1[:, :], float(N - 1), None, ALU.min)
                    dve.wait_ge(s_in, 16 * 5)
                    nc.vector.tensor_tensor(fl[:, :], pair[:, :, 0], prv[:, :, 0], ALU.is_equal)
                    nc.vector.tensor_scalar(srci[:, :], pair[:, :, 0], INACTIVE - 1, None, ALU.bitwise_and)
                    nc.vector.tensor_scalar(acti[:, :], pair[:, :, 0], 16, None, ALU.arith_shift_right)
                    nc.vector.tensor_tensor(lf[:, :], pair[:, :, 0], nxt[:, :, 0], ALU.is_equal).then_inc(s_v, 1)
                    dve.wait_ge(s_v, 1)
                    nc.vector.tensor_copy(flb[:, :], fl[:, :])
                    nc.vector.scalar_tensor_tensor(base[:, :], lf[:, :], SKIP, srci[:, :], ALU.mult, ALU.add).then_inc(s_v, 1)
                    dve.wait_ge(s_v, 2)
                    nc.vector.scalar_tensor_tensor(lf[:, :], acti[:, :], SKIP, base[:, :], ALU.mult, ALU.add)
                    nc.vector.tensor_scalar(i_f[:, :], acti[:, :], -SKIP, SKIP, ALU.mult, ALU.add).then_inc(s_v, 1)
                    dve.wait_ge(s_v, 3)
                    nc.vector.tensor_tensor(i_f[:, :], i_f[:, :], base[:, :], ALU.add).then_inc(s_v, 1)
                    dve.wait_ge(s_v, 4)
                    nc.vector.tensor_scalar(li[:, :], lf[:, :], SKIP, None, ALU.min)
                    nc.vector.tensor_scalar(ii[:, :], i_f[:, :], SKIP, None, ALU.min).then_inc(s_v, 1)

                @block.sync
                def _(sp):
                    sp.wait_ge(s_m, 1)
                    sp.dma_start(pair[:, :, :], sorted2.rearrange("(p j) w -> p j w", p=P)).then_inc(s_in, 16)
                    sp.dma_start(prv[0:1, 1:TILES, :], sorted2[0:TILES - 1, :].rearrange("(p j) w -> p j w", p=1)).then_inc(s_in, 16)
                    sp.dma_start(prv[1:P, :, :], sorted2[TILES - 1:EP - 1, :].rearrange("(p j) w -> p j w", j=TILES)).then_inc(s_in, 16)
                    sp.dma_start(nxt[0:P - 1, :, :], sorted2[1:EP - TILES + 1, :].rearrange("(p j) w -> p j w", j=TILES)).then_inc(s_in, 16)
                    sp.dma_start(nxt[P - 1:P, 0:TILES - 1, :], sorted2[EP - TILES + 1:EP, :].rearrange("(p j) w -> p j w", p=1)).then_inc(s_in, 16)
                    sp.wait_ge(s_v, 5)
                    sp.dma_start(ssame.rearrange("(p j) -> p j", p=P), flb[:, :]).then_inc(s_st, 16)
                    sp.dma_start(slast.rearrange("(p j) -> p j", p=P), li[:, :]).then_inc(s_st, 16)
                    sp.dma_start(ilast.rearrange("(p j) -> p j", p=P), ii[:, :]).then_inc(s_st, 16)
                    sp.wait_ge(s_st, 48)

        columns("colslast", slast, 1, [slcol])
        columns("colilast", ilast, 1, [ilcol])

        prop = ExitStack()
        with prop:
            flags = prop.enter_context(nc.sbuf_tensor("flags_source", [D, EX], U8))
            hh = prop.enter_context(nc.sbuf_tensor("hh", [P, TX, D], F32))
            cols = [prop.enter_context(nc.sbuf_tensor(f"faccol{i}", [P, TX], F32)) for i in range(2)]
            spread("flagsrc", ssame, flags, EX)
            n_active = rounds[0:1, 0:1]
            edge_phase("inact", "gcn", gidx=v1, table=x1, sidx=ilcol, target=aggs, flags=flags,
                       zeroed=(s_z, zero_count(aggs, agga, *sums)),
                       rounds_of=rounds[0:1, 1:2], first_round_of=rounds[0:1, 2:3])
            edge_phase("prop0", "init", gidx=v1, table=x1, hh=hh, cols=cols + [lastcol], wr=sums[0], flags=flags,
                       rounds_of=n_active)
            edge_phase("prop1", "first", gidx=lastcol, table=sums[0], gidx2=v1, table2=aggs, hh=hh, cols=cols,
                       wr=sums[1], flags=flags, rounds_of=n_active)
            common = dict(gidx=lastcol, hh=hh, cols=cols, flags=flags, rounds_of=n_active)
            with nc.Fori(0, (K_ITERS - 4) // 2):
                for n in range(2):
                    edge_phase(f"prop{2 + n}", "prop", table=sums[1 - n], wr=sums[n], **common)
            edge_phase("prop8", "prop", table=sums[1], wr=sums[0], **common)
            edge_phase("prop9", "prop", table=sums[0], sidx=slcol, target=agga, **common)
        dense_phase("node3", "prop")

        last = ExitStack()
        with last:
            flags = last.enter_context(nc.sbuf_tensor("flags_dest", [D, EP], U8))
            spread("flagdst", dsame, flags, EP)
            edge_phase("gcn", "gcn", gidx=srcg, table=x2, sidx=dlcol, target=aggd, weight=w_gcn[:, :], flags=flags)
            dense_phase("node4", "gcn")
            edge_phase("edge", "edge", gidx=srcg, table=x3, attr=a["edge_attr_17"], de=DE17, sidx=dlcol, target=aggd,
                       weight=w_n[:, :], flags=flags)
            dense_phase("node5", "edge")


_INS = ["x", "src", "dst", "edge_attr_17", "edge_attr_32", "L0_gnn_W1_msg", "L0_gnn_W1_edge", "L0_gnn_W1_root",
        "L0_gnn_b1", "L0_gnn_W2_msg", "L0_gnn_W2_edge", "L0_gnn_W2_root", "L0_gnn_b2", "L2_gnn_weight", "L2_gnn_bias",
        "L3_gnn_W1", "L3_gnn_b1", "L3_gnn_W2", "L3_gnn_b2", "L3_gnn_Ws", "L3_gnn_bs", "L3_gnn_Wn", "L3_gnn_bn"]


def kernel(**inputs):
    import concourse.bacc as _bacc
    from concourse.bass_utils import run_bass_kernel_spmd as _run
    nc = _bacc.Bacc("TRN2", target_bir_lowering=False, num_devices=1)
    arrays, args = {}, {}
    for name in _INS:
        v = np.ascontiguousarray(inputs[name])
        arrays[f"in_{name}"] = v
        args[name] = nc.dram_tensor(f"in_{name}", v.shape, mybir.dt.from_np(v.dtype), kind="ExternalInput").ap()
    out = nc.dram_tensor("out_0", (N, D), F32, kind="ExternalOutput").ap()
    build(nc, args, out)
    r = _run(nc, [arrays], core_ids=[0])
    return r.results[0]["out_0"]
```
